# Optimizing a Trainium2 kernel written in Bass

```python
import numpy as np
import jax
import jax.numpy as jnp

def _softmax(x, axis=-1):
    return jax.nn.softmax(x, axis=axis)

def _gelu(x):
    return jax.nn.gelu(x, approximate=True)

def _silu(x):
    return jax.nn.silu(x)

def _sigmoid(x):
    return jax.nn.sigmoid(x)

def _layernorm(x, axis=-1, eps=1e-05):
    m = jnp.mean(x, axis=axis, keepdims=True)
    v = jnp.var(x, axis=axis, keepdims=True)
    return (x - m) / jnp.sqrt(v + eps)

def _scatter_add(tgt, idx, src, axis=0):
    return tgt.at[idx].add(src)

def _segment_sum(src, seg, n):
    return jax.ops.segment_sum(src, seg, n)
kernel_name = 'mk_gnn_ffn_d2_gnn_r32_04d515'

def setup_inputs(seed: int=0):
    np.random.seed(seed)
    _w = jnp.asarray

    def _rec_inputs():
        import jax
        import jax.numpy as jnp
        _gk = jax.random.key(seed)
        x = -0.0002928 + 1 * jax.random.normal(jax.random.fold_in(_gk, 1), (256, 512), jnp.float32)
        src = jax.random.randint(jax.random.fold_in(_gk, 2), (8192,), 0, 256, jnp.int32)
        dst = jax.random.randint(jax.random.fold_in(_gk, 3), (8192,), 0, 256, jnp.int32)
        _o = jnp.argsort(dst, stable=True)
        src = src[_o]
        dst = dst[_o]
        edge_type_2 = jax.random.randint(jax.random.fold_in(_gk, 13), (8192,), 0, 2, jnp.int32)
        edge_weight = jax.random.uniform(jax.random.fold_in(_gk, 14), (8192,), jnp.float32, 0.0, 0.999996)
        return (x, src, dst, edge_type_2, edge_weight)
    x, src, dst, edge_type_2, edge_weight = _rec_inputs()

    def _L0_gnn_setup():
        import jax, jax.numpy as jnp
        import numpy as np
        N = 256
        D_IN = 512
        D_OUT = 128
        E = 8192
        key = jax.random.key(seed)
        k = jax.random.split(key, 6)
        glorot1 = np.sqrt(6.0 / (D_IN + D_OUT))
        return {'inputs': jax.random.normal(k[0], (N, D_IN), dtype=jnp.float32), 'emb_1': jax.random.uniform(k[1], (D_IN, D_OUT), minval=-glorot1, maxval=glorot1, dtype=jnp.float32), 'emb_2': jax.random.uniform(k[2], (D_IN, D_OUT), minval=-glorot1, maxval=glorot1, dtype=jnp.float32), 'alpha_p': jnp.zeros((1,), dtype=jnp.float32), 'beta_p': jnp.zeros((1,), dtype=jnp.float32), 'edge_vals': jax.random.uniform(k[3], (E,), dtype=jnp.float32), 'edge_row': jax.random.randint(k[4], (E,), 0, N, dtype=jnp.int32), 'edge_col': jax.random.randint(k[5], (E,), 0, N, dtype=jnp.int32), 'num_iters': 5}
    _L0_gnn_all = _L0_gnn_setup()
    _L0_gnn_in = {k: v for k, v in _L0_gnn_all.items() if k in ('emb_1', 'emb_2', 'alpha_p', 'beta_p')}
    del _L0_gnn_all

    def _L0_ffn_setup():
        import jax, jax.numpy as jnp
        import numpy as np
        B, S, H, E, F, TOP_K = (4, 64, 512, 16, 1024, 2)

        def _moe_forward(inputs, router_w, gate_w, up_w, down_w):
            b, s, h = inputs.shape
            x = inputs.reshape(-1, h)
            T = x.shape[0]
            router_logits = x @ router_w.T
            top_vals, top_idx = jax.lax.top_k(router_logits, TOP_K)
            weights = jax.nn.softmax(top_vals.astype(jnp.float32), axis=-1)
            combine = jnp.zeros((T, router_w.shape[0]), jnp.float32)
            combine = combine.at[jnp.arange(T)[:, None], top_idx].set(weights)

            def step(acc, ew):
                wg, wu, wd, ce = ew
                hid = jax.nn.silu(x @ wg) * (x @ wu)
                y = hid @ wd
                return (acc + ce[:, None] * y, None)
            out0 = jnp.zeros_like(x)
            out, _ = jax.lax.scan(step, out0, (gate_w, up_w, down_w, combine.T))
            return (out.reshape(b, s, h), router_logits, top_idx)
        key = jax.random.key(seed)
        k0, k1, k2, k3, k4 = jax.random.split(key, 5)
        scale = 0.02
        return {'inputs': jax.random.normal(k0, (B, S, H), dtype=jnp.float32), 'router_w': jax.random.normal(k1, (E, H), dtype=jnp.float32) * scale, 'gate_w': jax.random.normal(k2, (E, H, F), dtype=jnp.float32) * scale, 'up_w': jax.random.normal(k3, (E, H, F), dtype=jnp.float32) * scale, 'down_w': jax.random.normal(k4, (E, F, H), dtype=jnp.float32) * scale}
    _L0_ffn_all = _L0_ffn_setup()
    _L0_ffn_in = {k: v for k, v in _L0_ffn_all.items() if k in ('router_w', 'gate_w', 'up_w', 'down_w')}
    del _L0_ffn_all

    def _L1_gnn_setup():
        import jax, jax.numpy as jnp
        import numpy as np
        NUM_RELATIONS = 2
        NUM_BASES = 30
        HIDDEN = 512
        N_NODES = 10000
        N_EDGES = 5000

        def rgcn_gate_layer(x, row, col, edge_type, basis, att, gate_w, root, bias):
            H = x.shape[1]
            w = jnp.einsum('rb,bio->rio', att, basis)
            x_j = x[col]
            msgs = []
            for r in range(NUM_RELATIONS):
                gate = jax.nn.sigmoid(x_j @ gate_w[r, :, 0])
                msgs.append(gate[:, None] * x_j @ w[r])
            msg = jnp.where((edge_type == 0)[:, None], msgs[0], msgs[1])
            agg = jax.ops.segment_sum(msg, row, num_segments=x.shape[0])
            return agg + x @ root + bias
        key = jax.random.key(seed)
        ks = jax.random.split(key, 16)
        H, R, B = (HIDDEN, NUM_RELATIONS, NUM_BASES)
        bound = 1.0 / np.sqrt(B * H)
        u = lambda k, shape: jax.random.uniform(k, shape, jnp.float32, -bound, bound)
        inp = {'x': jax.random.normal(ks[0], (N_NODES, H), jnp.float32), 'edge_index': jax.random.randint(ks[1], (2, N_EDGES), 0, N_NODES, jnp.int32), 'edge_type': jax.random.randint(ks[2], (N_EDGES,), 0, R, jnp.int32), 'basis1': u(ks[3], (B, H, H)), 'att1': u(ks[4], (R, B)), 'gate_w1': u(ks[5], (R, H, 1)), 'root1': u(ks[6], (H, H)), 'bias1': u(ks[7], (H,)), 'basis2': u(ks[8], (B, H, H)), 'att2': u(ks[9], (R, B)), 'gate_w2': u(ks[10], (R, H, 1)), 'root2': u(ks[11], (H, H)), 'bias2': u(ks[12], (H,))}
        return inp
    _L1_gnn_all = _L1_gnn_setup()
    _L1_gnn_in = {k: v for k, v in _L1_gnn_all.items() if k in ('basis1', 'att1', 'gate_w1', 'root1', 'bias1', 'basis2', 'att2', 'gate_w2', 'root2', 'bias2')}
    del _L1_gnn_all

    def _L1_ffn_setup():
        import jax, jax.numpy as jnp
        import numpy as np
        B, T, D = (4, 256, 512)
        E, F, CAP = (8, 64, 128)
        key = jax.random.key(seed)
        ks = jax.random.split(key, 6)
        s = 0.02
        return {'x': jax.random.normal(ks[0], (B, T, D), dtype=jnp.float32), 'Wr': jax.random.normal(ks[1], (D, E), dtype=jnp.float32) * s, 'W1': jax.random.normal(ks[2], (E, D, F), dtype=jnp.float32) * s, 'b1': jax.random.normal(ks[3], (E, F), dtype=jnp.float32) * s, 'W2': jax.random.normal(ks[4], (E, F, D), dtype=jnp.float32) * s, 'b2': jax.random.normal(ks[5], (E, D), dtype=jnp.float32) * s}
    _L1_ffn_all = _L1_ffn_setup()
    _L1_ffn_in = {k: v for k, v in _L1_ffn_all.items() if k in ('Wr', 'W1', 'b1', 'W2', 'b2')}
    del _L1_ffn_all
    return {'x': x, 'src': src, 'dst': dst, 'edge_type_2': edge_type_2, 'edge_weight': edge_weight, 'L0_gnn_emb_1': _L0_gnn_in['emb_1'], 'L0_gnn_emb_2': _L0_gnn_in['emb_2'], 'L0_gnn_alpha_p': _L0_gnn_in['alpha_p'], 'L0_gnn_beta_p': _L0_gnn_in['beta_p'], 'L0_ffn_router_w': _L0_ffn_in['router_w'], 'L0_ffn_gate_w': _L0_ffn_in['gate_w'], 'L0_ffn_up_w': _L0_ffn_in['up_w'], 'L0_ffn_down_w': _L0_ffn_in['down_w'], 'L1_gnn_basis1': _L1_gnn_in['basis1'], 'L1_gnn_att1': _L1_gnn_in['att1'], 'L1_gnn_gate_w1': _L1_gnn_in['gate_w1'], 'L1_gnn_root1': _L1_gnn_in['root1'], 'L1_gnn_bias1': _L1_gnn_in['bias1'], 'L1_gnn_basis2': _L1_gnn_in['basis2'], 'L1_gnn_att2': _L1_gnn_in['att2'], 'L1_gnn_gate_w2': _L1_gnn_in['gate_w2'], 'L1_gnn_root2': _L1_gnn_in['root2'], 'L1_gnn_bias2': _L1_gnn_in['bias2'], 'L1_ffn_Wr': _L1_ffn_in['Wr'], 'L1_ffn_W1': _L1_ffn_in['W1'], 'L1_ffn_b1': _L1_ffn_in['b1'], 'L1_ffn_W2': _L1_ffn_in['W2'], 'L1_ffn_b2': _L1_ffn_in['b2']}

def reference(x, src, dst, edge_type_2, edge_weight, L0_gnn_emb_1, L0_gnn_emb_2, L0_gnn_alpha_p, L0_gnn_beta_p, L0_ffn_router_w, L0_ffn_gate_w, L0_ffn_up_w, L0_ffn_down_w, L1_gnn_basis1, L1_gnn_att1, L1_gnn_gate_w1, L1_gnn_root1, L1_gnn_bias1, L1_gnn_basis2, L1_gnn_att2, L1_gnn_gate_w2, L1_gnn_root2, L1_gnn_bias2, L1_ffn_Wr, L1_ffn_W1, L1_ffn_b1, L1_ffn_W2, L1_ffn_b2):
    import jax
    import jax.numpy as jnp

    def _L0_gnn_ref(inputs, emb_1, emb_2, alpha_p, beta_p, edge_vals, edge_row, edge_col, num_iters):
        import jax, jax.numpy as jnp
        import numpy as np
        N = 256
        D_IN = 512
        D_OUT = 128
        E = 8192
        n = inputs.shape[0]
        x1 = inputs @ emb_1
        x2 = inputs @ emb_2
        logits = x1 @ x2.T
        sim = jax.nn.softmax(jax.nn.leaky_relu(logits, 0.2), axis=-1)
        vals = edge_vals * sim[edge_row, edge_col]
        normalize = jax.ops.segment_sum(vals, edge_row, num_segments=n)[:, None]
        alpha = jnp.exp(alpha_p)
        beta = jnp.exp(beta_p)
        denom = beta + normalize * alpha + alpha

        def body(out, _):
            sp = jax.ops.segment_sum(vals[:, None] * out[edge_col], edge_row, num_segments=n)
            out = (inputs * beta + (sp + out) * alpha) / denom
            return (out, None)
        out, _ = jax.lax.scan(body, inputs, None, length=num_iters)
        return out

    def _L0_ffn_ref(inputs, router_w, gate_w, up_w, down_w):
        import jax, jax.numpy as jnp
        import numpy as np
        B, S, H, E, F, TOP_K = (4, 64, 512, 16, 1024, 2)

        def _moe_forward(inputs, router_w, gate_w, up_w, down_w):
            b, s, h = inputs.shape
            x = inputs.reshape(-1, h)
            T = x.shape[0]
            router_logits = x @ router_w.T
            top_vals, top_idx = jax.lax.top_k(router_logits, TOP_K)
            weights = jax.nn.softmax(top_vals.astype(jnp.float32), axis=-1)
            combine = jnp.zeros((T, router_w.shape[0]), jnp.float32)
            combine = combine.at[jnp.arange(T)[:, None], top_idx].set(weights)

            def step(acc, ew):
                wg, wu, wd, ce = ew
                hid = jax.nn.silu(x @ wg) * (x @ wu)
                y = hid @ wd
                return (acc + ce[:, None] * y, None)
            out0 = jnp.zeros_like(x)
            out, _ = jax.lax.scan(step, out0, (gate_w, up_w, down_w, combine.T))
            return (out.reshape(b, s, h), router_logits, top_idx)
        out, router_logits, selected_experts = _moe_forward(inputs, router_w, gate_w, up_w, down_w)
        return out

    def _L1_gnn_ref(x, edge_index, edge_type, basis1, att1, gate_w1, root1, bias1, basis2, att2, gate_w2, root2, bias2):
        import jax, jax.numpy as jnp
        import numpy as np
        NUM_RELATIONS = 2
        NUM_BASES = 30
        HIDDEN = 512
        N_NODES = 10000
        N_EDGES = 5000

        def rgcn_gate_layer(x, row, col, edge_type, basis, att, gate_w, root, bias):
            H = x.shape[1]
            w = jnp.einsum('rb,bio->rio', att, basis)
            x_j = x[col]
            msgs = []
            for r in range(NUM_RELATIONS):
                gate = jax.nn.sigmoid(x_j @ gate_w[r, :, 0])
                msgs.append(gate[:, None] * x_j @ w[r])
            msg = jnp.where((edge_type == 0)[:, None], msgs[0], msgs[1])
            agg = jax.ops.segment_sum(msg, row, num_segments=x.shape[0])
            return agg + x @ root + bias
        row, col = (edge_index[0], edge_index[1])
        h = jax.nn.relu(rgcn_gate_layer(x, row, col, edge_type, basis1, att1, gate_w1, root1, bias1))
        out = rgcn_gate_layer(h, row, col, edge_type, basis2, att2, gate_w2, root2, bias2)
        return out

    def _L1_ffn_ref(x, Wr, W1, b1, W2, b2):
        import jax, jax.numpy as jnp
        import numpy as np
        B, T, D = (4, 256, 512)
        E, F, CAP = (8, 64, 128)
        Bb, Tt, Dd = x.shape
        N = Bb * Tt
        C = min(CAP, N)
        x_flat = x.reshape(N, Dd)
        logits = x_flat @ Wr
        probs = jax.nn.softmax(logits, axis=0)
        vals, idx = jax.lax.top_k(probs.T, C)
        selected = x_flat[idx]
        h = jax.nn.gelu(jnp.einsum('ecd,edf->ecf', selected, W1) + b1[:, None, :], approximate=False)
        out_e = jnp.einsum('ecf,efd->ecd', h, W2) + b2[:, None, :]
        weighted = vals[..., None] * out_e
        output = jnp.zeros_like(x_flat).at[idx.reshape(-1)].add(weighted.reshape(-1, Dd))
        return output.reshape(Bb, Tt, Dd)
    edge_index = jnp.stack([src, dst])
    x = x + _L0_gnn_ref(_layernorm(x, axis=-1), L0_gnn_emb_1, L0_gnn_emb_2, L0_gnn_alpha_p, L0_gnn_beta_p, edge_weight, src, dst, 5)
    x = x + _L0_ffn_ref(_layernorm(x, axis=-1)[None], L0_ffn_router_w, L0_ffn_gate_w, L0_ffn_up_w, L0_ffn_down_w)[0]
    x = x + _L1_gnn_ref(_layernorm(x, axis=-1), edge_index, edge_type_2, L1_gnn_basis1, L1_gnn_att1, L1_gnn_gate_w1, L1_gnn_root1, L1_gnn_bias1, L1_gnn_basis2, L1_gnn_att2, L1_gnn_gate_w2, L1_gnn_root2, L1_gnn_bias2)
    x = x + _L1_ffn_ref(_layernorm(x, axis=-1)[None], L1_ffn_Wr, L1_ffn_W1, L1_ffn_b1, L1_ffn_W2, L1_ffn_b2)[0]
    return x

_drawn_inputs = setup_inputs


def setup_inputs(seed=0):
    import zlib

    import numpy as np

    out = dict(_drawn_inputs(seed))
    spreads = {}
    factors = {'L1_gnn_basis1': 8.0,
     'L1_gnn_att1': 8.0,
     'L1_gnn_gate_w1': 8.0,
     'L1_gnn_root1': 8.0,
     'L1_gnn_bias1': 8.0,
     'L1_gnn_basis2': 8.0,
     'L1_gnn_att2': 8.0,
     'L1_gnn_gate_w2': 8.0,
     'L1_gnn_root2': 8.0,
     'L1_gnn_bias2': 27.952,
     'L1_ffn_Wr': 8.0,
     'L1_ffn_W1': 8.0,
     'L1_ffn_b1': 64.0,
     'L1_ffn_W2': 8.0,
     'L1_ffn_b2': 60.117}
    for name, (base, spread) in spreads.items():
        noise = np.random.default_rng([zlib.crc32(name.encode()), seed]).standard_normal(out[name].shape)
        drawn = base * np.exp(spread * noise) if base else spread * noise
        out[name] = jnp.asarray(drawn.astype(out[name].dtype))
    for name, factor in factors.items():
        out[name] = (out[name] * factor).astype(out[name].dtype)
    return out
```

```python
from contextlib import ExitStack

import concourse.bass as bass
from concourse import mybir

F32 = mybir.dt.float32
BF16 = mybir.dt.bfloat16
I32 = mybir.dt.int32
ALU = mybir.AluOpType
ACT = mybir.ActivationFunctionType
AX = mybir.AxisListType

P = 128
N = 256
NT = N // P
H = 512
HC = H // P
E_EDGES = 8192
ECH = E_EDGES // P
ITERS = 5
NE, FF = 16, 1024
NR = NE + 4
CAP = 64
NB = 30
BG = NB // 4
WC = H // 64
E2, F2, C2 = 8, 64, 128
EPS = 1e-5

CONST = {}
_at = 0
for _name, _n in (("ident", P), ("before", P), ("ones", P), ("diag32", 32), ("diag64", 64),
                  ("earlier_expert", NE * NE), ("tie_order", NT * N), ("iota", N), ("slots", 2 * CAP)):
    CONST[_name] = (_at, _at + _n)
    _at += _n
NCONST = _at
LIMIT = CAP


def wait(eng, sem, value):
    if not (isinstance(value, int) and value <= 0):
        eng.wait_ge(sem, value)


class Chain:

    def __init__(self, eng, sem, base=0):
        self.eng, self.sem, self.base, self.n = eng, sem, base, 0

    def link(self, ins):
        self.n += 1
        ins.then_inc(self.sem, 1)
        self.eng.wait_ge(self.sem, self.base + self.n)


def build(nc, x_d, src_d, dst_d, type_d, ew_d, emb1_d, emb2_d, alpha_d, beta_d, rw_d, gate_d, up_d, down_d,
          basis1_d, att1_d, gw1_d, root1_d, bias1_d, basis2_d, att2_d, gw2_d, root2_d, bias2_d,
          wr_d, w1_d, b1_d, w2_d, b2_d, const_d, out_d):
    with ExitStack() as ctx:
        def sb(name, shape, dt=F32):
            return ctx.enter_context(nc.sbuf_tensor(name, shape, dt))

        def sem(name):
            return ctx.enter_context(nc.semaphore(name))

        bank = [ctx.enter_context(nc.psum_tensor(f"bank{i}", [P, 512], F32)) for i in range(8)]

        ring = sb("ring", [P, 6, 4096])
        wcomb = sb("wcomb", [P, 2 * WC, H])
        const = sb("const", [P, NCONST])

        def cst(name):
            a, b = CONST[name]
            return const[:, a:b]

        ident = cst("ident")
        iota_b = sb("iota_b", [P, N], BF16)
        zero_b = sb("zero_b", [P, 512], BF16)
        x = sb("x", [P, NT, H])
        h = sb("h", [P, NT, H])
        hT = sb("hT", [P, HC, N])
        CT = sb("CT", [P, 2, NT, N])
        attw = [sb(f"attw{l}", [P, BG, 64]) for l in range(2)]
        attl = [sb(f"attl{l}", [P, P]) for l in range(2)]
        attb = [sb(f"attb{l}", [P, 2, NB]) for l in range(2)]
        rwT = sb("rwT", [P, HC, NR])
        bias = [sb(f"bias{l}", [P, H]) for l in range(2)]
        stat = sb("stat", [P, NT, 6])
        mv = sb("mv", [P, NT, 2])
        rstd = sb("rstd", [P, NT])
        area = sb("area", [P, 4096 + 2048])
        small = sb("small", [P, 1024])

        NOH = 4
        onehot = area[:, 0:NOH * 6 * N // 2].bitcast(BF16).rearrange("p (q k n) -> p q k n", q=NOH, k=6)
        emb = area[:, 3072:4096].rearrange("p (k c d) -> p k c d", k=2, c=HC)
        sim_e = area[:, 4096:4608].rearrange("p (t s) -> p t s", t=NT)
        lrelu = area[:, 4608:5120].rearrange("p (t s) -> p t s", t=NT)
        x12T = area[:, 5120:5632]
        V = area[:, 0:512].rearrange("p (t s) -> p t s", t=NT)
        VT = area[:, 512:1024].rearrange("p (t s) -> p t s", t=NT)
        inb = area[:, 1024:2048].rearrange("p (t n) -> p t n", t=NT)
        Csb = area[:, 2048:3072].rearrange("p (t r s) -> p t r s", t=NT, r=2)
        out5 = area[:, 3072:5120].rearrange("p (q t n) -> p q t n", q=2, t=NT)
        xg = [area[:, 256 * q:256 * q + 256].rearrange("p (c s) -> p c s", c=HC) for q in range(2)]
        S = [area[:, 512 + 128 * q:640 + 128 * q].rearrange("p (t s) -> p t s", t=NT) for q in range(2)]
        SW = [area[:, 768 + 256 * q:1024 + 256 * q].rearrange("p (t s) -> p t s", t=NT) for q in range(2)]
        ST = [area[:, 1280 + 256 * q:1536 + 256 * q] for q in range(2)]
        sg = area[:, 1792:2304]
        hid = [area[:, 2304 + 512 * q:2816 + 512 * q] for q in range(2)]
        hidT = [area[:, 3328 + 512 * q:3840 + 512 * q] for q in range(2)]
        y = [area[:, 4352 + 512 * q:4864 + 512 * q] for q in range(2)]
        gx = area[:, 0:2048].rearrange("p (r t n) -> p r t n", r=2, t=NT)
        YT = area[:, 2048:4096].rearrange("p (c n) -> p c n", c=WC)
        act1 = area[:, 0:1024].rearrange("p (t n) -> p t n", t=NT)
        act1T = area[:, 1024:2048].rearrange("p (c n) -> p c n", c=HC)
        cmp = area[:, 2048:4096].bitcast(BF16).rearrange("p (t e s) -> p t e s", t=NT, e=E2)
        sgn = area[:, 4096:6144].bitcast(BF16).rearrange("p (t e s) -> p t e s", t=NT, e=E2)

        rw_sb = sb("rw_sb", [NR, H])
        idx_i = sb("idx_i", [P, 3, ECH], I32)
        ew = sb("ew", [P, ECH])
        edge = sb("edge", [P, 7, ECH])
        wpart = sb("wpart", [P, 3, ECH], BF16)
        wr = sb("wr", [P, HC, E2])
        b1 = sb("b1", [P, E2 * F2])
        b2 = sb("b2", [E2, H])

        def sm(a, n=1):
            return small[:, a:a + n]

        alpha, beta = sm(0), sm(1)
        rmax, nmax, rsum, rinv, norm = (sm(2 + 2 * i, 2) for i in range(5))
        den, rden, ra, rb = (sm(12 + 2 * i, 2) for i in range(4))
        ab = sm(20)
        RL = sm(32, 32).rearrange("p (t e) -> p t e", t=NT)
        cmpg = sm(64, 512).rearrange("p (t a b) -> p t a b", t=NT, a=NE)
        rank = sm(576, 32).rearrange("p (t e) -> p t e", t=NT)
        mask = sm(608, 32).rearrange("p (t e) -> p t e", t=NT)
        rexp = sm(640, 32).rearrange("p (t e) -> p t e", t=NT)
        ce = sm(672, 32).rearrange("p (t e) -> p t e", t=NT)
        posm = sm(704, 32).rearrange("p (t e) -> p t e", t=NT)
        m1, s1, r1 = (sm(736 + 2 * i, 2) for i in range(3))
        gates = sm(744, 4)
        over = sm(848, 32).rearrange("p (t e) -> p t e", t=NT)
        ce_over = sm(880, 32).rearrange("p (t e) -> p t e", t=NT)
        over_n = sm(912)
        flag = sb("flag", [1, 1], I32)
        pmx, pnm, psum_, pinv = (small[0:E2, 748 + i:749 + i] for i in range(4))
        prow = sb("prow", [E2, N])
        PT = sb("PT", [E2, N])
        prob = sm(768, 16).rearrange("p (t e) -> p t e", t=NT)
        npro = sm(784, 16).rearrange("p (t e) -> p t e", t=NT)
        sig = sm(800, 16).rearrange("p (t e) -> p t e", t=NT)
        tie = sm(816, 16).rearrange("p (t e) -> p t e", t=NT)
        sel = sm(832, 16).rearrange("p (t e) -> p t e", t=NT)

        SLOT = [(4, 5, 0), (1, 2, 3)]

        def root(l):
            return ring[:, 4, 2048 * l:2048 * l + 2048].rearrange("p (c n) -> p c n", c=HC)

        def w1v():
            return ring[:, 5, 0:2048].rearrange("p (c n) -> p c n", c=HC)

        def w2v():
            return ring[:, 5, 2048:4096].rearrange("p (c n) -> p c n", c=HC)

        ld_const, ld_x, ld_edges, ld_emb, ld_ab, ld_rw, ld_att, ld_small, ld_root, ld_ffn = (
            sem(n) for n in ("ld_const", "ld_x", "ld_edges", "ld_emb", "ld_ab", "ld_rw", "ld_att", "ld_small",
                             "ld_root", "ld_ffn"))
        basis_loaded = [sem(f"basis_loaded{q}") for q in range(2)]
        gate_loaded = [sem(f"gate_loaded{q}") for q in range(2)]
        up_loaded = [sem(f"up_loaded{q}") for q in range(2)]
        down_loaded = [sem(f"down_loaded{q}") for q in range(2)]
        dve_chain = sem("dve_chain")
        zeros_set, iota_set = sem("zeros_set"), sem("iota_set")
        normed = sem("normed")
        var_ready, std_ready = sem("var_ready"), sem("std_ready")
        transposed = sem("transposed")
        hT_copied = sem("hT_copied")
        x12_done, x12_copied, logits_done, scaled_done, nmax_ready, exp_done = (
            sem(n) for n in ("x12_done", "x12_copied", "logits_done", "scaled_done", "nmax_ready", "exp_done"))
        rwT_done, rwT_copied = sem("rwT_done"), sem("rwT_copied")
        attw_ready = sem("attw_ready")
        onehot_ready, onehot_used = sem("onehot_ready"), sem("onehot_used")
        combined = [sem(f"combined{q}") for q in range(2)]
        wcopied = [sem(f"wcopied{q}") for q in range(2)]
        ab_ready = sem("ab_ready")
        V_ready, VT_done, VT_copied = sem("V_ready"), sem("VT_done"), sem("VT_copied")
        C_copied, CT_done, CT_copied = sem("C_copied"), sem("CT_done"), sem("CT_copied")
        step_done, step_added = sem("step_done"), sem("step_added")
        router_done, rmax_ready, rexp_done, mask_ready, pos_done, routed = (
            sem(n) for n in ("router_done", "rmax_ready", "rexp_done", "mask_ready", "pos_done", "routed"))
        S_ready, xg_done, xg_copied, ST_done, ST_copied = (
            sem(n) for n in ("S_ready", "xg_done", "xg_copied", "ST_done", "ST_copied"))
        gate_done, up_done, silu_done, hid_ready, hidT_done, hidT_copied, down_done, y_copied, scattered = (
            sem(n) for n in ("gate_done", "up_done", "silu_done", "hid_ready", "hidT_done", "hidT_copied",
                             "down_done", "y_copied", "scattered"))
        glog_done, gate_sig, gx_ready, YT_done, YT_copied, rgcn_done, rgcn_added = (
            sem(n) for n in ("glog_done", "gate_sig", "gx_ready", "YT_done", "YT_copied", "rgcn_done", "rgcn_added"))
        plog_done, pnm_ready, pexp_done, prow_ready, pt_done, prob_copied, pb_done, tied, signed, sel_ready, selT_done, \
            selT_copied, f1_done, f1_biased, gelu_done, act1_ready, a1T_done, a1T_copied, f2_done, x_final = (
                sem(n) for n in ("plog_done", "pnm_ready", "pexp_done", "prow_ready", "pt_done", "prob_copied",
                                 "pb_done", "tied", "signed", "sel_ready", "selT_done", "selT_copied", "f1_done",
                                 "f1_biased", "gelu_done", "act1_ready", "a1T_done", "a1T_copied", "f2_done",
                                 "x_final"))
        over_counted, over_summed, over_flag = sem("over_counted"), sem("over_summed"), sem("over_flag")
        rest_loaded, rest_gate_up, rest_silu, rest_hid, rest_hidT, rest_hidT_copied, rest_down, rest_added = (
            sem(n) for n in ("rest_loaded", "rest_gate_up", "rest_silu", "rest_hid", "rest_hidT", "rest_hidT_copied",
                             "rest_down", "rest_added"))
        stored = sem("stored")

        block = ctx.enter_context(nc.Block())

        BASIS_DMAS = 10

        @block.sync
        def _(sp):
            def basis_chunk(basis_d, c, q):
                for j in range(2):
                    rows = basis_d[0:4 * BG, bass.ds(c * 64 + 32 * j, 32), :].rearrange("(g b) i o -> b i g o", b=4)
                    for b in range(4):
                        sp.dma_start(ring[32 * b:32 * b + 32, 2 * q + j, 0:BG * H].rearrange("p (g o) -> p g o", g=BG),
                                     rows[b]).then_inc(basis_loaded[q], 16)
                for b in range(2):
                    sp.dma_start(ring[64 * b:64 * b + 64, 2 * q + 1, BG * H:BG * H + H],
                                 basis_d[4 * BG + b, bass.ds(c * 64, 64), :]).then_inc(basis_loaded[q], 16)

            for l, basis_d in enumerate((basis1_d, basis2_d)):
                if l == 0:
                    for q in range(2):
                        basis_chunk(basis_d, q, q)
                with sp.Fori(1 - l, WC // 2) as i:
                    for q in range(2):
                        sp.wait_ge(combined[q], i + l * WC // 2)
                        basis_chunk(basis_d, 2 * i + q, q)

            def expert_weights(e, q):
                g, u, d = SLOT[q]
                sp.dma_start(ring[:, g, :].rearrange("p (c f) -> p c f", c=HC),
                             gate_d[bass.ds(e, 1)].rearrange("e (c p) f -> p (e c) f", p=P)).then_inc(gate_loaded[q], 16)
                sp.dma_start(ring[:, u, :].rearrange("p (c f) -> p c f", c=HC),
                             up_d[bass.ds(e, 1)].rearrange("e (c p) f -> p (e c) f", p=P)).then_inc(up_loaded[q], 16)

            def expert_down(e, q):
                sp.dma_start(ring[:, SLOT[q][2], :].rearrange("p (c n) -> p c n", c=FF // P),
                             down_d[bass.ds(e, 1)].rearrange("e (c p) n -> p (e c) n", p=P)).then_inc(down_loaded[q], 16)

            expert_weights(0, 0)
            sp.wait_ge(combined[0], WC)
            expert_down(0, 0)
            sp.wait_ge(combined[1], WC)
            expert_weights(1, 1)
            expert_down(1, 1)
            with sp.Fori(1, NE // 2) as i:
                for q in range(2):
                    sp.wait_ge(up_done, 2 * i + q - 1)
                    expert_weights(2 * i + q, q)
                    sp.wait_ge(down_done, 2 * i + q - 1)
                    expert_down(2 * i + q, q)
            sp.wait_ge(up_done, NE - 1)
            for l, root_d in enumerate((root1_d, root2_d)):
                sp.dma_start(root(l), root_d.rearrange("(c p) n -> p c n", p=P)).then_inc(ld_root, 16)
            sp.dma_start(w2v(), w2_d.rearrange("e f n -> (e f) n").rearrange("(c p) n -> p c n", p=P)).then_inc(ld_ffn, 16)
            for c in range(HC):
                sp.dma_start(w1v()[:, c].rearrange("p (e f) -> p e f", e=E2),
                             w1_d[:, c * P:(c + 1) * P, :].rearrange("e p f -> p e f")).then_inc(ld_ffn, 16)
            sp.wait_ge(scattered, NE)
            sp.wait_ge(over_flag, 1)
            with sp.If(sp.value_load(flag[:], min_val=0, max_val=NT * P * NE) > 0):
                with sp.Fori(0, NE) as e:
                    sp.wait_ge(rest_added, e * NT + 1)
                    for k, (w_d, n) in enumerate(((gate_d, HC), (up_d, HC), (down_d, FF // P))):
                        sp.dma_start(ring[:, k, :].rearrange("p (c f) -> p c f", c=n),
                                     w_d[bass.ds(e, 1)].rearrange("e (c p) f -> p (e c) f", p=P)).then_inc(rest_loaded, 16)
            sp.wait_ge(x_final, 1)
            sp.dma_start(out_d.rearrange("(t p) n -> p t n", p=P), x[:]).then_inc(stored, 16)
            sp.wait_ge(stored, 16)

        @block.gpsimd
        def _(pool):
            pool.memset(zero_b[:], 0.0).then_inc(zeros_set, 1)

        @block.scalar
        def _(act):
            act.dma_start(x[:], x_d.rearrange("(t p) n -> p t n", p=P)).then_inc(ld_x, 16)
            act.dma_start(const[:], const_d).then_inc(ld_const, 16)
            for k, e_d in enumerate((emb1_d, emb2_d)):
                act.dma_start(emb[:, k], e_d.rearrange("(c p) d -> p c d", p=P)).then_inc(ld_emb, 16)
            for l, a_d in enumerate((att1_d, att2_d)):
                act.dma_start(attb[l][:], a_d.unsqueeze(0).broadcast_to([P, 2, NB])).then_inc(ld_att, 16)
            for k, e_d in enumerate((src_d, dst_d, type_d)):
                act.dma_start(idx_i[:, k], e_d.rearrange("(p c) -> p c", p=P)).then_inc(ld_edges, 16)
            act.dma_start(ew[:], ew_d.rearrange("(p c) -> p c", p=P)).then_inc(ld_edges, 16)
            act.dma_start(alpha, alpha_d.unsqueeze(0).broadcast_to([P, 1])).then_inc(ld_ab, 16)
            act.dma_start(beta, beta_d.unsqueeze(0).broadcast_to([P, 1])).then_inc(ld_ab, 16)
            act.dma_start(rw_sb[0:NE], rw_d).then_inc(ld_rw, 16)
            for l, g_d in enumerate((gw1_d, gw2_d)):
                act.dma_start(rw_sb[NE + 2 * l:NE + 2 * l + 2], g_d.rearrange("r n a -> r (n a)")).then_inc(ld_rw, 16)
            for l, b_d in enumerate((bias1_d, bias2_d)):
                act.dma_start(bias[l][:], b_d.unsqueeze(0).broadcast_to([P, H])).then_inc(ld_small, 16)
            act.dma_start(wr[:], wr_d.rearrange("(c p) e -> p c e", p=P)).then_inc(ld_small, 16)
            act.dma_start(b1[:], b1_d.rearrange("e f -> (e f)").unsqueeze(0).broadcast_to([P, E2 * F2])).then_inc(ld_small, 16)
            act.dma_start(b2[:], b2_d).then_inc(ld_small, 16)

            def ln_sqrt(n):
                act.wait_ge(var_ready, n)
                act.activation(rstd[:], rstd[:], ACT.Sqrt).then_inc(std_ready, 1)

            ln_sqrt(1)
            act.wait_ge(logits_done, 1)
            act.mul(lrelu, bank[5][:].rearrange("p (t s) -> p t s", t=NT), 0.2).then_inc(scaled_done, 1)
            act.wait_ge(nmax_ready, 1)
            for t in range(NT):
                act.activation(sim_e[:, t], lrelu[:, t], ACT.Exp, bias=nmax[:, t:t + 1],
                               accum_out=rsum[:, t:t + 1]).then_inc(exp_done, 1)
            act.wait_ge(ld_ab, 32)
            act.activation(small[:, 0:2], small[:, 0:2], ACT.Exp).then_inc(ab_ready, 1)
            for l in range(2):
                with act.Fori(0, WC // 2) as i:
                    for q in range(2):
                        act.wait_ge(combined[q], i + l * WC // 2 + 1)
                        act.copy(wcomb[:, bass.ds(i * 2 + l * WC + q, 1), :].rearrange("p a n -> p (a n)"),
                                 bank[3 + q][:]).then_inc(wcopied[q], 1)
            ln_sqrt(2)
            act.wait_ge(rmax_ready, 1)
            for t in range(NT):
                act.activation(rexp[:, t], RL[:, t], ACT.Exp, bias=m1[:, t:t + 1]).then_inc(rexp_done, 1)

            def copy_xg(e, q):
                act.wait_ge(xg_done, e + 1)
                act.copy(xg[q], bank[5][:, 0:HC * CAP].rearrange("p (c s) -> p c s", c=HC)).then_inc(xg_copied, 1)

            def expert(e, q, last=False):
                act.wait_ge(gate_done, e + 1)
                wait(act, hid_ready, e)
                act.activation(sg, bank[2][:], ACT.Silu).then_inc(silu_done, 1)
                if not last:
                    copy_xg(e + 1, 1 - q)
                act.wait_ge(down_done, e + 1)
                act.copy(y[q], bank[4][:]).then_inc(y_copied, 1)

            copy_xg(0, 0)
            expert(0, 0)
            expert(1, 1)
            with act.Fori(1, NE // 2 - 1) as i:
                for q in range(2):
                    expert(2 * i + q, q)
            expert(NE - 2, 0)
            expert(NE - 1, 1, last=True)

            act.wait_ge(scattered, NE)
            act.wait_ge(over_flag, 1)
            with act.If(act.value_load(flag[:], min_val=0, max_val=NT * P * NE) > 0):
                with act.Fori(0, NE) as e:
                    for k in range(2 * NT):
                        act.wait_ge(rest_gate_up, e * 2 * NT + k + 1)
                        act.activation(sg, bank[2][:], ACT.Silu).then_inc(rest_silu, 1)

            ln_sqrt(3)
            for l in range(2):
                act.wait_ge(glog_done, l + 1)
                act.activation(gates, bank[7][:, 0:4], ACT.Sigmoid).then_inc(gate_sig, 1)
                act.wait_ge(gate_sig, l + 1)
                for t in range(NT):
                    act.mul(gx[:, 1, t], h[:, t], gates[:, 2 * t + 1:2 * t + 2]).then_inc(gx_ready, 1)
                for k in (1, 3):
                    act.wait_ge(YT_done, 4 * l + k + 1)
                    act.copy(YT[:, 2 * k:2 * k + 2], bank[k][:].rearrange("p (c n) -> p c n", c=2)).then_inc(YT_copied, 1)
            ln_sqrt(4)
            act.wait_ge(pnm_ready, 1)
            act.activation(prow[:], bank[7][0:E2, 0:N], ACT.Exp, bias=pnm, accum_out=psum_).then_inc(pexp_done, 1)
            act.wait_ge(prob_copied, 1)
            act.wait_ge(pb_done, 1)
            for k, half in enumerate((range(E2 // 2, E2), range(E2 // 2))):
                wait(act, tied, k)
                for e in half:
                    for t in range(NT):
                        ins = act.activation(sgn[:, t, e], bank[e // 2][:, (e % 2) * N:(e % 2) * N + N], ACT.Sign,
                                             bias=npro[:, t, e:e + 1], accum_out=sig[:, t, e:e + 1])
                ins.then_inc(signed, 1)
            for t in range(NT):
                act.wait_ge(f1_biased, t + 1)
                act.activation(act1[:, t], act1[:, t], ACT.Gelu).then_inc(gelu_done, 1)

        @block.vector
        def _(dve):
            chain = Chain(dve, dve_chain)
            link = chain.link

            def layer_norm(n, before=()):
                for t in range(NT):
                    link(dve.bn_stats(stat[:, t], x[:, t]))
                for t in range(NT):
                    link(dve.bn_aggr(mv[:, t], stat[:, t]))
                dve.tensor_scalar(rstd[:], mv[:, :, 1], EPS, None, ALU.add).then_inc(var_ready, 1)
                dve.wait_ge(std_ready, n)
                link(dve.reciprocal(rstd[:], rstd[:]))
                for t in range(NT):
                    dve.tensor_scalar(h[:, t], x[:, t], mv[:, t, 0:1], rstd[:, t:t + 1], ALU.subtract,
                                      ALU.mult).then_inc(normed, 1)

            def copy_hT(n):
                for t in range(NT):
                    dve.wait_ge(transposed, NT * (n - 1) + t + 1)
                    dve.tensor_copy(hT[:, :, t * P:(t + 1) * P],
                                    bank[5 + t][:].rearrange("p (c n) -> p c n", c=HC)).then_inc(hT_copied, 1)

            dve.wait_ge(ld_x, 16)
            layer_norm(1)
            dve.wait_ge(ld_const, 16)
            link(dve.tensor_copy(iota_b[:], cst("iota")))
            dve.wait_ge(ld_att, 32)
            for l in range(2):
                for b in range(4):
                    q = slice(32 * b, 32 * b + 32)
                    dve.tensor_tensor(
                        attw[l][q].rearrange("p g (r i) -> p g r i", r=2),
                        cst("diag32")[q].unsqueeze(1).unsqueeze(1).broadcast_to([32, BG, 2, 32]),
                        attb[l][q, :, b:4 * BG:4].rearrange("p r g -> p g r").unsqueeze(3).broadcast_to([32, BG, 2, 32]),
                        ALU.mult).then_inc(attw_ready, 1)
                for b in range(2):
                    q = slice(64 * b, 64 * b + 64)
                    dve.tensor_tensor(
                        attl[l][q].rearrange("p (j r i) -> p j r i", j=2, r=2),
                        cst("diag64")[q].rearrange("p (j i) -> p j i", j=2).unsqueeze(2).broadcast_to([64, 2, 2, 32]),
                        attb[l][q, :, 4 * BG + b:4 * BG + b + 1].unsqueeze(1).broadcast_to([64, 2, 2, 32]),
                        ALU.mult).then_inc(attw_ready, 1)
            copy_hT(1)
            dve.wait_ge(x12_done, 1)
            dve.tensor_copy(x12T, bank[7][:]).then_inc(x12_copied, 1)
            dve.wait_ge(rwT_done, 1)
            dve.tensor_copy(rwT[:], bank[6][:, 0:HC * NR].rearrange("p (c e) -> p c e", c=HC)).then_inc(rwT_copied, 1)
            dve.wait_ge(scaled_done, 1)
            link(dve.tensor_tensor(lrelu, lrelu, bank[5][:].rearrange("p (t s) -> p t s", t=NT), ALU.max))
            link(dve.tensor_reduce(rmax, lrelu, AX.X, ALU.max))
            dve.tensor_scalar(nmax, rmax, -1.0, None, ALU.mult).then_inc(nmax_ready, 1)
            dve.wait_ge(ld_edges, 64)
            link(dve.tensor_copy(edge[:, 0:3], idx_i[:]))
            link(dve.tensor_scalar(edge[:, 2], edge[:, 2], 0.0, None, ALU.is_equal))
            link(dve.tensor_scalar(edge[:, 3], edge[:, 2], -1.0, 1.0, ALU.mult, ALU.add))
            link(dve.tensor_copy(wpart[:, 0], ew[:]))
            link(dve.tensor_tensor(ew[:], ew[:], wpart[:, 0], ALU.subtract))
            link(dve.tensor_copy(wpart[:, 1], ew[:]))
            link(dve.tensor_tensor(ew[:], ew[:], wpart[:, 1], ALU.subtract))
            link(dve.tensor_copy(wpart[:, 2], ew[:]))
            link(dve.tensor_copy(edge[:, 4:7], wpart[:]))
            def edge_onehots(i):
                wait(dve, onehot_used, i * NOH)
                for k in range(NOH):
                    col = [edge[:, m, bass.ds(i * NOH + k, 1)] for m in range(7)]
                    dve.tensor_scalar(onehot[:, k, 0], iota_b[:], col[0], None, ALU.is_equal)
                    for m in range(5):
                        ins = dve.tensor_scalar(onehot[:, k, 1 + m], iota_b[:], col[1], col[2 + m],
                                                ALU.is_equal, ALU.mult)
                    ins.then_inc(onehot_ready, 1)

            edge_onehots(0)
            with dve.Fori(1, ECH // NOH) as i:
                edge_onehots(i)

            dve.wait_ge(exp_done, NT)
            dve.wait_ge(onehot_used, ECH)
            link(dve.reciprocal(rinv, rsum))
            A = bank[0][:].rearrange("p (t s) -> p t s", t=NT)
            for t in range(NT):
                link(dve.scalar_tensor_tensor(V[:, t], sim_e[:, t], rinv[:, t:t + 1], A[:, t], ALU.mult, ALU.mult,
                                              accum_out=norm[:, t:t + 1]))
            for t in range(NT):
                d = V[:, t, t * P:(t + 1) * P]
                dve.tensor_tensor(d, d, ident, ALU.add).then_inc(V_ready, 1)
            for t in range(NT):
                dve.tensor_copy(Csb[:, t], bank[1 + t][:].rearrange("p (r s) -> p r s", r=2)).then_inc(C_copied, 1)
            dve.wait_ge(ab_ready, 1)
            link(dve.tensor_tensor(ab, alpha, beta, ALU.add))
            link(dve.tensor_scalar(den, norm, alpha, ab, ALU.mult, ALU.add))
            link(dve.reciprocal(rden, den))
            link(dve.tensor_scalar(ra, rden, alpha, None, ALU.mult))
            link(dve.tensor_scalar(rb, rden, beta, None, ALU.mult))
            for t in range(NT):
                link(dve.tensor_scalar(inb[:, t], h[:, t], rb[:, t:t + 1], None, ALU.mult))
            dve.wait_ge(VT_done, 1)
            dve.tensor_copy(VT, bank[5][:].rearrange("p (t s) -> p t s", t=NT)).then_inc(VT_copied, 1)
            for r in range(2):
                dve.wait_ge(CT_done, r + 1)
                dve.tensor_copy(CT[:, r], bank[3 + r][:].rearrange("p (t s) -> p t s", t=NT)).then_inc(CT_copied, 1)
            for k in range(ITERS):
                for t in range(NT):
                    dve.wait_ge(step_done, NT * k + t + 1)
                    dve.scalar_tensor_tensor(out5[:, k % 2, t], bank[6 + t][:], ra[:, t:t + 1], inb[:, t],
                                             ALU.mult, ALU.add).then_inc(step_added, 1)
            dve.wait_ge(step_added, NT * ITERS)
            link(dve.tensor_tensor(x[:], x[:], out5[:, (ITERS - 1) % 2], ALU.add))

            layer_norm(2)
            copy_hT(2)
            dve.wait_ge(router_done, 1)
            link(dve.tensor_copy(RL, bank[7][:, 0:NT * NE].rearrange("p (t e) -> p t e", t=NT)))
            link(dve.tensor_reduce(m1, RL, AX.X, ALU.max))
            dve.tensor_scalar(m1, m1, -1.0, None, ALU.mult).then_inc(rmax_ready, 1)
            eq = lrelu.rearrange("p t (a b) -> p t a b", a=NE)
            for t in range(NT):
                other = RL[:, t].unsqueeze(1).broadcast_to([P, NE, NE])
                own = RL[:, t].unsqueeze(2).broadcast_to([P, NE, NE])
                link(dve.tensor_tensor(cmpg[:, t], other, own, ALU.is_gt))
                link(dve.tensor_tensor(eq[:, t], other, own, ALU.is_equal))
                link(dve.tensor_tensor(eq[:, t], eq[:, t],
                                       cst("earlier_expert").rearrange("p (a b) -> p a b", a=NE), ALU.mult))
            link(dve.tensor_tensor(cmpg, cmpg, eq, ALU.add))
            link(dve.tensor_reduce(rank, cmpg, AX.X, ALU.add))
            dve.tensor_scalar(mask, rank, 1.5, None, ALU.is_lt).then_inc(mask_ready, 1)
            dve.wait_ge(mask_ready, 1)
            dve.wait_ge(rexp_done, NT)
            link(dve.tensor_tensor(rexp, rexp, mask, ALU.mult))
            link(dve.tensor_reduce(s1, rexp, AX.X, ALU.add))
            link(dve.reciprocal(r1, s1))
            for t in range(NT):
                link(dve.tensor_scalar(ce[:, t], rexp[:, t], r1[:, t:t + 1], None, ALU.mult))
            dve.wait_ge(pos_done, 1)
            pos = bank[7][:, 64:64 + NT * NE].rearrange("p (t e) -> p t e", t=NT)
            link(dve.scalar_tensor_tensor(posm, pos, 1.0, mask, ALU.add, ALU.mult))
            link(dve.tensor_scalar(posm, posm, -1.0, None, ALU.add))
            link(dve.tensor_scalar(over, posm, LIMIT - 0.5, None, ALU.is_ge))
            link(dve.tensor_tensor(ce_over, ce, over, ALU.mult))
            dve.tensor_reduce(over_n, over, AX.XY, ALU.add).then_inc(over_counted, 1)
            dve.wait_ge(over_summed, 1)
            dve.tensor_copy(flag[:], bank[7][0:1, 128:129]).then_inc(over_flag, 1)

            slots = cst("slots")

            def select(e, q):
                for t in range(NT):
                    dve.tensor_scalar(S[q][:, t], slots[:, 0:CAP], posm[:, t, bass.ds(e, 1)], None,
                                      ALU.is_equal).then_inc(S_ready, 1)
                    dve.tensor_scalar(SW[q][:, t], slots, posm[:, t, bass.ds(e, 1)], ce[:, t, bass.ds(e, 1)],
                                      ALU.is_equal, ALU.mult).then_inc(S_ready, 1)

            def copy_ST(e, q):
                dve.wait_ge(ST_done, e + 1)
                dve.tensor_copy(ST[q], bank[6][:, 0:N]).then_inc(ST_copied, 1)

            def expert(e, q, last=False):
                if not last:
                    select(e + 1, 1 - q)
                dve.wait_ge(silu_done, e + 1)
                dve.wait_ge(up_done, e + 1)
                dve.tensor_tensor(hid[q], sg, bank[3][:], ALU.mult).then_inc(hid_ready, 1)
                if not last:
                    wait(dve, scattered, e)
                    copy_ST(e + 1, 1 - q)
                dve.wait_ge(hidT_done, e + 1)
                dve.tensor_copy(hidT[q], bank[7][:]).then_inc(hidT_copied, 1)

            select(0, 0)
            copy_ST(0, 0)
            expert(0, 0)
            expert(1, 1)
            with dve.Fori(1, NE // 2 - 1) as i:
                for q in range(2):
                    expert(2 * i + q, q)
            expert(NE - 2, 0)
            expert(NE - 1, 1, last=True)
            dve.wait_ge(scattered, NE)
            for t in range(NT):
                link(dve.tensor_tensor(x[:, t], x[:, t], bank[t][:], ALU.add))

            with dve.If(dve.value_load(flag[:], min_val=0, max_val=NT * P * NE) > 0):
                dve.tensor_copy(small[:, 1022:1023], over_n).then_inc(rest_added, 1)
                with dve.Fori(0, NE) as e:
                    for t in range(NT):
                        for f in range(2):
                            k = 2 * t + f
                            dve.wait_ge(rest_silu, e * 2 * NT + k + 1)
                            dve.tensor_tensor(hid[0], sg, bank[3][:], ALU.mult).then_inc(rest_hid, 1)
                            dve.wait_ge(rest_hidT, e * 2 * NT + k + 1)
                            dve.tensor_copy(hidT[0], bank[7][:]).then_inc(rest_hidT_copied, 1)
                        dve.wait_ge(rest_down, e * NT + t + 1)
                        dve.scalar_tensor_tensor(x[:, t], bank[4][:], ce_over[:, t, bass.ds(e, 1)], x[:, t],
                                                 ALU.mult, ALU.add).then_inc(rest_added, 1)
                dve.wait_ge(rest_added, NE * NT + 1)

            layer_norm(3)
            dve.wait_ge(ld_small, 16 * 5)
            for l in range(2):
                copy_hT(3 + l)
                dve.wait_ge(gate_sig, l + 1)
                for t in range(NT):
                    dve.tensor_scalar(gx[:, 0, t], h[:, t], gates[:, 2 * t:2 * t + 1], None,
                                      ALU.mult).then_inc(gx_ready, 1)
                for k in (0, 2):
                    dve.wait_ge(YT_done, 4 * l + k + 1)
                    dve.tensor_copy(YT[:, 2 * k:2 * k + 2],
                                    bank[k][:].rearrange("p (c n) -> p c n", c=2)).then_inc(YT_copied, 1)
                for t in range(NT):
                    dve.wait_ge(rgcn_done, NT * l + t + 1)
                    if l == 0:
                        dve.wait_ge(gx_ready, 4)
                        link(dve.tensor_tensor(h[:, t], bank[5 + t][:], bias[l][:], ALU.add))
                        dve.tensor_scalar(h[:, t], h[:, t], 0.0, None, ALU.max).then_inc(normed, 1)
                    else:
                        link(dve.tensor_tensor(x[:, t], x[:, t], bias[l][:], ALU.add))
                        link(dve.tensor_tensor(x[:, t], x[:, t], bank[5 + t][:], ALU.add))

            layer_norm(4)
            copy_hT(5)
            dve.wait_ge(plog_done, 1)
            link(dve.tensor_reduce(pmx, bank[7][0:E2, 0:N], AX.X, ALU.max))
            dve.tensor_scalar(pnm, pmx, -1.0, None, ALU.mult).then_inc(pnm_ready, 1)
            for t in range(NT):
                dve.wait_ge(f1_done, t + 1)
                dve.tensor_tensor(act1[:, t], bank[5 + t][:], b1[:], ALU.add).then_inc(f1_biased, 1)
            dve.wait_ge(pexp_done, 1)
            link(dve.reciprocal(pinv, psum_))
            dve.tensor_scalar(prow[:], prow[:], pinv, None, ALU.mult).then_inc(prow_ready, 1)
            dve.wait_ge(pt_done, 1)
            link(dve.tensor_copy(prob, bank[7][:, 256:256 + NT * E2].rearrange("p (t e) -> p t e", t=NT)))
            dve.tensor_scalar(npro, prob, -1.0, None, ALU.mult).then_inc(prob_copied, 1)
            dve.wait_ge(pb_done, 1)
            order = cst("tie_order").rearrange("p (t s) -> p t s", t=NT)
            for k, half in enumerate((range(E2 // 2), range(E2 // 2, E2))):
                wait(dve, signed, k)
                for e in half:
                    for t in range(NT):
                        ins = dve.scalar_tensor_tensor(cmp[:, t, e], bank[e // 2][:, (e % 2) * N:(e % 2) * N + N],
                                                       prob[:, t, e:e + 1], order[:, t], ALU.is_equal, ALU.mult,
                                                       accum_out=tie[:, t, e:e + 1])
                ins.then_inc(tied, 1)
            dve.wait_ge(tied, 2)
            dve.wait_ge(signed, 2)
            link(dve.scalar_tensor_tensor(tie, sig, 0.5, tie, ALU.mult, ALU.add))
            link(dve.tensor_scalar(tie, tie, float(C2 - N // 2) - 0.25, None, ALU.is_lt))
            dve.tensor_tensor(sel, tie, prob, ALU.mult).then_inc(sel_ready, 1)
            dve.wait_ge(sel_ready, 1)
            for t in range(NT):
                dve.wait_ge(gelu_done, t + 1)
                a = act1[:, t].rearrange("p (e f) -> p e f", e=E2)
                dve.tensor_tensor(a, a, sel[:, t].unsqueeze(2).broadcast_to([P, E2, F2]),
                                  ALU.mult).then_inc(act1_ready, 1)
            dve.wait_ge(selT_done, 1)
            dve.tensor_copy(PT[:], bank[7][0:E2, 0:N]).then_inc(selT_copied, 1)
            for t in range(NT):
                dve.wait_ge(a1T_done, t + 1)
                dve.tensor_copy(act1T[:, :, t * P:(t + 1) * P],
                                bank[5 + t][:].rearrange("p (c n) -> p c n", c=HC)).then_inc(a1T_copied, 1)
            for t in range(NT):
                dve.wait_ge(f2_done, t + 1)
                link(dve.tensor_tensor(x[:, t], x[:, t], bank[t][:], ALU.add))
            dve.tensor_copy(small[:, 0:1], small[:, 1:2]).then_inc(x_final, 1)

        @block.tensor
        def _(pe):
            def mm(out, lhsT, rhs, start, stop):
                return pe.matmul(out, lhsT, rhs, start=start, stop=stop, skip_group_check=True)

            def transpose_h(n):
                for t in range(NT):
                    pe.wait_ge(normed, NT * (n - 1) + t + 1)
                    for c in range(HC):
                        ins = pe.transpose(bank[5 + t][:, c * P:(c + 1) * P], h[:, t, c * P:(c + 1) * P], ident)
                    ins.then_inc(transposed, 1)

            pe.wait_ge(ld_const, 16)
            transpose_h(1)
            pe.wait_ge(hT_copied, NT)
            pe.wait_ge(ld_emb, 32)
            for k in range(2):
                for c in range(HC):
                    ins = mm(bank[7][:, k * N:(k + 1) * N], emb[:, k, c], hT[:, c], c == 0, c == HC - 1)
            ins.then_inc(x12_done, 1)
            pe.wait_ge(ld_rw, 48)
            for c in range(HC):
                ins = pe.transpose(bank[6][:, c * NR:(c + 1) * NR], rw_sb[:, c * P:(c + 1) * P], ident[0:NR, 0:NR])
            ins.then_inc(rwT_done, 1)
            pe.wait_ge(x12_copied, 1)
            for t in range(NT):
                ins = mm(bank[5][:, t * N:(t + 1) * N], x12T[:, t * P:(t + 1) * P], x12T[:, N:2 * N], True, True)
            ins.then_inc(logits_done, 1)

            pe.wait_ge(zeros_set, 1)
            for k in range(3):
                mm(bank[k][:], zero_b[:, 0:P], zero_b[:], True, False)

            def edges(ch, k):
                pe.wait_ge(onehot_ready, ch + 1)
                for t in range(NT):
                    lhsT = onehot[:, k, 0, t * P:(t + 1) * P]
                    mm(bank[1 + t][:], lhsT, onehot[:, k, 1:3].rearrange("p a n -> p (a n)"), False, False)
                    for m in range(3):
                        ins = mm(bank[0][:, t * N:(t + 1) * N], lhsT, onehot[:, k, 3 + m], False, False)
                ins.then_inc(onehot_used, 1)

            def combine(l, i, q):
                pe.wait_ge(basis_loaded[q], (i + l * WC // 2 + 1) * 16 * BASIS_DMAS)
                wait(pe, wcopied[q], i + l * WC // 2)
                acc = bank[3 + q]
                for g in range(BG):
                    for j in range(2):
                        mm(acc[64 * j:64 * j + 64, :], attw[l][:, g], ring[:, 2 * q + j, g * H:(g + 1) * H],
                           g == 0, False)
                mm(acc[:], attl[l][:], ring[:, 2 * q + 1, BG * H:(BG + 1) * H], False, True).then_inc(combined[q], 1)

            pe.wait_ge(attw_ready, 12)
            EPC = ECH // (2 * WC)

            def combine_pair(l, i):
                for q in range(2):
                    combine(l, i, q)
                    for k in range(EPC):
                        edges((i * 2 + l * WC + q) * EPC + k, k % NOH)

            combine_pair(0, 0)
            for l in range(2):
                with pe.Fori(1 - l, WC // 2) as i:
                    combine_pair(l, i)

            pe.wait_ge(V_ready, NT)
            for s in range(NT):
                for t in range(NT):
                    ins = pe.transpose(bank[5][:, s * N + t * P:s * N + (t + 1) * P], V[:, t, s * P:(s + 1) * P], ident)
            ins.then_inc(VT_done, 1)
            pe.wait_ge(C_copied, NT)
            for q in range(2):
                pe.wait_ge(wcopied[q], WC)
            for r in range(2):
                for d in range(NT):
                    for t in range(NT):
                        ins = pe.transpose(bank[3 + r][:, d * N + t * P:d * N + (t + 1) * P],
                                           Csb[:, t, r, d * P:(d + 1) * P], ident)
                ins.then_inc(CT_done, 1)
            pe.wait_ge(VT_copied, 1)
            for k in range(ITERS):
                if k:
                    pe.wait_ge(step_added, NT * k)
                for t in range(NT):
                    for s in range(NT):
                        cur = h[:, s] if k == 0 else out5[:, (k - 1) % 2, s]
                        ins = mm(bank[6 + t][:], VT[:, s, t * P:(t + 1) * P], cur, s == 0, s == NT - 1)
                    ins.then_inc(step_done, 1)

            transpose_h(2)
            pe.wait_ge(hT_copied, 2 * NT)
            pe.wait_ge(rwT_copied, 1)
            for t in range(NT):
                for c in range(HC):
                    ins = mm(bank[7][:, t * NE:(t + 1) * NE], hT[:, c, t * P:(t + 1) * P], rwT[:, c, 0:NE], c == 0, c == HC - 1)
            ins.then_inc(router_done, 1)
            pe.wait_ge(mask_ready, 1)
            mm(bank[7][:, 64:64 + NE], cst("before"), mask[:, 0], True, True)
            mm(bank[7][:, 64 + NE:64 + 2 * NE], cst("before"), mask[:, 1], True, False)
            mm(bank[7][:, 64 + NE:64 + 2 * NE], cst("ones"), mask[:, 0], False, True).then_inc(pos_done, 1)

            pe.wait_ge(over_counted, 1)
            mm(bank[7][0:1, 128:129], over_n, cst("ones")[:, 0:1], True, True).then_inc(over_summed, 1)

            for t in range(NT):
                mm(bank[t][:], zero_b[:, 0:P], zero_b[:], True, False)

            def gather(e, q):
                pe.wait_ge(S_ready, 4 * (e + 1))
                wait(pe, xg_copied, e)
                for c in range(HC):
                    for s in range(NT):
                        ins = mm(bank[5][:, c * CAP:(c + 1) * CAP], h[:, s, c * P:(c + 1) * P], S[q][:, s],
                                 s == 0, s == NT - 1)
                ins.then_inc(xg_done, 1)
                wait(pe, ST_copied, e)
                for t in range(NT):
                    ins = pe.transpose(bank[6][:, t * P:(t + 1) * P], SW[q][:, t], ident)
                ins.then_inc(ST_done, 1)

            def scatter(e, q):
                pe.wait_ge(y_copied, e + 1)
                pe.wait_ge(ST_copied, e + 1)
                for t in range(NT):
                    ins = mm(bank[t][:], ST[q][:, t * P:(t + 1) * P], y[q], False, False)
                ins.then_inc(scattered, 1)

            def expert(e, q, first=False, last=False):
                g, u, d = SLOT[q]
                pe.wait_ge(gate_loaded[q], 16 * (e // 2 + 1) if isinstance(e, int) else (e - q) * 8 + 16)
                pe.wait_ge(xg_copied, e + 1)
                wait(pe, silu_done, e)
                for c in range(HC):
                    for f in range(2):
                        ins = mm(bank[2][64 * f:64 * f + 64, :], xg[q][:, c], ring[:, g, c * FF + f * 512:c * FF + f * 512 + 512],
                                 c == 0, c == HC - 1)
                ins.then_inc(gate_done, 1)
                pe.wait_ge(up_loaded[q], 16 * (e // 2 + 1) if isinstance(e, int) else (e - q) * 8 + 16)
                wait(pe, hid_ready, e)
                for c in range(HC):
                    for f in range(2):
                        ins = mm(bank[3][64 * f:64 * f + 64, :], xg[q][:, c], ring[:, u, c * FF + f * 512:c * FF + f * 512 + 512],
                                 c == 0, c == HC - 1)
                ins.then_inc(up_done, 1)
                if not first:
                    scatter(e - 1, 1 - q)
                if not last:
                    gather(e + 1, 1 - q)
                pe.wait_ge(hid_ready, e + 1)
                wait(pe, hidT_copied, e)
                for c in range(HC):
                    ins = pe.transpose(bank[7][:, c * P:(c + 1) * P], hid[q][:, c * P:(c + 1) * P], ident)
                ins.then_inc(hidT_done, 1)
                pe.wait_ge(down_loaded[q], 16 * (e // 2 + 1) if isinstance(e, int) else (e - q) * 8 + 16)
                pe.wait_ge(hidT_copied, e + 1)
                wait(pe, y_copied, e)
                for c in range(HC):
                    for f in range(2):
                        ins = mm(bank[4][64 * f:64 * f + 64, :], hidT[q][:, c * P + 64 * f:c * P + 64 * f + 64],
                                 ring[:, d, (f * HC + c) * H:(f * HC + c + 1) * H], c == 0, c == HC - 1)
                ins.then_inc(down_done, 1)

            gather(0, 0)
            expert(0, 0, first=True)
            expert(1, 1)
            with pe.Fori(1, NE // 2 - 1) as i:
                for q in range(2):
                    expert(2 * i + q, q)
            expert(NE - 2, 0)
            expert(NE - 1, 1, last=True)
            scatter(NE - 1, 1)

            pe.wait_ge(y_copied, NE)
            with pe.If(pe.value_load(flag[:], min_val=0, max_val=NT * P * NE) > 0):
                with pe.Fori(0, NE) as e:
                    pe.wait_ge(rest_loaded, e * 48 + 48)
                    for t in range(NT):
                        for f in range(2):
                            k = 2 * t + f
                            for w, b in ((0, 2), (1, 3)):
                                for c in range(HC):
                                    ins = mm(bank[b][:], hT[:, c, t * P:(t + 1) * P],
                                             ring[:, w, c * FF + f * 512:c * FF + f * 512 + 512], c == 0, c == HC - 1)
                            ins.then_inc(rest_gate_up, 1)
                            pe.wait_ge(rest_hid, e * 2 * NT + k + 1)
                            for c in range(HC):
                                ins = pe.transpose(bank[7][:, c * P:(c + 1) * P], hid[0][:, c * P:(c + 1) * P], ident)
                            ins.then_inc(rest_hidT, 1)
                            pe.wait_ge(rest_hidT_copied, e * 2 * NT + k + 1)
                            pe.wait_ge(rest_added, e * NT + t + 1)
                            for c in range(HC):
                                ins = mm(bank[4][:], hidT[0][:, c * P:(c + 1) * P],
                                         ring[:, 2, (f * HC + c) * H:(f * HC + c + 1) * H],
                                         f == 0 and c == 0, f == 1 and c == HC - 1)
                        ins.then_inc(rest_down, 1)

            pe.wait_ge(ld_root, 32)
            pe.wait_ge(ld_small, 16 * 5)
            for l in range(2):
                transpose_h(3 + l)
                pe.wait_ge(hT_copied, (3 + l) * NT)
                for t in range(NT):
                    for c in range(HC):
                        ins = mm(bank[7][:, 2 * t:2 * t + 2], hT[:, c, t * P:(t + 1) * P], rwT[:, c, NE + 2 * l:NE + 2 * l + 2], c == 0, c == HC - 1)
                ins.then_inc(glog_done, 1)
                for t in range(NT):
                    for c in range(HC):
                        mm(bank[5 + t][:], hT[:, c, t * P:(t + 1) * P], root(l)[:, c], c == 0, False)
                pe.wait_ge(gx_ready, 4 * (l + 1))
                wait(pe, YT_copied, 4 * l)
                pe.wait_ge(CT_copied, 2)
                for k in range(WC // 2):
                    for c in (2 * k, 2 * k + 1):
                        for s in range(NT):
                            for j in range(2):
                                for r in range(2):
                                    o = 32 * (2 * j + r)
                                    ins = mm(bank[k][o:o + 32, (c % 2) * N:(c % 2 + 1) * N],
                                             gx[:, r, s, c * 64 + 32 * j:c * 64 + 32 * j + 32], CT[:, r, s],
                                             s == 0, s == NT - 1)
                    ins.then_inc(YT_done, 1)
                pe.wait_ge(YT_copied, 4 * (l + 1))
                for t in range(NT):
                    for c in range(WC):
                        ins = mm(bank[5 + t][:], YT[:, c, t * P:(t + 1) * P], wcomb[:, l * WC + c], False, c == WC - 1)
                    ins.then_inc(rgcn_done, 1)

            transpose_h(5)
            pe.wait_ge(hT_copied, 5 * NT)
            for c in range(HC):
                ins = mm(bank[7][0:E2, 0:N], wr[:, c], hT[:, c], c == 0, c == HC - 1)
            ins.then_inc(plog_done, 1)
            pe.wait_ge(ld_ffn, 16 * (1 + HC))
            for t in range(NT):
                for c in range(HC):
                    ins = mm(bank[5 + t][:], hT[:, c, t * P:(t + 1) * P], w1v()[:, c], c == 0, c == HC - 1)
                ins.then_inc(f1_done, 1)
            pe.wait_ge(prow_ready, 1)
            for t in range(NT):
                ins = pe.transpose(bank[7][:, 256 + t * E2:256 + (t + 1) * E2], prow[:, t * P:(t + 1) * P], ident[0:E2, 0:E2])
            ins.then_inc(pt_done, 1)
            pe.wait_ge(prob_copied, 1)
            for e in range(E2):
                for t in range(NT):
                    ins = pe.transpose(bank[e // 2][:, (e % 2) * N + t * P:(e % 2) * N + (t + 1) * P],
                                       prob[:, t, e:e + 1].broadcast_to([P, P]), ident)
            ins.then_inc(pb_done, 1)
            pe.wait_ge(sel_ready, 1)
            for t in range(NT):
                ins = pe.transpose(bank[7][0:E2, t * P:(t + 1) * P], sel[:, t], ident)
            ins.then_inc(selT_done, 1)
            for t in range(NT):
                pe.wait_ge(act1_ready, t + 1)
                for c in range(HC):
                    ins = pe.transpose(bank[5 + t][:, c * P:(c + 1) * P], act1[:, t, c * P:(c + 1) * P], ident)
                ins.then_inc(a1T_done, 1)
            pe.wait_ge(selT_copied, 1)
            for t in range(NT):
                mm(bank[t][:], PT[:, t * P:(t + 1) * P], b2[:], True, False)
                pe.wait_ge(a1T_copied, t + 1)
                for c in range(HC):
                    ins = mm(bank[t][:], act1T[:, c, t * P:(t + 1) * P], w2v()[:, c], False, c == HC - 1)
                ins.then_inc(f2_done, 1)


_INS = ["x", "src", "dst", "edge_type_2", "edge_weight", "L0_gnn_emb_1", "L0_gnn_emb_2", "L0_gnn_alpha_p",
        "L0_gnn_beta_p", "L0_ffn_router_w", "L0_ffn_gate_w", "L0_ffn_up_w", "L0_ffn_down_w", "L1_gnn_basis1",
        "L1_gnn_att1", "L1_gnn_gate_w1", "L1_gnn_root1", "L1_gnn_bias1", "L1_gnn_basis2", "L1_gnn_att2",
        "L1_gnn_gate_w2", "L1_gnn_root2", "L1_gnn_bias2", "L1_ffn_Wr", "L1_ffn_W1", "L1_ffn_b1", "L1_ffn_W2",
        "L1_ffn_b2"]


def constants():
    import numpy as np
    c = np.zeros((P, NCONST), np.float32)

    def put(name, value):
        a, b = CONST[name]
        c[:, a:b] = value

    p = np.arange(P)
    put("ident", np.eye(P))
    put("before", p[:, None] < p[None, :])
    put("ones", 1.0)
    put("diag32", p[:, None] % 32 == np.arange(32)[None, :])
    put("diag64", p[:, None] % 64 == np.arange(64)[None, :])
    e = np.arange(NE)
    put("earlier_expert", (e[None, :] < e[:, None]).reshape(1, -1))
    t = np.arange(NT)[None, :, None] * P + p[:, None, None]
    put("tie_order", np.where(np.arange(N)[None, None, :] < t, 0.5, -0.5).reshape(P, -1))
    put("iota", np.arange(N))
    s = np.arange(2 * CAP) % CAP
    put("slots", np.where(s < LIMIT, s, -5))
    return c


def kernel(**inputs):
    import numpy as _np
    import concourse.bacc as _bacc
    from concourse import mybir as _mybir
    from concourse.bass_utils import run_bass_kernel_spmd as _run

    nc = _bacc.Bacc("TRN2", target_bir_lowering=False, num_devices=1)
    arrays, args = {}, []
    for name in _INS + ["shape_constants"]:
        a = constants() if name == "shape_constants" else _np.ascontiguousarray(inputs[name])
        arrays[f"in_{name}_dram"] = a
        args.append(nc.dram_tensor(f"in_{name}_dram", a.shape, _mybir.dt.from_np(a.dtype), kind="ExternalInput").ap())
    args.append(nc.dram_tensor("out_0_dram", (N, H), F32, kind="ExternalOutput").ap())
    build(nc, *args)
    r = _run(nc, [arrays], core_ids=[0])
    return r.results[0]["out_0_dram"]
```

```python
from contextlib import ExitStack

import concourse.bass as bass
from concourse import mybir

F32 = mybir.dt.float32
BF16 = mybir.dt.bfloat16
I32 = mybir.dt.int32
ALU = mybir.AluOpType
ACT = mybir.ActivationFunctionType
AX = mybir.AxisListType

P = 128
N = 256
NT = N // P
H = 512
HC = H // P
E_EDGES = 8192
ECH = E_EDGES // P
ITERS = 5
NE, FF = 16, 1024
NR = NE + 4
CAP = 64
NB = 30
BK = [P, P, P, (NB - 24) * 16]
BG = len(BK)
WC = H // 64
EARLY = 2
EPAIRS = 3
EPC = 12
EFIRST = ECH - 2 * EPC * (EPAIRS - 1)
E2, F2, C2 = 8, 64, 128
EPS = 1e-5

CONST = {}
_at = 0
for _name, _n in (("ident", P), ("before", P), ("ones", P), ("diag16", 16), ("block16", 8),
                  ("regroup", P),
                  ("earlier_expert", NE * NE), ("tie_order", NT * N), ("iota", N), ("slots", 2 * CAP)):
    CONST[_name] = (_at, _at + _n)
    _at += _n
NCONST = _at
LIMIT = CAP


def wait(eng, sem, value):
    if not (isinstance(value, int) and value <= 0):
        eng.wait_ge(sem, value)


class Chain:

    def __init__(self, eng, sem, base=0):
        self.eng, self.sem, self.base, self.n = eng, sem, base, 0

    def link(self, ins):
        self.n += 1
        ins.then_inc(self.sem, 1)
        self.eng.wait_ge(self.sem, self.base + self.n)


def build(nc, x_d, src_d, dst_d, type_d, ew_d, emb1_d, emb2_d, alpha_d, beta_d, rw_d, gate_d, up_d, down_d,
          basis1_d, att1_d, gw1_d, root1_d, bias1_d, basis2_d, att2_d, gw2_d, root2_d, bias2_d,
          wr_d, w1_d, b1_d, w2_d, b2_d, const_d, out_d):
    with ExitStack() as ctx:
        def sb(name, shape, dt=F32):
            return ctx.enter_context(nc.sbuf_tensor(name, shape, dt))

        def sem(name):
            return ctx.enter_context(nc.semaphore(name))

        bank = [ctx.enter_context(nc.psum_tensor(f"bank{i}", [P, 512], F32)) for i in range(8)]

        ring = sb("ring", [P, 6, 4096])
        wcomb = sb("wcomb", [P, 2 * WC, H])
        const = sb("const", [P, NCONST])

        def cst(name):
            a, b = CONST[name]
            return const[:, a:b]

        ident = cst("ident")
        iota_b = sb("iota_b", [P, N], BF16)
        zero_b = sb("zero_b", [P, 512], BF16)
        x = sb("x", [P, NT, H])
        h = sb("h", [P, NT, H])
        hT = sb("hT", [P, HC, N])
        CT = sb("CT", [P, 2, NT, N])
        attw = [sb(f"attw{l}", [P, BG, 2, 16]) for l in range(2)]
        atts = sb("atts", [P, 2, BG, 2])
        wstage = sb("wstage", [P, 2, H])
        root = sb("root", [P, HC, H])
        attb = [sb(f"attb{l}", [P, 2, NB]) for l in range(2)]
        rwT = sb("rwT", [P, HC, NR])
        bias = [sb(f"bias{l}", [P, H]) for l in range(2)]
        stat = sb("stat", [P, NT, 6])
        mv = sb("mv", [P, NT, 2])
        rstd = sb("rstd", [P, NT])
        area = sb("area", [P, 4096 + 2048])
        small = sb("small", [P, 1024])

        NOH = 4
        onehot = area[:, 0:NOH * 5 * N // 2].bitcast(BF16).rearrange("p (q k n) -> p q k n", q=NOH, k=5)
        emb = area[:, 3072:4096].rearrange("p (k c d) -> p k c d", k=2, c=HC)
        sim_e = area[:, 4096:4608].rearrange("p (t s) -> p t s", t=NT)
        lrelu = area[:, 4608:5120].rearrange("p (t s) -> p t s", t=NT)
        x12T = area[:, 5120:5632]
        V = area[:, 0:512].rearrange("p (t s) -> p t s", t=NT)
        VT = area[:, 512:1024].rearrange("p (t s) -> p t s", t=NT)
        inb = area[:, 1024:2048].rearrange("p (t n) -> p t n", t=NT)
        out5 = area[:, 3072:5120].rearrange("p (q t n) -> p q t n", q=2, t=NT)
        xg = [area[:, 512 * q:512 * q + 256].rearrange("p (c s) -> p c s", c=HC) for q in range(2)]
        ST = [area[:, 512 * q + 256:512 * q + 512] for q in range(2)]
        S = [area[:, 1024 + 128 * q:1152 + 128 * q].rearrange("p (t s) -> p t s", t=NT) for q in range(2)]
        SW = [area[:, 1280 + 256 * q:1536 + 256 * q].rearrange("p (t s) -> p t s", t=NT) for q in range(2)]
        sg = area[:, 1792:2304]
        hid = [area[:, 2304 + 512 * q:2816 + 512 * q] for q in range(2)]
        hidT = [area[:, 3328 + 512 * q:3840 + 512 * q] for q in range(2)]
        y = [area[:, 4352 + 512 * q:4864 + 512 * q] for q in range(2)]
        count_onehot = area[:, 5376:6144].bitcast(BF16).rearrange("p (q k n) -> p q k n", q=2, k=3)
        gx = area[:, 0:2048].rearrange("p (r t n) -> p r t n", r=2, t=NT)
        YT = area[:, 2048:4096].rearrange("p (c n) -> p c n", c=WC)
        act1 = area[:, 0:1024].rearrange("p (t n) -> p t n", t=NT)
        act1T = area[:, 1024:2048].rearrange("p (c n) -> p c n", c=HC)
        cmp = area[:, 2048:4096].bitcast(BF16).rearrange("p (t e s) -> p t e s", t=NT, e=E2)
        sgn = area[:, 4096:6144].bitcast(BF16).rearrange("p (t e s) -> p t e s", t=NT, e=E2)

        rw_sb = area[0:NR, 5632:6144]
        idx_i = sb("idx_i", [P, 3, ECH], I32)
        ew = sb("ew", [P, ECH])
        edge = sb("edge", [P, 7, ECH])
        wpart = sb("wpart", [P, 3, ECH], BF16)
        wr = sb("wr", [P, HC, E2])
        b1 = sb("b1", [P, E2 * F2])
        b2 = sb("b2", [E2, H])

        def sm(a, n=1):
            return small[:, a:a + n]

        alpha, beta = sm(0), sm(1)
        rmax, nmax, rsum, rinv, norm = (sm(2 + 2 * i, 2) for i in range(5))
        den, rden, ra, rb = (sm(12 + 2 * i, 2) for i in range(4))
        ab = sm(20)
        RL = sm(32, 32).rearrange("p (t e) -> p t e", t=NT)
        cmpg = sm(64, 512).rearrange("p (t a b) -> p t a b", t=NT, a=NE)
        rank = sm(576, 32).rearrange("p (t e) -> p t e", t=NT)
        mask = sm(608, 32).rearrange("p (t e) -> p t e", t=NT)
        rexp = sm(640, 32).rearrange("p (t e) -> p t e", t=NT)
        ce = sm(672, 32).rearrange("p (t e) -> p t e", t=NT)
        posm = sm(704, 32).rearrange("p (t e) -> p t e", t=NT)
        m1, s1, r1 = (sm(736 + 2 * i, 2) for i in range(3))
        gates = sm(744, 4)
        over = sm(848, 32).rearrange("p (t e) -> p t e", t=NT)
        attp = sm(64, 128).rearrange("p (l r b) -> p l r b", l=2, r=2)
        ce_over = sm(880, 32).rearrange("p (t e) -> p t e", t=NT)
        over_n = sm(912)
        flag = sb("flag", [1, 1], I32)
        pmx, pnm, psum_, pinv = (small[0:E2, 748 + i:749 + i] for i in range(4))
        prow = sb("prow", [E2, N])
        PT = sb("PT", [E2, N])
        prob = sm(768, 16).rearrange("p (t e) -> p t e", t=NT)
        npro = sm(784, 16).rearrange("p (t e) -> p t e", t=NT)
        sig = sm(800, 16).rearrange("p (t e) -> p t e", t=NT)
        tie = sm(816, 16).rearrange("p (t e) -> p t e", t=NT)
        sel = sm(832, 16).rearrange("p (t e) -> p t e", t=NT)

        SLOT = [(4, 5, 0), (1, 2, 3)]

        LATE = [((4, 5), (0, 1), (2, 3))[n % 3] for n in range(WC - EARLY)]

        def w1v():
            return ring[:, 4, 0:2048].rearrange("p (c n) -> p c n", c=HC)

        def w2v():
            return ring[:, 4, 2048:4096].rearrange("p (c n) -> p c n", c=HC)

        ld_const, ld_x, ld_edges, ld_emb, ld_ab, ld_rw, ld_att, ld_small, ld_root, ld_ffn = (
            sem(n) for n in ("ld_const", "ld_x", "ld_edges", "ld_emb", "ld_ab", "ld_rw", "ld_att", "ld_small",
                             "ld_root", "ld_ffn"))
        basis_loaded = [sem(f"basis_loaded{q}") for q in range(2)]
        gate_loaded = [sem(f"gate_loaded{q}") for q in range(2)]
        up_loaded = [sem(f"up_loaded{q}") for q in range(2)]
        down_loaded = [sem(f"down_loaded{q}") for q in range(2)]
        dve_chain = sem("dve_chain")
        zeros_set, iota_set = sem("zeros_set"), sem("iota_set")
        normed = sem("normed")
        var_ready, std_ready = sem("var_ready"), sem("std_ready")
        transposed = sem("transposed")
        hT_copied = sem("hT_copied")
        x12_done, x12_copied, logits_done, scaled_done, nmax_ready, exp_done = (
            sem(n) for n in ("x12_done", "x12_copied", "logits_done", "scaled_done", "nmax_ready", "exp_done"))
        rwT_done, rwT_copied = sem("rwT_done"), sem("rwT_copied")
        attw_ready = sem("attw_ready")
        onehot_ready, onehot_scaled, onehot_used = sem("onehot_ready"), sem("onehot_scaled"), sem("onehot_used")
        combined = [sem(f"combined{q}") for q in range(2)]
        wstaged = [sem(f"wstaged{q}") for q in range(2)]
        regrouped = [sem(f"regrouped{q}") for q in range(2)]
        wcopied = [sem(f"wcopied{q}") for q in range(2)]
        late_loaded = [sem(f"late_loaded{n}") for n in range(WC - EARLY)]
        late_combined, late_staged, late_regrouped, late_copied = (
            sem(n) for n in ("late_combined", "late_staged", "late_regrouped", "late_copied"))
        root_used = sem("root_used")
        ab_ready = sem("ab_ready")
        V_ready, VT_done, VT_copied = sem("V_ready"), sem("VT_done"), sem("VT_copied")
        count_ready, count_used, CT_copied = sem("count_ready"), sem("count_used"), sem("CT_copied")
        step_done, step_added = sem("step_done"), sem("step_added")
        router_done, rmax_ready, rexp_done, mask_ready, pos_done, routed = (
            sem(n) for n in ("router_done", "rmax_ready", "rexp_done", "mask_ready", "pos_done", "routed"))
        S_ready, gathered, gather_copied = (sem(n) for n in ("S_ready", "gathered", "gather_copied"))
        gate_done, up_done, silu_done, hid_ready, hidT_done, hidT_copied, down_done, y_copied, scattered = (
            sem(n) for n in ("gate_done", "up_done", "silu_done", "hid_ready", "hidT_done", "hidT_copied",
                             "down_done", "y_copied", "scattered"))
        glog_done, gate_sig, gx_ready, YT_done, YT_copied, rgcn_done, rgcn_added = (
            sem(n) for n in ("glog_done", "gate_sig", "gx_ready", "YT_done", "YT_copied", "rgcn_done", "rgcn_added"))
        plog_done, pnm_ready, pexp_done, prow_ready, pt_done, prob_copied, pb_done, tied, signed, sel_ready, selT_done, \
            selT_copied, f1_done, f1_biased, gelu_done, act1_ready, a1T_done, a1T_copied, f2_done, x_final = (
                sem(n) for n in ("plog_done", "pnm_ready", "pexp_done", "prow_ready", "pt_done", "prob_copied",
                                 "pb_done", "tied", "signed", "sel_ready", "selT_done", "selT_copied", "f1_done",
                                 "f1_biased", "gelu_done", "act1_ready", "a1T_done", "a1T_copied", "f2_done",
                                 "x_final"))
        over_counted, over_summed, over_flag = sem("over_counted"), sem("over_summed"), sem("over_flag")
        rest_loaded, rest_gate_up, rest_silu, rest_hid, rest_hidT, rest_hidT_copied, rest_down, rest_added = (
            sem(n) for n in ("rest_loaded", "rest_gate_up", "rest_silu", "rest_hid", "rest_hidT", "rest_hidT_copied",
                             "rest_down", "rest_added"))
        stored = sem("stored")

        block = ctx.enter_context(nc.Block())

        CPE = ECH // NE

        def step_bank(k, t):
            return bank[((6, 7), (5, 0))[k % 2][t]][:]

        BASIS_DMAS = BG

        @block.sync
        def _(sp):
            def basis_chunk(basis_d, c, slots, loaded):
                for g in range(BG):
                    rows = basis_d[8 * g:8 * g + BK[g] // 16, bass.ds(c * 64, 64), :]
                    sp.dma_start(ring[0:BK[g], slots[g // 2], g % 2 * 4 * H:(g % 2 + 1) * 4 * H],
                                 rows.rearrange("b (i j) o -> b i (j o)", j=4)).then_inc(loaded, 16)

            for k, e_d in enumerate((src_d, dst_d, type_d)):
                sp.dma_start(idx_i[:, k], e_d.rearrange("(p c) -> p c", p=P)).then_inc(ld_edges, 16)
            sp.dma_start(ew[:], ew_d.rearrange("(p c) -> p c", p=P)).then_inc(ld_edges, 16)
            sp.dma_start(const[:], const_d).then_inc(ld_const, 16)
            sp.dma_start(x[:], x_d.rearrange("(t p) n -> p t n", p=P)).then_inc(ld_x, 16)
            for k, e_d in enumerate((emb1_d, emb2_d)):
                sp.dma_start(emb[:, k], e_d.rearrange("(c p) d -> p c d", p=P)).then_inc(ld_emb, 16)
            for q in range(2):
                basis_chunk(basis1_d, q, (2 * q, 2 * q + 1), basis_loaded[q])
            with sp.Fori(1, WC // 2) as i:
                for q in range(2):
                    sp.wait_ge(combined[q], i)
                    basis_chunk(basis1_d, 2 * i + q, (2 * q, 2 * q + 1), basis_loaded[q])

            def expert_weights(e, q):
                g, u, d = SLOT[q]
                sp.dma_start(ring[:, g, :].rearrange("p (c f) -> p c f", c=HC),
                             gate_d[bass.ds(e, 1)].rearrange("e (c p) f -> p (e c) f", p=P)).then_inc(gate_loaded[q], 16)
                sp.dma_start(ring[:, u, :].rearrange("p (c f) -> p c f", c=HC),
                             up_d[bass.ds(e, 1)].rearrange("e (c p) f -> p (e c) f", p=P)).then_inc(up_loaded[q], 16)

            def expert_down(e, q):
                sp.dma_start(ring[:, SLOT[q][2], :].rearrange("p (c n) -> p c n", c=FF // P),
                             down_d[bass.ds(e, 1)].rearrange("e (c p) n -> p (e c) n", p=P)).then_inc(down_loaded[q], 16)

            expert_weights(0, 0)
            for i in range(EARLY // 2):
                for q in range(2):
                    sp.wait_ge(combined[q], WC // 2 + i)
                    basis_chunk(basis2_d, 2 * i + q, (2 * q, 2 * q + 1), basis_loaded[q])
            sp.wait_ge(combined[0], (WC + EARLY) // 2)
            expert_down(0, 0)
            sp.wait_ge(combined[1], (WC + EARLY) // 2)
            expert_weights(1, 1)
            expert_down(1, 1)
            with sp.Fori(1, NE // 2) as i:
                for q in range(2):
                    sp.wait_ge(up_done, 2 * i + q - 1)
                    expert_weights(2 * i + q, q)
                    sp.wait_ge(down_done, 2 * i + q - 1)
                    expert_down(2 * i + q, q)
            sp.dma_start(root[:], root1_d.rearrange("(c p) n -> p c n", p=P)).then_inc(ld_root, 16)
            for l, b_d in enumerate((bias1_d, bias2_d)):
                sp.dma_start(bias[l][:], b_d.unsqueeze(0).broadcast_to([P, H])).then_inc(ld_small, 16)
            sp.dma_start(wr[:], wr_d.rearrange("(c p) e -> p c e", p=P)).then_inc(ld_small, 16)
            sp.dma_start(b1[:], b1_d.rearrange("e f -> (e f)").unsqueeze(0).broadcast_to([P, E2 * F2])).then_inc(ld_small, 16)
            sp.dma_start(b2[:], b2_d).then_inc(ld_small, 16)
            sp.wait_ge(up_done, NE - 1)
            basis_chunk(basis2_d, EARLY, LATE[0], late_loaded[0])
            sp.wait_ge(scattered, NE)
            sp.wait_ge(over_flag, 1)
            with sp.If(sp.value_load(flag[:], min_val=0, max_val=NT * P * NE) > 0):
                with sp.Fori(0, NE) as e:
                    sp.wait_ge(rest_added, e * NT + 1)
                    for k, (w_d, n) in enumerate(((gate_d, HC), (up_d, HC), (down_d, FF // P))):
                        sp.dma_start(ring[:, k, :].rearrange("p (c f) -> p c f", c=n),
                                     w_d[bass.ds(e, 1)].rearrange("e (c p) f -> p (e c) f", p=P)).then_inc(rest_loaded, 16)
            for n in range(1, WC - EARLY):
                if n == 3:
                    sp.wait_ge(root_used, 1)
                    sp.dma_start(root[:], root2_d.rearrange("(c p) n -> p c n", p=P)).then_inc(ld_root, 16)
                wait(sp, late_combined, n - 2)
                basis_chunk(basis2_d, EARLY + n, LATE[n], late_loaded[n])
            sp.wait_ge(late_combined, 4)
            sp.dma_start(w2v(), w2_d.rearrange("e f n -> (e f) n").rearrange("(c p) n -> p c n", p=P)).then_inc(ld_ffn, 16)
            for c in range(HC):
                sp.dma_start(w1v()[:, c].rearrange("p (e f) -> p e f", e=E2),
                             w1_d[:, c * P:(c + 1) * P, :].rearrange("e p f -> p e f")).then_inc(ld_ffn, 16)
            sp.wait_ge(x_final, 1)
            sp.dma_start(out_d.rearrange("(t p) n -> p t n", p=P), x[:]).then_inc(stored, 16)
            sp.wait_ge(stored, 16)

        @block.gpsimd
        def _(pool):
            pool.memset(zero_b[:], 0.0).then_inc(zeros_set, 1)

        @block.scalar
        def _(act):
            for l, a_d in enumerate((att1_d, att2_d)):
                act.dma_start(attb[l][:], a_d.unsqueeze(0).broadcast_to([P, 2, NB])).then_inc(ld_att, 16)
            act.dma_start(alpha, alpha_d.unsqueeze(0).broadcast_to([P, 1])).then_inc(ld_ab, 16)
            act.dma_start(beta, beta_d.unsqueeze(0).broadcast_to([P, 1])).then_inc(ld_ab, 16)
            act.dma_start(rw_sb[0:NE], rw_d).then_inc(ld_rw, 16)
            for l, g_d in enumerate((gw1_d, gw2_d)):
                act.dma_start(rw_sb[NE + 2 * l:NE + 2 * l + 2], g_d.rearrange("r n a -> r (n a)")).then_inc(ld_rw, 16)
            def ln_sqrt(n):
                for t in range(NT):
                    act.wait_ge(var_ready, NT * (n - 1) + t + 1)
                    act.activation(rstd[:, t:t + 1], rstd[:, t:t + 1], ACT.Sqrt).then_inc(std_ready, 1)

            def scale_onehots(ch, k):
                act.wait_ge(onehot_ready, ch + 1)
                for m in (1, 2):
                    ins = act.mul(onehot[:, k, 2 + m], onehot[:, k, 1], edge[:, 4 + m, bass.ds(ch, 1)])
                ins.then_inc(onehot_scaled, 1)

            def stage(q, n):
                act.wait_ge(combined[q], n + 1)
                act.copy(wstage[:, q], bank[3 + q][:]).then_inc(wstaged[q], 1)

            def keep(q, n):
                act.wait_ge(regrouped[q], n + 1)
                act.copy(wcomb[:, bass.ds(n * 2 + q, 1), :].rearrange("p a n -> p (a n)"),
                         bank[3 + q][:]).then_inc(wcopied[q], 1)

            def weights_and_edges(i):
                for q in range(2):
                    for k in range(EPC):
                        scale_onehots(EFIRST + (2 * i - 2 + q) * EPC + k, k % NOH)
                    stage(q, i)
                    keep(1 - q, i - 1 + q)

            for k in range(NOH):
                scale_onehots(k, k)
            ln_sqrt(1)
            for k in range(NOH):
                scale_onehots(NOH + k, k)
            act.wait_ge(logits_done, 1)
            act.mul(lrelu, bank[5][:].rearrange("p (t s) -> p t s", t=NT), 0.2).then_inc(scaled_done, 1)
            for k in range(NOH):
                scale_onehots(2 * NOH + k, k)
            act.wait_ge(nmax_ready, 1)
            for t in range(NT):
                act.activation(sim_e[:, t], lrelu[:, t], ACT.Exp, bias=nmax[:, t:t + 1],
                               accum_out=rsum[:, t:t + 1]).then_inc(exp_done, 1)
            act.wait_ge(ld_ab, 32)
            act.activation(small[:, 0:2], small[:, 0:2], ACT.Exp).then_inc(ab_ready, 1)
            stage(0, 0)
            for k in range(3 * NOH, EFIRST):
                scale_onehots(k, k % NOH)
            stage(1, 0)
            keep(0, 0)
            with act.Fori(1, EPAIRS) as i:
                weights_and_edges(i)
            stage(0, EPAIRS)
            keep(1, EPAIRS - 1)
            keep(0, EPAIRS)
            stage(1, EPAIRS)
            keep(1, EPAIRS)
            ln_sqrt(2)
            stage(0, WC // 2)
            keep(0, WC // 2)
            act.wait_ge(rmax_ready, 1)
            for t in range(NT):
                act.activation(rexp[:, t], RL[:, t], ACT.Exp, bias=m1[:, t:t + 1]).then_inc(rexp_done, 1)
            stage(1, WC // 2)
            keep(1, WC // 2)

            def copy_gathered(e, q):
                act.wait_ge(gathered, e + 1)
                act.copy(area[:, 512 * q:512 * q + 512], bank[5][:]).then_inc(gather_copied, 1)

            def expert(e, q, last=False):
                act.wait_ge(gate_done, e + 1)
                wait(act, hid_ready, e)
                act.activation(sg, bank[2][:], ACT.Silu).then_inc(silu_done, 1)
                if not last:
                    copy_gathered(e + 1, 1 - q)
                act.wait_ge(hidT_done, e + 1)
                act.copy(hidT[q], bank[2][:]).then_inc(hidT_copied, 1)
                act.wait_ge(down_done, e + 1)
                act.copy(y[q], bank[4][:]).then_inc(y_copied, 1)

            copy_gathered(0, 0)
            expert(0, 0)
            expert(1, 1)
            with act.Fori(1, NE // 2 - 1) as i:
                for q in range(2):
                    expert(2 * i + q, q)
            expert(NE - 2, 0)
            expert(NE - 1, 1, last=True)
            act.wait_ge(count_used, ECH)
            for t in range(NT):
                act.copy(CT[:, :, t], bank[6 + t][:].rearrange("p (r s) -> p r s", r=2)).then_inc(CT_copied, 1)

            act.wait_ge(scattered, NE)
            act.wait_ge(over_flag, 1)
            with act.If(act.value_load(flag[:], min_val=0, max_val=NT * P * NE) > 0):
                with act.Fori(0, NE) as e:
                    for k in range(2 * NT):
                        act.wait_ge(rest_gate_up, e * 2 * NT + k + 1)
                        act.activation(sg, bank[2][:], ACT.Silu).then_inc(rest_silu, 1)

            def late_copies(n):
                act.wait_ge(late_combined, n + 1)
                act.copy(wstage[:, 0], bank[4][:]).then_inc(late_staged, 1)
                act.wait_ge(late_regrouped, n + 1)
                act.copy(wcomb[:, WC + EARLY + n], bank[4][:]).then_inc(late_copied, 1)

            ln_sqrt(3)
            for l in range(2):
                act.wait_ge(glog_done, l + 1)
                act.activation(gates, bank[7][:, 0:4], ACT.Sigmoid).then_inc(gate_sig, 1)
                act.wait_ge(gate_sig, l + 1)
                for t in range(NT):
                    act.mul(gx[:, 1, t], h[:, t], gates[:, 2 * t + 1:2 * t + 2]).then_inc(gx_ready, 1)
                late_copies(3 * l)
                for k in (1, 3):
                    act.wait_ge(YT_done, 4 * l + k + 1)
                    act.copy(YT[:, 2 * k:2 * k + 2], bank[k][:].rearrange("p (c n) -> p c n", c=2)).then_inc(YT_copied, 1)
                late_copies(3 * l + 1)
                late_copies(3 * l + 2)
            ln_sqrt(4)
            act.wait_ge(pnm_ready, 1)
            act.activation(prow[:], bank[7][0:E2, 0:N], ACT.Exp, bias=pnm, accum_out=psum_).then_inc(pexp_done, 1)
            act.wait_ge(prob_copied, 1)
            act.wait_ge(pb_done, 1)
            for k, half in enumerate((range(E2 // 2, E2), range(E2 // 2))):
                wait(act, tied, k)
                for e in half:
                    for t in range(NT):
                        ins = act.activation(sgn[:, t, e], bank[e // 2][:, (e % 2) * N:(e % 2) * N + N], ACT.Sign,
                                             bias=npro[:, t, e:e + 1], accum_out=sig[:, t, e:e + 1])
                ins.then_inc(signed, 1)
            for t in range(NT):
                act.wait_ge(f1_biased, t + 1)
                act.activation(act1[:, t], act1[:, t], ACT.Gelu).then_inc(gelu_done, 1)

        @block.vector
        def _(dve):
            chain = Chain(dve, dve_chain)
            link = chain.link

            def layer_norm(n, finish_x=None):
                for t in range(NT):
                    if finish_x:
                        finish_x(t)
                    link(dve.bn_stats(stat[:, t], x[:, t]))
                    link(dve.bn_aggr(mv[:, t], stat[:, t]))
                    dve.tensor_scalar(rstd[:, t:t + 1], mv[:, t, 1:2], EPS, None, ALU.add).then_inc(var_ready, 1)
                    dve.wait_ge(std_ready, NT * (n - 1) + t + 1)
                    link(dve.reciprocal(rstd[:, t:t + 1], rstd[:, t:t + 1]))
                    dve.tensor_scalar(h[:, t], x[:, t], mv[:, t, 0:1], rstd[:, t:t + 1], ALU.subtract,
                                      ALU.mult).then_inc(normed, 1)

            def copy_hT(n):
                for t in range(NT):
                    dve.wait_ge(transposed, NT * (n - 1) + t + 1)
                    dve.tensor_copy(hT[:, :, t * P:(t + 1) * P],
                                    bank[5 + t][:].rearrange("p (c n) -> p c n", c=HC)).then_inc(hT_copied, 1)

            dve.wait_ge(ld_edges, 64)
            link(dve.tensor_copy(edge[:, 0:3], idx_i[:]))
            link(dve.tensor_scalar(edge[:, 3], edge[:, 2], 0.0, None, ALU.is_equal))
            link(dve.tensor_scalar(edge[:, 2], edge[:, 3], -1.0, 1.0, ALU.mult, ALU.add))
            link(dve.tensor_copy(wpart[:, 0], ew[:]))
            link(dve.tensor_tensor(ew[:], ew[:], wpart[:, 0], ALU.subtract))
            link(dve.tensor_copy(wpart[:, 1], ew[:]))
            link(dve.tensor_tensor(ew[:], ew[:], wpart[:, 1], ALU.subtract))
            link(dve.tensor_copy(wpart[:, 2], ew[:]))
            link(dve.tensor_copy(edge[:, 4:7], wpart[:]))
            dve.wait_ge(ld_const, 16)
            link(dve.tensor_copy(iota_b[:], cst("iota")))

            def edge_onehots(i, first=False):
                for k in range(NOH):
                    ch = i * NOH + k
                    col = [edge[:, m, bass.ds(ch, 1)] for m in range(5)]
                    if not first:
                        dve.wait_ge(onehot_used, ch - (NOH - 1))
                    dve.tensor_scalar(onehot[:, k, 1], iota_b[:], col[1], None, ALU.is_equal)
                    dve.tensor_scalar(onehot[:, k, 0], iota_b[:], col[0], None, ALU.is_equal)
                    dve.tensor_scalar(onehot[:, k, 2], iota_b[:], col[1], col[4], ALU.is_equal,
                                      ALU.mult).then_inc(onehot_ready, 1)

            edge_onehots(0, first=True)
            dve.wait_ge(ld_x, 16)
            layer_norm(1)
            dve.wait_ge(ld_att, 32)
            for l in range(2):
                for g in range(BG):
                    nb = BK[g] // 16
                    link(dve.tensor_tensor(attp[:, l, :, 0:nb], attb[l][:, :, 8 * g:8 * g + nb],
                                           cst("block16")[:, 0:nb].unsqueeze(1).broadcast_to([P, 2, nb]), ALU.mult))
                    link(dve.tensor_reduce(atts[:, l, g], attp[:, l, :, 0:nb], AX.X, ALU.add))
                dve.tensor_tensor(attw[l][:], cst("diag16").unsqueeze(1).unsqueeze(1).broadcast_to([P, BG, 2, 16]),
                                  atts[:, l].unsqueeze(3).broadcast_to([P, BG, 2, 16]), ALU.mult).then_inc(attw_ready, 1)
            copy_hT(1)
            edge_onehots(1)
            dve.wait_ge(x12_done, 1)
            dve.tensor_copy(x12T, bank[7][:]).then_inc(x12_copied, 1)
            dve.wait_ge(rwT_done, 1)
            dve.tensor_copy(rwT[:], bank[6][:, 0:HC * NR].rearrange("p (c e) -> p c e", c=HC)).then_inc(rwT_copied, 1)
            edge_onehots(2)
            dve.wait_ge(scaled_done, 1)
            link(dve.tensor_tensor(lrelu, lrelu, bank[5][:].rearrange("p (t s) -> p t s", t=NT), ALU.max))
            link(dve.tensor_reduce(rmax, lrelu, AX.X, ALU.max))
            dve.tensor_scalar(nmax, rmax, -1.0, None, ALU.mult).then_inc(nmax_ready, 1)
            with dve.Fori(3, ECH // NOH) as i:
                edge_onehots(i)

            dve.wait_ge(exp_done, NT)
            dve.wait_ge(onehot_used, ECH)
            link(dve.reciprocal(rinv, rsum))
            A = bank[0][:].rearrange("p (t s) -> p t s", t=NT)
            for t in range(NT):
                link(dve.scalar_tensor_tensor(V[:, t], sim_e[:, t], rinv[:, t:t + 1], A[:, t], ALU.mult, ALU.mult,
                                              accum_out=norm[:, t:t + 1]))
            for t in range(NT):
                d = V[:, t, t * P:(t + 1) * P]
                dve.tensor_tensor(d, d, ident, ALU.add).then_inc(V_ready, 1)
            dve.wait_ge(ab_ready, 1)
            link(dve.tensor_tensor(ab, alpha, beta, ALU.add))
            link(dve.tensor_scalar(den, norm, alpha, ab, ALU.mult, ALU.add))
            link(dve.reciprocal(rden, den))
            link(dve.tensor_scalar(ra, rden, alpha, None, ALU.mult))
            link(dve.tensor_scalar(rb, rden, beta, None, ALU.mult))
            for t in range(NT):
                link(dve.tensor_scalar(inb[:, t], h[:, t], rb[:, t:t + 1], None, ALU.mult))
            dve.wait_ge(VT_done, 1)
            dve.tensor_copy(VT, bank[5][:].rearrange("p (t s) -> p t s", t=NT)).then_inc(VT_copied, 1)
            for k in range(ITERS):
                for t in range(NT):
                    dve.wait_ge(step_done, NT * k + t + 1)
                    dve.scalar_tensor_tensor(out5[:, k % 2, t], step_bank(k, t), ra[:, t:t + 1], inb[:, t],
                                             ALU.mult, ALU.add).then_inc(step_added, 1)
            dve.wait_ge(step_added, NT * ITERS)

            layer_norm(2, lambda t: link(dve.tensor_tensor(x[:, t], x[:, t], out5[:, (ITERS - 1) % 2, t], ALU.add)))
            copy_hT(2)
            dve.wait_ge(router_done, 1)
            link(dve.tensor_copy(RL, bank[7][:, 0:NT * NE].rearrange("p (t e) -> p t e", t=NT)))
            link(dve.tensor_reduce(m1, RL, AX.X, ALU.max))
            dve.tensor_scalar(m1, m1, -1.0, None, ALU.mult).then_inc(rmax_ready, 1)
            eq = lrelu.rearrange("p t (a b) -> p t a b", a=NE)
            for t in range(NT):
                other = RL[:, t].unsqueeze(1).broadcast_to([P, NE, NE])
                own = RL[:, t].unsqueeze(2).broadcast_to([P, NE, NE])
                link(dve.tensor_tensor(cmpg[:, t], other, own, ALU.is_gt))
                link(dve.tensor_tensor(eq[:, t], other, own, ALU.is_equal))
                link(dve.tensor_tensor(eq[:, t], eq[:, t],
                                       cst("earlier_expert").rearrange("p (a b) -> p a b", a=NE), ALU.mult))
            link(dve.tensor_tensor(cmpg, cmpg, eq, ALU.add))
            link(dve.tensor_reduce(rank, cmpg, AX.X, ALU.add))
            dve.tensor_scalar(mask, rank, 1.5, None, ALU.is_lt).then_inc(mask_ready, 1)
            dve.wait_ge(mask_ready, 1)
            dve.wait_ge(rexp_done, NT)
            link(dve.tensor_tensor(rexp, rexp, mask, ALU.mult))
            link(dve.tensor_reduce(s1, rexp, AX.X, ALU.add))
            link(dve.reciprocal(r1, s1))
            for t in range(NT):
                link(dve.tensor_scalar(ce[:, t], rexp[:, t], r1[:, t:t + 1], None, ALU.mult))
            dve.wait_ge(pos_done, 1)
            pos = bank[7][:, 64:64 + NT * NE].rearrange("p (t e) -> p t e", t=NT)
            link(dve.scalar_tensor_tensor(posm, pos, 1.0, mask, ALU.add, ALU.mult))
            link(dve.tensor_scalar(posm, posm, -1.0, None, ALU.add))
            link(dve.tensor_scalar(over, posm, LIMIT - 0.5, None, ALU.is_ge))
            link(dve.tensor_tensor(ce_over, ce, over, ALU.mult))
            dve.tensor_reduce(over_n, over, AX.XY, ALU.add).then_inc(over_counted, 1)
            dve.wait_ge(over_summed, 1)
            dve.tensor_copy(flag[:], bank[7][0:1, 128:129]).then_inc(over_flag, 1)

            slots = cst("slots")

            def select(e, q):
                for t in range(NT):
                    dve.tensor_scalar(S[q][:, t], slots[:, 0:CAP], posm[:, t, bass.ds(e, 1)], None,
                                      ALU.is_equal).then_inc(S_ready, 1)
                    dve.tensor_scalar(SW[q][:, t], slots, posm[:, t, bass.ds(e, 1)], ce[:, t, bass.ds(e, 1)],
                                      ALU.is_equal, ALU.mult).then_inc(S_ready, 1)

            def count_onehots(ch, k):
                col = [edge[:, m, bass.ds(ch, 1)] for m in range(4)]
                wait(dve, count_used, ch - 1)
                dve.tensor_scalar(count_onehot[:, k, 0], iota_b[:], col[1], None, ALU.is_equal)
                dve.tensor_scalar(count_onehot[:, k, 1], iota_b[:], col[0], col[3], ALU.is_equal, ALU.mult)
                dve.tensor_scalar(count_onehot[:, k, 2], iota_b[:], col[0], col[2], ALU.is_equal,
                                  ALU.mult).then_inc(count_ready, 1)

            def expert(e, q, last=False):
                for k in range(2):
                    count_onehots(e * CPE + k, k)
                if not last:
                    select(e + 1, 1 - q)
                dve.wait_ge(silu_done, e + 1)
                dve.wait_ge(up_done, e + 1)
                dve.tensor_tensor(hid[q], sg, bank[3][:], ALU.mult).then_inc(hid_ready, 1)
                for k in range(2, CPE):
                    count_onehots(e * CPE + k, k % 2)

            select(0, 0)
            expert(0, 0)
            expert(1, 1)
            with dve.Fori(1, NE // 2 - 1) as i:
                for q in range(2):
                    expert(2 * i + q, q)
            expert(NE - 2, 0)
            expert(NE - 1, 1, last=True)
            dve.wait_ge(scattered, NE)
            for t in range(NT):
                link(dve.tensor_tensor(x[:, t], x[:, t], bank[t][:], ALU.add))

            with dve.If(dve.value_load(flag[:], min_val=0, max_val=NT * P * NE) > 0):
                dve.tensor_copy(small[:, 1022:1023], over_n).then_inc(rest_added, 1)
                with dve.Fori(0, NE) as e:
                    for t in range(NT):
                        for f in range(2):
                            k = 2 * t + f
                            dve.wait_ge(rest_silu, e * 2 * NT + k + 1)
                            dve.tensor_tensor(hid[0], sg, bank[3][:], ALU.mult).then_inc(rest_hid, 1)
                            dve.wait_ge(rest_hidT, e * 2 * NT + k + 1)
                            dve.tensor_copy(hidT[0], bank[2][:]).then_inc(rest_hidT_copied, 1)
                        dve.wait_ge(rest_down, e * NT + t + 1)
                        dve.scalar_tensor_tensor(x[:, t], bank[4][:], ce_over[:, t, bass.ds(e, 1)], x[:, t],
                                                 ALU.mult, ALU.add).then_inc(rest_added, 1)
                dve.wait_ge(rest_added, NE * NT + 1)

            layer_norm(3)
            dve.wait_ge(ld_small, 16 * 5)
            for l in range(2):
                copy_hT(3 + l)
                dve.wait_ge(gate_sig, l + 1)
                for t in range(NT):
                    dve.tensor_scalar(gx[:, 0, t], h[:, t], gates[:, 2 * t:2 * t + 1], None,
                                      ALU.mult).then_inc(gx_ready, 1)
                for k in (0, 2):
                    dve.wait_ge(YT_done, 4 * l + k + 1)
                    dve.tensor_copy(YT[:, 2 * k:2 * k + 2],
                                    bank[k][:].rearrange("p (c n) -> p c n", c=2)).then_inc(YT_copied, 1)
                if l == 1:
                    for t in range(NT):
                        link(dve.tensor_tensor(x[:, t], x[:, t], bias[l][:], ALU.add))
                else:
                    for t in range(NT):
                        dve.wait_ge(rgcn_done, NT * l + t + 1)
                        dve.wait_ge(gx_ready, 4)
                        link(dve.tensor_tensor(h[:, t], bank[5 + t][:], bias[l][:], ALU.add))
                        dve.tensor_scalar(h[:, t], h[:, t], 0.0, None, ALU.max).then_inc(normed, 1)

            def second_layer(t):
                dve.wait_ge(rgcn_done, NT + t + 1)
                link(dve.tensor_tensor(x[:, t], x[:, t], bank[5 + t][:], ALU.add))

            layer_norm(4, second_layer)
            copy_hT(5)
            dve.wait_ge(plog_done, 1)
            link(dve.tensor_reduce(pmx, bank[7][0:E2, 0:N], AX.X, ALU.max))
            dve.tensor_scalar(pnm, pmx, -1.0, None, ALU.mult).then_inc(pnm_ready, 1)
            dve.wait_ge(pexp_done, 1)
            link(dve.reciprocal(pinv, psum_))
            dve.tensor_scalar(prow[:], prow[:], pinv, None, ALU.mult).then_inc(prow_ready, 1)

            def bias_f1(t):
                dve.wait_ge(f1_done, t + 1)
                dve.tensor_tensor(act1[:, t], bank[5 + t][:], b1[:], ALU.add).then_inc(f1_biased, 1)

            dve.wait_ge(pt_done, 1)
            link(dve.tensor_copy(prob, bank[7][:, 256:256 + NT * E2].rearrange("p (t e) -> p t e", t=NT)))
            dve.tensor_scalar(npro, prob, -1.0, None, ALU.mult).then_inc(prob_copied, 1)
            bias_f1(0)
            dve.wait_ge(pb_done, 1)
            order = cst("tie_order").rearrange("p (t s) -> p t s", t=NT)
            for k, half in enumerate((range(E2 // 2), range(E2 // 2, E2))):
                wait(dve, signed, k)
                for e in half:
                    for t in range(NT):
                        ins = dve.scalar_tensor_tensor(cmp[:, t, e], bank[e // 2][:, (e % 2) * N:(e % 2) * N + N],
                                                       prob[:, t, e:e + 1], order[:, t], ALU.is_equal, ALU.mult,
                                                       accum_out=tie[:, t, e:e + 1])
                ins.then_inc(tied, 1)
                if k == 0:
                    bias_f1(1)
            dve.wait_ge(tied, 2)
            dve.wait_ge(signed, 2)
            link(dve.scalar_tensor_tensor(tie, sig, 0.5, tie, ALU.mult, ALU.add))
            link(dve.tensor_scalar(tie, tie, float(C2 - N // 2) - 0.25, None, ALU.is_lt))
            dve.tensor_tensor(sel, tie, prob, ALU.mult).then_inc(sel_ready, 1)
            dve.wait_ge(sel_ready, 1)
            for t in range(NT):
                dve.wait_ge(gelu_done, t + 1)
                a = act1[:, t].rearrange("p (e f) -> p e f", e=E2)
                dve.tensor_tensor(a, a, sel[:, t].unsqueeze(2).broadcast_to([P, E2, F2]),
                                  ALU.mult).then_inc(act1_ready, 1)
            dve.wait_ge(selT_done, 1)
            dve.tensor_copy(PT[:], bank[7][0:E2, 0:N]).then_inc(selT_copied, 1)
            for t in range(NT):
                dve.wait_ge(a1T_done, t + 1)
                dve.tensor_copy(act1T[:, :, t * P:(t + 1) * P],
                                bank[5 + t][:].rearrange("p (c n) -> p c n", c=HC)).then_inc(a1T_copied, 1)
            for t in range(NT):
                dve.wait_ge(f2_done, t + 1)
                link(dve.tensor_tensor(x[:, t], x[:, t], bank[t][:], ALU.add))
            dve.tensor_copy(small[:, 0:1], small[:, 1:2]).then_inc(x_final, 1)

        @block.tensor
        def _(pe):
            def mm(out, lhsT, rhs, start, stop):
                return pe.matmul(out, lhsT, rhs, start=start, stop=stop, skip_group_check=True)

            def transpose_h(n):
                for t in range(NT):
                    pe.wait_ge(normed, NT * (n - 1) + t + 1)
                    for c in range(HC):
                        ins = pe.transpose(bank[5 + t][:, c * P:(c + 1) * P], h[:, t, c * P:(c + 1) * P], ident)
                    ins.then_inc(transposed, 1)

            def edges(ch, k):
                pe.wait_ge(onehot_ready, ch + 1)
                pe.wait_ge(onehot_scaled, ch + 1)
                for t in range(NT):
                    lhsT = onehot[:, k, 0, t * P:(t + 1) * P]
                    for m in range(3):
                        ins = mm(bank[0][:, t * N:(t + 1) * N], lhsT, onehot[:, k, 2 + m], False, False)
                ins.then_inc(onehot_used, 1)

            def combine(l, slots, acc):
                for g in range(BG):
                    for j in range(4):
                        ins = mm(acc[32 * j:32 * j + 32, :], attw[l][0:BK[g], g].rearrange("p r i -> p (r i)"),
                                 ring[0:BK[g], slots[g // 2], (g % 2 * 4 + j) * H:(g % 2 * 4 + j + 1) * H],
                                 g == 0, g == BG - 1)
                return ins

            def combine_early(l, q, n):
                pe.wait_ge(basis_loaded[q], (n + 1) * 16 * BASIS_DMAS)
                wait(pe, wcopied[q], n)
                combine(l, (2 * q, 2 * q + 1), bank[3 + q]).then_inc(combined[q], 1)

            def regroup(q, n):
                pe.wait_ge(wstaged[q], n + 1)
                mm(bank[3 + q][:], cst("regroup"), wstage[:, q], True, True).then_inc(regrouped[q], 1)

            def weights_and_edges(i):
                for q in range(2):
                    for k in range(EPC):
                        if k == EPC - NOH:
                            combine_early(0, q, i)
                            regroup(1 - q, i - 1 + q)
                        edges(EFIRST + (2 * i - 2 + q) * EPC + k, k % NOH)

            pe.wait_ge(zeros_set, 1)
            mm(bank[0][:], zero_b[:, 0:P], zero_b[:], True, False)
            for k in range(NOH):
                edges(k, k)

            transpose_h(1)
            pe.wait_ge(hT_copied, NT)
            pe.wait_ge(ld_emb, 32)
            for k in range(2):
                for c in range(HC):
                    ins = mm(bank[7][:, k * N:(k + 1) * N], emb[:, k, c], hT[:, c], c == 0, c == HC - 1)
            ins.then_inc(x12_done, 1)
            pe.wait_ge(ld_rw, 48)
            for c in range(HC):
                ins = pe.transpose(bank[6][:, c * NR:(c + 1) * NR], rw_sb[:, c * P:(c + 1) * P], ident[0:NR, 0:NR])
            ins.then_inc(rwT_done, 1)
            for k in range(NOH):
                edges(NOH + k, k)
            pe.wait_ge(x12_copied, 1)
            for t in range(NT):
                ins = mm(bank[5][:, t * N:(t + 1) * N], x12T[:, t * P:(t + 1) * P], x12T[:, N:2 * N], True, True)
            ins.then_inc(logits_done, 1)

            pe.wait_ge(attw_ready, 2)
            combine_early(0, 0, 0)
            for k in range(2 * NOH, EFIRST):
                if k == EFIRST - NOH:
                    combine_early(0, 1, 0)
                    regroup(0, 0)
                edges(k, k % NOH)
            with pe.Fori(1, EPAIRS) as i:
                weights_and_edges(i)
            combine_early(0, 0, EPAIRS)
            regroup(1, EPAIRS - 1)

            pe.wait_ge(V_ready, NT)
            for s in range(NT):
                for t in range(NT):
                    ins = pe.transpose(bank[5][:, s * N + t * P:s * N + (t + 1) * P], V[:, t, s * P:(s + 1) * P], ident)
            ins.then_inc(VT_done, 1)
            regroup(0, EPAIRS)
            pe.wait_ge(VT_copied, 1)
            for k in range(ITERS):
                if k == 2:
                    combine_early(0, 1, EPAIRS)
                for s in range(NT):
                    wait(pe, step_added, NT * (k - 1) + s + 1)
                    for t in range(NT):
                        cur = h[:, s] if k == 0 else out5[:, (k - 1) % 2, s]
                        ins = mm(step_bank(k, t), VT[:, s, t * P:(t + 1) * P], cur, s == 0, s == NT - 1)
                        if s == NT - 1:
                            ins.then_inc(step_done, 1)

            regroup(1, WC // 2 - 1)
            combine_early(1, 0, WC // 2)
            transpose_h(2)
            pe.wait_ge(hT_copied, 2 * NT)
            pe.wait_ge(rwT_copied, 1)
            for t in range(NT):
                for c in range(HC):
                    ins = mm(bank[7][:, t * NE:(t + 1) * NE], hT[:, c, t * P:(t + 1) * P], rwT[:, c, 0:NE], c == 0, c == HC - 1)
            ins.then_inc(router_done, 1)
            regroup(0, WC // 2)
            combine_early(1, 1, WC // 2)
            pe.wait_ge(mask_ready, 1)
            mm(bank[7][:, 64:64 + NE], cst("before"), mask[:, 0], True, True)
            mm(bank[7][:, 64 + NE:64 + 2 * NE], cst("before"), mask[:, 1], True, False)
            mm(bank[7][:, 64 + NE:64 + 2 * NE], cst("ones"), mask[:, 0], False, True).then_inc(pos_done, 1)

            pe.wait_ge(over_counted, 1)
            mm(bank[7][0:1, 128:129], over_n, cst("ones")[:, 0:1], True, True).then_inc(over_summed, 1)

            pe.wait_ge(over_flag, 1)
            for b in (0, 1, 6, 7):
                mm(bank[b][:], zero_b[:, 0:P], zero_b[:], True, False)

            def gather(e, q):
                pe.wait_ge(S_ready, 4 * (e + 1))
                wait(pe, gather_copied, e)
                for c in range(HC):
                    for s in range(NT):
                        ins = mm(bank[5][:, c * CAP:(c + 1) * CAP], h[:, s, c * P:(c + 1) * P], S[q][:, s],
                                 s == 0, s == NT - 1)
                for t in range(NT):
                    ins = pe.transpose(bank[5][:, N + t * P:N + (t + 1) * P], SW[q][:, t], ident)
                ins.then_inc(gathered, 1)

            def count_edges(e, first, end):
                for k in range(first, end):
                    pe.wait_ge(count_ready, e * CPE + k + 1)
                    for t in range(NT):
                        ins = mm(bank[6 + t][:], count_onehot[:, k % 2, 0, t * P:(t + 1) * P],
                                 count_onehot[:, k % 2, 1:3].rearrange("p r n -> p (r n)"), False, False)
                    ins.then_inc(count_used, 1)

            def scatter(e, q):
                pe.wait_ge(y_copied, e + 1)
                for t in range(NT):
                    ins = mm(bank[t][:], ST[q][:, t * P:(t + 1) * P], y[q], False, False)
                ins.then_inc(scattered, 1)

            def expert(e, q, first=False, last=False):
                g, u, d = SLOT[q]
                pe.wait_ge(gate_loaded[q], 16 * (e // 2 + 1) if isinstance(e, int) else (e - q) * 8 + 16)
                pe.wait_ge(gather_copied, e + 1)
                for c in range(HC):
                    for f in range(2):
                        ins = mm(bank[2][64 * f:64 * f + 64, :], xg[q][:, c], ring[:, g, c * FF + f * 512:c * FF + f * 512 + 512],
                                 c == 0, c == HC - 1)
                ins.then_inc(gate_done, 1)
                pe.wait_ge(up_loaded[q], 16 * (e // 2 + 1) if isinstance(e, int) else (e - q) * 8 + 16)
                wait(pe, hid_ready, e)
                for c in range(HC):
                    for f in range(2):
                        ins = mm(bank[3][64 * f:64 * f + 64, :], xg[q][:, c], ring[:, u, c * FF + f * 512:c * FF + f * 512 + 512],
                                 c == 0, c == HC - 1)
                ins.then_inc(up_done, 1)
                if not first:
                    scatter(e - 1, 1 - q)
                if not last:
                    gather(e + 1, 1 - q)
                pe.wait_ge(hid_ready, e + 1)
                for c in range(HC):
                    ins = pe.transpose(bank[2][:, c * P:(c + 1) * P], hid[q][:, c * P:(c + 1) * P], ident)
                ins.then_inc(hidT_done, 1)
                count_edges(e, 0, 2)
                pe.wait_ge(down_loaded[q], 16 * (e // 2 + 1) if isinstance(e, int) else (e - q) * 8 + 16)
                pe.wait_ge(hidT_copied, e + 1)
                wait(pe, y_copied, e)
                for c in range(HC):
                    for f in range(2):
                        ins = mm(bank[4][64 * f:64 * f + 64, :], hidT[q][:, c * P + 64 * f:c * P + 64 * f + 64],
                                 ring[:, d, (f * HC + c) * H:(f * HC + c + 1) * H], c == 0, c == HC - 1)
                ins.then_inc(down_done, 1)
                count_edges(e, 2, CPE)

            regroup(1, WC // 2)
            gather(0, 0)
            for q in range(2):
                pe.wait_ge(wcopied[q], (WC + EARLY) // 2)
            expert(0, 0, first=True)
            expert(1, 1)
            with pe.Fori(1, NE // 2 - 1) as i:
                for q in range(2):
                    expert(2 * i + q, q)
            expert(NE - 2, 0)
            expert(NE - 1, 1, last=True)
            scatter(NE - 1, 1)

            pe.wait_ge(y_copied, NE)
            with pe.If(pe.value_load(flag[:], min_val=0, max_val=NT * P * NE) > 0):
                with pe.Fori(0, NE) as e:
                    pe.wait_ge(rest_loaded, e * 48 + 48)
                    for t in range(NT):
                        for f in range(2):
                            k = 2 * t + f
                            for w, b in ((0, 2), (1, 3)):
                                for c in range(HC):
                                    ins = mm(bank[b][:], hT[:, c, t * P:(t + 1) * P],
                                             ring[:, w, c * FF + f * 512:c * FF + f * 512 + 512], c == 0, c == HC - 1)
                            ins.then_inc(rest_gate_up, 1)
                            pe.wait_ge(rest_hid, e * 2 * NT + k + 1)
                            for c in range(HC):
                                ins = pe.transpose(bank[2][:, c * P:(c + 1) * P], hid[0][:, c * P:(c + 1) * P], ident)
                            ins.then_inc(rest_hidT, 1)
                            pe.wait_ge(rest_hidT_copied, e * 2 * NT + k + 1)
                            pe.wait_ge(rest_added, e * NT + t + 1)
                            for c in range(HC):
                                ins = mm(bank[4][:], hidT[0][:, c * P:(c + 1) * P],
                                         ring[:, 2, (f * HC + c) * H:(f * HC + c + 1) * H],
                                         f == 0 and c == 0, f == 1 and c == HC - 1)
                        ins.then_inc(rest_down, 1)

            def combine_late(n):
                pe.wait_ge(late_loaded[n], 16 * BASIS_DMAS)
                wait(pe, late_copied, n)
                combine(1, LATE[n], bank[4]).then_inc(late_combined, 1)

            def regroup_late(n):
                pe.wait_ge(late_staged, n + 1)
                mm(bank[4][:], cst("regroup"), wstage[:, 0], True, True).then_inc(late_regrouped, 1)

            pe.wait_ge(ld_small, 16 * 5)
            pe.wait_ge(CT_copied, NT)
            for l in range(2):
                transpose_h(3 + l)
                pe.wait_ge(hT_copied, (3 + l) * NT)
                for t in range(NT):
                    for c in range(HC):
                        ins = mm(bank[7][:, 2 * t:2 * t + 2], hT[:, c, t * P:(t + 1) * P], rwT[:, c, NE + 2 * l:NE + 2 * l + 2], c == 0, c == HC - 1)
                ins.then_inc(glog_done, 1)
                pe.wait_ge(ld_root, 16 * (l + 1))
                for t in range(NT):
                    for c in range(HC):
                        ins = mm(bank[5 + t][:], hT[:, c, t * P:(t + 1) * P], root[:, c], c == 0, False)
                ins.then_inc(root_used, 1)
                combine_late(3 * l)
                pe.wait_ge(gx_ready, 4 * (l + 1))
                wait(pe, YT_copied, 4 * l)
                for k in range(WC // 2):
                    for c in (2 * k, 2 * k + 1):
                        for s in range(NT):
                            for j in range(2):
                                for r in range(2):
                                    o = 32 * (2 * j + r)
                                    ins = mm(bank[k][o:o + 32, (c % 2) * N:(c % 2 + 1) * N],
                                             gx[:, r, s, c * 64 + 32 * j:c * 64 + 32 * j + 32], CT[:, r, s],
                                             s == 0, s == NT - 1)
                    ins.then_inc(YT_done, 1)
                    if k == 0:
                        regroup_late(3 * l)
                combine_late(3 * l + 1)
                pe.wait_ge(YT_copied, 4 * (l + 1))
                if l == 0:
                    for t in range(NT):
                        for c in range(WC):
                            ins = mm(bank[5 + t][:], YT[:, c, t * P:(t + 1) * P], wcomb[:, c], False, c == WC - 1)
                        ins.then_inc(rgcn_done, 1)
                        if t == 0:
                            regroup_late(1)
                    combine_late(2)
                    regroup_late(2)
                else:
                    def add(t, first, end):
                        for c in range(first, end):
                            ins = mm(bank[5 + t][:], YT[:, c, t * P:(t + 1) * P], wcomb[:, WC + c], False, c == WC - 1)
                        return ins

                    add(0, 0, WC - 4)
                    regroup_late(4)
                    add(1, 0, WC - 4)
                    combine_late(5)
                    pe.wait_ge(late_copied, WC - EARLY - 1)
                    add(0, WC - 4, WC - 1)
                    regroup_late(5)
                    add(1, WC - 4, WC - 1)
                    pe.wait_ge(late_copied, WC - EARLY)
                    for t in range(NT):
                        add(t, WC - 1, WC).then_inc(rgcn_done, 1)

            transpose_h(5)
            pe.wait_ge(hT_copied, 5 * NT)
            for c in range(HC):
                ins = mm(bank[7][0:E2, 0:N], wr[:, c], hT[:, c], c == 0, c == HC - 1)
            ins.then_inc(plog_done, 1)
            pe.wait_ge(ld_ffn, 16 * (1 + HC))

            def first_product(t):
                for c in range(HC):
                    ins = mm(bank[5 + t][:], hT[:, c, t * P:(t + 1) * P], w1v()[:, c], c == 0, c == HC - 1)
                ins.then_inc(f1_done, 1)

            first_product(0)
            pe.wait_ge(prow_ready, 1)
            for t in range(NT):
                ins = pe.transpose(bank[7][:, 256 + t * E2:256 + (t + 1) * E2], prow[:, t * P:(t + 1) * P], ident[0:E2, 0:E2])
            ins.then_inc(pt_done, 1)
            pe.wait_ge(prob_copied, 1)
            for e in range(E2):
                for t in range(NT):
                    ins = pe.transpose(bank[e // 2][:, (e % 2) * N + t * P:(e % 2) * N + (t + 1) * P],
                                       prob[:, t, e:e + 1].broadcast_to([P, P]), ident)
            ins.then_inc(pb_done, 1)
            first_product(1)
            pe.wait_ge(sel_ready, 1)
            for t in range(NT):
                ins = pe.transpose(bank[7][0:E2, t * P:(t + 1) * P], sel[:, t], ident)
            ins.then_inc(selT_done, 1)
            for t in range(NT):
                pe.wait_ge(act1_ready, t + 1)
                for c in range(HC):
                    ins = pe.transpose(bank[5 + t][:, c * P:(c + 1) * P], act1[:, t, c * P:(c + 1) * P], ident)
                ins.then_inc(a1T_done, 1)
            pe.wait_ge(selT_copied, 1)
            for t in range(NT):
                mm(bank[t][:], PT[:, t * P:(t + 1) * P], b2[:], True, False)
                pe.wait_ge(a1T_copied, t + 1)
                for c in range(HC):
                    ins = mm(bank[t][:], act1T[:, c, t * P:(t + 1) * P], w2v()[:, c], False, c == HC - 1)
                ins.then_inc(f2_done, 1)


_INS = ["x", "src", "dst", "edge_type_2", "edge_weight", "L0_gnn_emb_1", "L0_gnn_emb_2", "L0_gnn_alpha_p",
        "L0_gnn_beta_p", "L0_ffn_router_w", "L0_ffn_gate_w", "L0_ffn_up_w", "L0_ffn_down_w", "L1_gnn_basis1",
        "L1_gnn_att1", "L1_gnn_gate_w1", "L1_gnn_root1", "L1_gnn_bias1", "L1_gnn_basis2", "L1_gnn_att2",
        "L1_gnn_gate_w2", "L1_gnn_root2", "L1_gnn_bias2", "L1_ffn_Wr", "L1_ffn_W1", "L1_ffn_b1", "L1_ffn_W2",
        "L1_ffn_b2"]


def constants():
    import numpy as np
    c = np.zeros((P, NCONST), np.float32)

    def put(name, value):
        a, b = CONST[name]
        c[:, a:b] = value

    p = np.arange(P)
    put("ident", np.eye(P))
    put("before", p[:, None] < p[None, :])
    put("ones", 1.0)
    put("diag16", p[:, None] % 16 == np.arange(16)[None, :])
    put("block16", p[:, None] // 16 == np.arange(8)[None, :])
    j, r, i = p // 32, p // 16 % 2, p % 16
    i = 4 * i + j
    put("regroup", (64 * (i // 32) + 32 * r + i % 32)[:, None] == p[None, :])
    e = np.arange(NE)
    put("earlier_expert", (e[None, :] < e[:, None]).reshape(1, -1))
    t = np.arange(NT)[None, :, None] * P + p[:, None, None]
    put("tie_order", np.where(np.arange(N)[None, None, :] < t, 0.5, -0.5).reshape(P, -1))
    put("iota", np.arange(N))
    s = np.arange(2 * CAP) % CAP
    put("slots", np.where(s < LIMIT, s, -5))
    return c


def kernel(**inputs):
    import numpy as _np
    import concourse.bacc as _bacc
    from concourse import mybir as _mybir
    from concourse.bass_utils import run_bass_kernel_spmd as _run

    nc = _bacc.Bacc("TRN2", target_bir_lowering=False, num_devices=1)
    arrays, args = {}, []
    for name in _INS + ["shape_constants"]:
        a = constants() if name == "shape_constants" else _np.ascontiguousarray(inputs[name])
        arrays[f"in_{name}_dram"] = a
        args.append(nc.dram_tensor(f"in_{name}_dram", a.shape, _mybir.dt.from_np(a.dtype), kind="ExternalInput").ap())
    args.append(nc.dram_tensor("out_0_dram", (N, H), F32, kind="ExternalOutput").ap())
    build(nc, *args)
    r = _run(nc, [arrays], core_ids=[0])
    return r.results[0]["out_0_dram"]
```

```python
from contextlib import ExitStack

import concourse.bass as bass
from concourse import mybir

F32 = mybir.dt.float32
BF16 = mybir.dt.bfloat16
I32 = mybir.dt.int32
ALU = mybir.AluOpType
ACT = mybir.ActivationFunctionType
AX = mybir.AxisListType

P = 128
N = 256
NT = N // P
H = 512
HC = H // P
E_EDGES = 8192
ECH = E_EDGES // P
ITERS = 5
NE, FF = 16, 1024
CAP = 64
NB = 30
BK = [P, P, P, (NB - 24) * 16]
BG = len(BK)
WC = H // 64
EARLY = 2
LATE_END = WC - 2
EPAIRS = 3
EPC = 12
EFIRST = ECH - 2 * EPC * (EPAIRS - 1)
E2, F2, C2 = 8, 64, 128
EPS = 1e-5
CPE = ECH // NE
PACK = 2 * (2 * CPE * P)
ROUND = 1.5 * 2**23

CONST = {}
_at = 0
for _name, _n in (("iota", N), ("ident", P), ("before", P), ("ones", P), ("diag16", 16), ("block16", 8),
                  ("regroup", P),
                  ("earlier_expert", NE * NE), ("slots", 2 * CAP), ("tie_order", NT * N)):
    CONST[_name] = (_at, _at + _n)
    _at += _n
NCONST = _at
LIMIT = CAP


def wait(eng, sem, value):
    if not (isinstance(value, int) and value <= 0):
        eng.wait_ge(sem, value)


class Chain:

    def __init__(self, eng, sem, base=0):
        self.eng, self.sem, self.base, self.n = eng, sem, base, 0

    def link(self, ins):
        self.n += 1
        ins.then_inc(self.sem, 1)
        self.eng.wait_ge(self.sem, self.base + self.n)


def build(nc, x_d, src_d, dst_d, type_d, ew_d, emb1_d, emb2_d, alpha_d, beta_d, rw_d, gate_d, up_d, down_d,
          basis1_d, att1_d, gw1_d, root1_d, bias1_d, basis2_d, att2_d, gw2_d, root2_d, bias2_d,
          wr_d, w1_d, b1_d, w2_d, b2_d, const_d, out_d):
    with ExitStack() as ctx:
        def sb(name, shape, dt=F32):
            return ctx.enter_context(nc.sbuf_tensor(name, shape, dt))

        def sem(name):
            return ctx.enter_context(nc.semaphore(name))

        bank = [ctx.enter_context(nc.psum_tensor(f"bank{i}", [P, 512], F32)) for i in range(8)]

        ring = sb("ring", [P, 6, 4096])
        wcomb = sb("wcomb", [P, 2 * WC, H])
        const = sb("const", [P, NCONST])

        def cst(name):
            a, b = CONST[name]
            return const[:, a:b]

        ident = cst("ident")
        iota_b = sb("iota_b", [P, N], BF16)
        zero_b = sb("zero_b", [P, 512], BF16)
        x = sb("x", [P, NT, H])
        h = sb("h", [P, NT, H])
        hT = sb("hT", [P, HC, N])
        CT = sb("CT", [P, 2, NT, N])
        attw = [sb(f"attw{l}", [P, BG, 2, 16]) for l in range(2)]
        atts = sb("atts", [P, 2, BG, 2])
        wstage = sb("wstage", [P, 2, H])
        root = sb("root", [P, HC, H])
        attb = [sb(f"attb{l}", [P, 2, NB]) for l in range(2)]
        rwT = sb("rwT", [P, HC, NE])
        bias = [sb(f"bias{l}", [P, H]) for l in range(2)]
        stat = sb("stat", [P, NT, 6])
        mv = sb("mv", [P, NT, 2])
        rstd = sb("rstd", [P, NT])
        area = sb("area", [P, 4096 + 2048])
        small = sb("small", [P, 1024])

        NOH = 8
        onehot = area[:, 0:NOH * 5 * N // 2].bitcast(BF16).rearrange("p (q k n) -> p q k n", q=NOH, k=5)
        later = wcomb[:, WC + EARLY:, :].rearrange("p a n -> p (a n)")
        emb = later[:, 0:1024].rearrange("p (k c d) -> p k c d", k=2, c=HC)
        sim_e = later[:, 1024:1536].rearrange("p (t s) -> p t s", t=NT)
        lrelu = later[:, 1536:2048].rearrange("p (t s) -> p t s", t=NT)
        x12T = later[:, 2048:2560]
        gate_w = later[:, 0:2048].rearrange("p (l r n) -> p l r n", l=2, r=2)
        count_1, count_0 = later[:, 2048:2560], later[:, 2560:3072]
        V = area[:, 0:512].rearrange("p (t s) -> p t s", t=NT)
        VT = area[:, 512:1024].rearrange("p (t s) -> p t s", t=NT)
        inb = area[:, 1024:2048].rearrange("p (t n) -> p t n", t=NT)
        out5 = area[:, 3072:5120].rearrange("p (q t n) -> p q t n", q=2, t=NT)
        xg = [area[:, 512 * q:512 * q + 256].rearrange("p (c s) -> p c s", c=HC) for q in range(2)]
        ST = [area[:, 512 * q + 256:512 * q + 512] for q in range(2)]
        S = [area[:, 1024 + 128 * q:1152 + 128 * q].rearrange("p (t s) -> p t s", t=NT) for q in range(2)]
        SW = [area[:, 1280 + 256 * q:1536 + 256 * q].rearrange("p (t s) -> p t s", t=NT) for q in range(2)]
        sg = area[:, 1792:2304]
        hid = [area[:, 2304 + 512 * q:2816 + 512 * q] for q in range(2)]
        hidT = [area[:, 3328 + 512 * q:3840 + 512 * q] for q in range(2)]
        y = [area[:, 4352 + 512 * q:4864 + 512 * q] for q in range(2)]
        count_onehot = area[:, 5376:5888].bitcast(BF16).rearrange("p (q k n) -> p q k n", q=2, k=2)
        gx = area[:, 0:2048].rearrange("p (r t n) -> p r t n", r=2, t=NT)
        gate_products = area[:, 4096:6144].rearrange("p (t r n) -> p t r n", t=NT, r=2)
        YT = area[:, 2048:4096].rearrange("p (c n) -> p c n", c=WC)
        act1 = area[:, 0:1024].rearrange("p (t n) -> p t n", t=NT)
        act1T = area[:, 1024:2048].rearrange("p (c n) -> p c n", c=HC)
        cmp = area[:, 2048:4096].bitcast(BF16).rearrange("p (t e s) -> p t e s", t=NT, e=E2)

        rw_sb = area[0:NE, 5632:6144]
        idx_i = sb("idx_i", [P, 3, ECH], I32)
        ew = sb("ew", [P, ECH])
        edge = sb("edge", [P, 7, ECH])
        wpart = sb("wpart", [P, 3, ECH], BF16)
        wr = sb("wr", [P, HC, E2])
        b1 = sb("b1", [P, E2 * F2])
        b2 = sb("b2", [E2, H])

        def sm(a, n=1):
            return small[:, a:a + n]

        alpha, beta = sm(0), sm(1)
        rmax, nmax, rsum, rinv, norm = (sm(2 + 2 * i, 2) for i in range(5))
        den, rden, ra, rb = (sm(12 + 2 * i, 2) for i in range(4))
        ab = sm(20)
        RL = sm(32, 32).rearrange("p (t e) -> p t e", t=NT)
        cmpg = sm(64, 512).rearrange("p (t a b) -> p t a b", t=NT, a=NE)
        rank = sm(576, 32).rearrange("p (t e) -> p t e", t=NT)
        mask = sm(608, 32).rearrange("p (t e) -> p t e", t=NT)
        rexp = sm(640, 32).rearrange("p (t e) -> p t e", t=NT)
        ce = sm(672, 32).rearrange("p (t e) -> p t e", t=NT)
        posm = sm(704, 32).rearrange("p (t e) -> p t e", t=NT)
        m1, s1, r1 = (sm(736 + 2 * i, 2) for i in range(3))
        gates = sm(744, 4)
        gate_logits = sm(752, 4)
        over = sm(848, 32).rearrange("p (t e) -> p t e", t=NT)
        attp = sm(64, 128).rearrange("p (l r b) -> p l r b", l=2, r=2)
        ce_over = sm(880, 32).rearrange("p (t e) -> p t e", t=NT)
        over_n = sm(912)
        spare = sm(1020)
        flag = sb("flag", [1, 1], I32)
        pmx, pnm, psum_, pinv = (small[0:E2, 748 + i:749 + i] for i in range(4))
        prow = sb("prow", [E2, N])
        PT = sb("PT", [E2, N])
        prob = sm(768, 16).rearrange("p (t e) -> p t e", t=NT)
        rank2 = sm(784, 16).rearrange("p (t e) -> p t e", t=NT)
        sel = sm(832, 16).rearrange("p (t e) -> p t e", t=NT)

        SLOT = [(4, 5, 0), (1, 2, 3)]
        LATE = [(4, 5), (4, 5), (0, 1), (4, 5)]
        late_bank = [bank[4], bank[4], bank[4], bank[3]]
        pair_basis = ring[:, 0:4, :].rearrange("p a n -> p (a n)")

        PAIR_BASES = ((0, 12), (12, 16), (16, 22), (22, NB))

        def w1v():
            return ring[:, 2, 0:2048].rearrange("p (c n) -> p c n", c=HC)

        def w2v():
            return ring[:, 2, 2048:4096].rearrange("p (c n) -> p c n", c=HC)

        ld_const, ld_x, ld_edges, ld_emb, ld_ab, ld_rw, ld_att, ld_bias, ld_root, ld_ffn = (
            sem(n) for n in ("ld_const", "ld_x", "ld_edges", "ld_emb", "ld_ab", "ld_rw", "ld_att", "ld_bias",
                             "ld_root", "ld_ffn"))
        basis_loaded = [sem(f"basis_loaded{q}") for q in range(2)]
        gate_loaded = [sem(f"gate_loaded{q}") for q in range(2)]
        up_loaded = [sem(f"up_loaded{q}") for q in range(2)]
        down_loaded = [sem(f"down_loaded{q}") for q in range(2)]
        ld_iota, ld_gates = sem("ld_iota"), [sem(f"ld_gates{l}") for l in range(2)]
        dve_chain = sem("dve_chain")
        zeros_set = sem("zeros_set")
        normed = sem("normed")
        var_ready, std_ready = sem("var_ready"), sem("std_ready")
        transposed = sem("transposed")
        hT_copied = sem("hT_copied")
        x12_done, x12_copied, logits_done, scaled_done, nmax_ready, exp_done = (
            sem(n) for n in ("x12_done", "x12_copied", "logits_done", "scaled_done", "nmax_ready", "exp_done"))
        rwT_done, rwT_copied = sem("rwT_done"), sem("rwT_copied")
        attw_ready = sem("attw_ready")
        onehot_ready, onehot_scaled, onehot_used = sem("onehot_ready"), sem("onehot_scaled"), sem("onehot_used")
        combined = [sem(f"combined{q}") for q in range(2)]
        wstaged = [sem(f"wstaged{q}") for q in range(2)]
        regrouped = [sem(f"regrouped{q}") for q in range(2)]
        wcopied = [sem(f"wcopied{q}") for q in range(2)]
        late_loaded = [sem(f"late_loaded{n}") for n in range(LATE_END - EARLY)]
        pair_loaded = [sem(f"pair_loaded{g}") for g in range(BG)]
        pair_added = sem("pair_added")
        late_combined, late_staged, late_regrouped, late_copied = (
            sem(n) for n in ("late_combined", "late_staged", "late_regrouped", "late_copied"))
        root_used = sem("root_used")
        ab_ready = sem("ab_ready")
        V_ready, VT_done, VT_copied = sem("V_ready"), sem("VT_done"), sem("VT_copied")
        count_ready, count_used, unpacked, counted = (
            sem(n) for n in ("count_ready", "count_used", "unpacked", "counted"))
        step_done, step_added = sem("step_done"), sem("step_added")
        router_done, rmax_ready, rexp_done, mask_ready, pos_done = (
            sem(n) for n in ("router_done", "rmax_ready", "rexp_done", "mask_ready", "pos_done"))
        S_ready, gathered, gather_copied = (sem(n) for n in ("S_ready", "gathered", "gather_copied"))
        gate_done, up_done, silu_done, hid_ready, hidT_done, hidT_copied, down_done, y_copied, scattered = (
            sem(n) for n in ("gate_done", "up_done", "silu_done", "hid_ready", "hidT_done", "hidT_copied",
                             "down_done", "y_copied", "scattered"))
        tile_0_scattered = sem("tile_0_scattered")
        glog_done, gate_sig, gx_ready, YT_done, YT_copied, rgcn_done = (
            sem(n) for n in ("glog_done", "gate_sig", "gx_ready", "YT_done", "YT_copied", "rgcn_done"))
        plog_done, pnm_ready, pexp_done, prow_ready, pt_done, prob_copied, pb_done, sel_ready, selT_done, \
            selT_copied, f1_done, f1_biased, gelu_done, act1_ready, a1T_done, a1T_copied, f2_done, x_final = (
                sem(n) for n in ("plog_done", "pnm_ready", "pexp_done", "prow_ready", "pt_done", "prob_copied",
                                 "pb_done", "sel_ready", "selT_done", "selT_copied", "f1_done",
                                 "f1_biased", "gelu_done", "act1_ready", "a1T_done", "a1T_copied", "f2_done",
                                 "x_final"))
        over_counted, over_summed, over_flag = sem("over_counted"), sem("over_summed"), sem("over_flag")
        rest_loaded, rest_gate_up, rest_silu, rest_hid, rest_hidT, rest_hidT_copied, rest_down, rest_added = (
            sem(n) for n in ("rest_loaded", "rest_gate_up", "rest_silu", "rest_hid", "rest_hidT", "rest_hidT_copied",
                             "rest_down", "rest_added"))
        stored = sem("stored")

        block = ctx.enter_context(nc.Block())

        def step_bank(k, t):
            return bank[((6, 7), (5, 0))[k % 2][t]][:]

        BASIS_DMAS = BG

        @block.sync
        def _(sp):
            def basis_chunk(basis_d, c, slots, loaded):
                for g in range(BG):
                    rows = basis_d[8 * g:8 * g + BK[g] // 16, bass.ds(c * 64, 64), :]
                    sp.dma_start(ring[0:BK[g], slots[g // 2], g % 2 * 4 * H:(g % 2 + 1) * 4 * H],
                                 rows.rearrange("b (i j) o -> b i (j o)", j=4)).then_inc(loaded, 16)

            for k, e_d in enumerate((src_d, dst_d, type_d)):
                sp.dma_start(idx_i[:, k], e_d.rearrange("(p c) -> p c", p=P)).then_inc(ld_edges, 16)
            sp.dma_start(ew[:], ew_d.rearrange("(p c) -> p c", p=P)).then_inc(ld_edges, 16)
            late_const = CONST["tie_order"][0]
            sp.dma_start(const[:, N:late_const], const_d[:, N:late_const]).then_inc(ld_const, 16)
            sp.dma_start(x[:], x_d.rearrange("(t p) n -> p t n", p=P)).then_inc(ld_x, 16)
            for k, e_d in enumerate((emb1_d, emb2_d)):
                sp.dma_start(emb[:, k], e_d.rearrange("(c p) d -> p c d", p=P)).then_inc(ld_emb, 16)
            for q in range(2):
                basis_chunk(basis1_d, q, (2 * q, 2 * q + 1), basis_loaded[q])
            with sp.Fori(1, WC // 2) as i:
                for q in range(2):
                    sp.wait_ge(combined[q], i)
                    basis_chunk(basis1_d, 2 * i + q, (2 * q, 2 * q + 1), basis_loaded[q])

            def expert_gate(e, q):
                sp.dma_start(ring[:, SLOT[q][0], :].rearrange("p (c f) -> p c f", c=HC),
                             gate_d[bass.ds(e, 1)].rearrange("e (c p) f -> p (e c) f", p=P)).then_inc(gate_loaded[q], 16)

            def expert_up(e, q):
                sp.dma_start(ring[:, SLOT[q][1], :].rearrange("p (c f) -> p c f", c=HC),
                             up_d[bass.ds(e, 1)].rearrange("e (c p) f -> p (e c) f", p=P)).then_inc(up_loaded[q], 16)

            def expert_down(e, q):
                sp.dma_start(ring[:, SLOT[q][2], :].rearrange("p (c n) -> p c n", c=FF // P),
                             down_d[bass.ds(e, 1)].rearrange("e (c p) n -> p (e c) n", p=P)).then_inc(down_loaded[q], 16)

            expert_gate(0, 0)
            expert_up(0, 0)
            for i in range(EARLY // 2):
                for q in range(2):
                    sp.wait_ge(combined[q], WC // 2 + i)
                    basis_chunk(basis2_d, 2 * i + q, (2 * q, 2 * q + 1), basis_loaded[q])
            sp.wait_ge(combined[0], (WC + EARLY) // 2)
            expert_down(0, 0)
            expert_gate(1, 1)
            sp.wait_ge(combined[1], (WC + EARLY) // 2)
            expert_up(1, 1)
            expert_down(1, 1)
            with sp.Fori(1, NE // 2) as i:
                for q in range(2):
                    sp.wait_ge(up_done, 2 * i + q - 1)
                    expert_gate(2 * i + q, q)
                    expert_up(2 * i + q, q)
                    sp.wait_ge(down_done, 2 * i + q - 1)
                    expert_down(2 * i + q, q)
            for l, g_d in enumerate((gw1_d, gw2_d)):
                sp.dma_start(gate_w[:, l], g_d.rearrange("r n a -> r (n a)").unsqueeze(0)
                             .broadcast_to([P, 2, H])).then_inc(ld_gates[l], 16)
                if l == 0:
                    sp.dma_start(root[:], root1_d.rearrange("(c p) n -> p c n", p=P)).then_inc(ld_root, 16)
            for l, b_d in enumerate((bias1_d, bias2_d)):
                sp.dma_start(bias[l][:], b_d.unsqueeze(0).broadcast_to([P, H])).then_inc(ld_bias, 16)
            sp.wait_ge(up_done, NE - 1)
            basis_chunk(basis2_d, EARLY, LATE[0], late_loaded[0])
            sp.wait_ge(scattered, NE)
            sp.wait_ge(over_flag, 1)
            with sp.If(sp.value_load(flag[:], min_val=0, max_val=NT * P * NE) > 0):
                with sp.Fori(0, NE) as e:
                    sp.wait_ge(rest_added, e * NT + 1)
                    for k, (w_d, n) in enumerate(((gate_d, HC), (up_d, HC), (down_d, FF // P))):
                        sp.dma_start(ring[:, k, :].rearrange("p (c f) -> p c f", c=n),
                                     w_d[bass.ds(e, 1)].rearrange("e (c p) f -> p (e c) f", p=P)).then_inc(rest_loaded, 16)
                sp.wait_ge(rest_added, NE * NT + 1)
            for g in range(BG):
                if g == 2:
                    sp.wait_ge(late_combined, 1)
                    basis_chunk(basis2_d, EARLY + 1, LATE[1], late_loaded[1])
                    sp.wait_ge(root_used, 1)
                    sp.dma_start(root[:], root2_d.rearrange("(c p) n -> p c n", p=P)).then_inc(ld_root, 16)
                nb = BK[g] // 16
                sp.dma_start(ring[:, g, 0:nb * H].rearrange("p (b o) -> p b o", b=nb),
                             basis2_d[8 * g:8 * g + nb, H - P:H, :].rearrange("b i o -> i b o")).then_inc(pair_loaded[g], 16)
            sp.wait_ge(pair_added, 2 * 16)
            basis_chunk(basis2_d, EARLY + 2, LATE[2], late_loaded[2])
            sp.wait_ge(late_combined, 2)
            basis_chunk(basis2_d, EARLY + 3, LATE[3], late_loaded[3])
            sp.dma_start(wr[:], wr_d.rearrange("(c p) e -> p c e", p=P)).then_inc(ld_ffn, 16)
            sp.dma_start(b1[:], b1_d.rearrange("e f -> (e f)").unsqueeze(0).broadcast_to([P, E2 * F2])).then_inc(ld_ffn, 16)
            sp.dma_start(b2[:], b2_d).then_inc(ld_ffn, 16)
            sp.dma_start(const[:, late_const:], const_d[:, late_const:]).then_inc(ld_ffn, 16)
            sp.wait_ge(pair_added, 2 * NB)
            sp.dma_start(w2v(), w2_d.rearrange("e f n -> (e f) n").rearrange("(c p) n -> p c n", p=P)).then_inc(ld_ffn, 16)
            for c in range(HC):
                sp.dma_start(w1v()[:, c].rearrange("p (e f) -> p e f", e=E2),
                             w1_d[:, c * P:(c + 1) * P, :].rearrange("e p f -> p e f")).then_inc(ld_ffn, 16)
            for t in range(NT):
                sp.wait_ge(x_final, t + 1)
                sp.dma_start(out_d[t * P:(t + 1) * P, :], x[:, t]).then_inc(stored, 16)
            sp.wait_ge(stored, 16 * NT)

        @block.gpsimd
        def _(pool):
            pool.memset(zero_b[:], 0.0).then_inc(zeros_set, 1)
            pool.memset(CT[:], 0.0).then_inc(zeros_set, 1)

        @block.scalar
        def _(act):
            act.dma_start(cst("iota"), const_d[:, 0:N]).then_inc(ld_iota, 16)
            for l, a_d in enumerate((att1_d, att2_d)):
                act.dma_start(attb[l][:], a_d.unsqueeze(0).broadcast_to([P, 2, NB])).then_inc(ld_att, 16)
            act.dma_start(alpha, alpha_d.unsqueeze(0).broadcast_to([P, 1])).then_inc(ld_ab, 16)
            act.dma_start(beta, beta_d.unsqueeze(0).broadcast_to([P, 1])).then_inc(ld_ab, 16)
            act.dma_start(rw_sb[0:NE], rw_d).then_inc(ld_rw, 16)

            def ln_sqrt(n, tiles=range(NT)):
                for t in tiles:
                    act.wait_ge(var_ready, NT * (n - 1) + t + 1)
                    act.activation(rstd[:, t:t + 1], rstd[:, t:t + 1], ACT.Sqrt).then_inc(std_ready, 1)

            def copy_hT(n, tiles=range(NT)):
                for t in tiles:
                    act.wait_ge(transposed, NT * (n - 1) + t + 1)
                    act.copy(hT[:, :, t * P:(t + 1) * P],
                             bank[5 + t][:].rearrange("p (c n) -> p c n", c=HC)).then_inc(hT_copied, 1)

            def scale_onehots(ch, k):
                act.wait_ge(onehot_ready, ch + 1)
                for m in (1, 2):
                    ins = act.mul(onehot[:, k, 2 + m], onehot[:, k, 1], edge[:, 4 + m, bass.ds(ch, 1)])
                ins.then_inc(onehot_scaled, 1)

            def stage(q, n):
                act.wait_ge(combined[q], n + 1)
                act.copy(wstage[:, q], bank[3 + q][:]).then_inc(wstaged[q], 1)

            def keep(q, n):
                act.wait_ge(regrouped[q], n + 1)
                act.copy(wcomb[:, bass.ds(n * 2 + q, 1), :].rearrange("p a n -> p (a n)"),
                         bank[3 + q][:]).then_inc(wcopied[q], 1)

            def weights_and_edges(i):
                for q in range(2):
                    for k in range(EPC):
                        scale_onehots(EFIRST + (2 * i - 2 + q) * EPC + k, (q * EPC + k) % NOH)
                    stage(q, i)
                    keep(1 - q, i - 1 + q)

            for k in range(4):
                scale_onehots(k, k)
            ln_sqrt(1)
            for k in range(4, 8):
                scale_onehots(k, k)
            act.wait_ge(logits_done, 1)
            act.mul(lrelu, bank[5][:].rearrange("p (t s) -> p t s", t=NT), 0.2).then_inc(scaled_done, 1)
            for k in range(8, EFIRST):
                scale_onehots(k, k % NOH)
            act.wait_ge(nmax_ready, 1)
            for t in range(NT):
                act.activation(sim_e[:, t], lrelu[:, t], ACT.Exp, bias=nmax[:, t:t + 1],
                               accum_out=rsum[:, t:t + 1]).then_inc(exp_done, 1)
            act.wait_ge(ld_ab, 32)
            act.activation(small[:, 0:2], small[:, 0:2], ACT.Exp).then_inc(ab_ready, 1)
            stage(0, 0)
            stage(1, 0)
            keep(0, 0)
            with act.Fori(1, EPAIRS) as i:
                weights_and_edges(i)
            stage(0, EPAIRS)
            keep(1, EPAIRS - 1)
            keep(0, EPAIRS)
            stage(1, EPAIRS)
            keep(1, EPAIRS)
            ln_sqrt(2)
            stage(0, WC // 2)
            keep(0, WC // 2)
            act.wait_ge(rmax_ready, 1)
            for t in range(NT):
                act.activation(rexp[:, t], RL[:, t], ACT.Exp, bias=m1[:, t:t + 1]).then_inc(rexp_done, 1)
            stage(1, WC // 2)
            keep(1, WC // 2)

            def copy_gathered(e, q):
                act.wait_ge(gathered, e + 1)
                act.copy(area[:, 512 * q:512 * q + 512], bank[5][:]).then_inc(gather_copied, 1)

            def expert(e, q, last=False):
                act.wait_ge(gate_done, e + 1)
                wait(act, hid_ready, e)
                act.activation(sg, bank[2][:], ACT.Silu).then_inc(silu_done, 1)
                if not last:
                    copy_gathered(e + 1, 1 - q)
                act.wait_ge(hidT_done, e + 1)
                act.copy(hidT[q], bank[2][:]).then_inc(hidT_copied, 1)
                act.wait_ge(down_done, e + 1)
                act.copy(y[q], bank[4][:]).then_inc(y_copied, 1)

            copy_gathered(0, 0)
            expert(0, 0)
            expert(1, 1)
            with act.Fori(1, NE // 2 - 1) as i:
                for q in range(2):
                    expert(2 * i + q, q)
            expert(NE - 2, 0)
            expert(NE - 1, 1, last=True)

            act.wait_ge(zeros_set, 1)
            act.activation(spare, zero_b[:, 0:1], ACT.Sqrt)

            act.wait_ge(scattered, NE)
            act.wait_ge(over_flag, 1)
            with act.If(act.value_load(flag[:], min_val=0, max_val=NT * P * NE) > 0):
                with act.Fori(0, NE) as e:
                    for k in range(2 * NT):
                        act.wait_ge(rest_gate_up, e * 2 * NT + k + 1)
                        act.activation(sg, bank[2][:], ACT.Silu).then_inc(rest_silu, 1)

            def late_stage(n):
                act.wait_ge(late_combined, n + 1)
                act.copy(wstage[:, 0], late_bank[n][:]).then_inc(late_staged, 1)

            def late_keep(n):
                act.wait_ge(late_regrouped, n + 1)
                act.copy(wcomb[:, WC + EARLY + n], late_bank[n][:]).then_inc(late_copied, 1)

            for t in range(NT):
                ln_sqrt(3, (t,))
                copy_hT(3, (t,))
            for l in range(2):
                if l == 1:
                    for t in range(NT):
                        copy_hT(4, (t,))
                        (late_stage if t == 0 else late_keep)(1)
                act.wait_ge(glog_done, NT * (l + 1))
                act.activation(gates, gate_logits, ACT.Sigmoid).then_inc(gate_sig, 1)
                act.wait_ge(gate_sig, l + 1)
                for t in range(NT):
                    act.mul(gx[:, 1, t], h[:, t], gates[:, 2 * t + 1:2 * t + 2]).then_inc(gx_ready, 1)
                if l == 0:
                    late_stage(0)
                    late_keep(0)
                for k in range(WC // 2):
                    act.wait_ge(YT_done, 4 * l + k + 1)
                    act.copy(YT[:, 2 * k:2 * k + 2], bank[k][:].rearrange("p (c n) -> p c n", c=2)).then_inc(YT_copied, 1)
            for n in (2, 3):
                late_stage(n)
                late_keep(n)
            for t in range(NT):
                ln_sqrt(4, (t,))
                copy_hT(5, (t,))
            act.wait_ge(pnm_ready, 1)
            act.activation(prow[:], bank[7][0:E2, 0:N], ACT.Exp, bias=pnm, accum_out=psum_).then_inc(pexp_done, 1)

            def copy_act1T(t):
                act.wait_ge(selT_done, t + 1)
                act.copy(PT[:, t * P:(t + 1) * P], bank[(7, 2)[t]][0:E2, 0:P]).then_inc(selT_copied, 1)
                act.wait_ge(a1T_done, t + 1)
                act.copy(act1T[:, :, t * P:(t + 1) * P],
                         bank[5 + t][:].rearrange("p (c n) -> p c n", c=HC)).then_inc(a1T_copied, 1)

            for t in range(NT):
                act.wait_ge(f1_biased, t + 1)
                act.activation(act1[:, t], act1[:, t], ACT.Gelu).then_inc(gelu_done, 1)
                copy_act1T(t)

        @block.vector
        def _(dve):
            chain = Chain(dve, dve_chain)
            link = chain.link

            def layer_norm(n, finish_x=None, tiles=range(NT)):
                for t in tiles:
                    if finish_x:
                        finish_x(t)
                    link(dve.bn_stats(stat[:, t], x[:, t]))
                    link(dve.bn_aggr(mv[:, t], stat[:, t]))
                    dve.tensor_scalar(rstd[:, t:t + 1], mv[:, t, 1:2], EPS, None, ALU.add).then_inc(var_ready, 1)
                    dve.wait_ge(std_ready, NT * (n - 1) + t + 1)
                    link(dve.reciprocal(rstd[:, t:t + 1], rstd[:, t:t + 1]))
                    dve.tensor_scalar(h[:, t], x[:, t], mv[:, t, 0:1], rstd[:, t:t + 1], ALU.subtract,
                                      ALU.mult).then_inc(normed, 1)

            def copy_hT(n, tiles=range(NT)):
                for t in tiles:
                    dve.wait_ge(transposed, NT * (n - 1) + t + 1)
                    dve.tensor_copy(hT[:, :, t * P:(t + 1) * P],
                                    bank[5 + t][:].rearrange("p (c n) -> p c n", c=HC)).then_inc(hT_copied, 1)

            dve.wait_ge(ld_edges, 64)
            link(dve.tensor_copy(edge[:, 0:3], idx_i[:]))
            link(dve.tensor_scalar(edge[:, 3], edge[:, 2], 0.0, None, ALU.is_equal))
            link(dve.tensor_scalar(edge[:, 2], edge[:, 3], 1.0 - PACK, float(PACK), ALU.mult, ALU.add))
            link(dve.tensor_copy(wpart[:, 0], ew[:]))
            link(dve.tensor_tensor(ew[:], ew[:], wpart[:, 0], ALU.subtract))
            link(dve.tensor_copy(wpart[:, 1], ew[:]))
            link(dve.tensor_tensor(ew[:], ew[:], wpart[:, 1], ALU.subtract))
            link(dve.tensor_copy(wpart[:, 2], ew[:]))
            link(dve.tensor_copy(edge[:, 4:7], wpart[:]))
            dve.wait_ge(ld_iota, 16)
            link(dve.tensor_copy(iota_b[:], cst("iota")))

            def edge_onehots(first, chunks, fresh=False):
                for k in chunks:
                    ch = first + k
                    col = [edge[:, m, bass.ds(ch, 1)] for m in range(5)]
                    b = k % NOH
                    if not fresh:
                        dve.wait_ge(onehot_used, ch - (NOH - 1))
                    dve.tensor_scalar(onehot[:, b, 1], iota_b[:], col[1], None, ALU.is_equal)
                    dve.tensor_scalar(onehot[:, b, 0], iota_b[:], col[0], None, ALU.is_equal)
                    dve.tensor_scalar(onehot[:, b, 2], iota_b[:], col[1], col[4], ALU.is_equal,
                                      ALU.mult).then_inc(onehot_ready, 1)

            edge_onehots(0, range(4), fresh=True)
            dve.wait_ge(ld_x, 16)
            layer_norm(1)
            copy_hT(1)
            edge_onehots(0, range(4, 8), fresh=True)
            dve.wait_ge(ld_const, 16)
            dve.wait_ge(ld_att, 32)
            for l in range(2):
                for g in range(BG):
                    nb = BK[g] // 16
                    link(dve.tensor_tensor(attp[:, l, :, 0:nb], attb[l][:, :, 8 * g:8 * g + nb],
                                           cst("block16")[:, 0:nb].unsqueeze(1).broadcast_to([P, 2, nb]), ALU.mult))
                    link(dve.tensor_reduce(atts[:, l, g], attp[:, l, :, 0:nb], AX.X, ALU.add))
                dve.tensor_tensor(attw[l][:], cst("diag16").unsqueeze(1).unsqueeze(1).broadcast_to([P, BG, 2, 16]),
                                  atts[:, l].unsqueeze(3).broadcast_to([P, BG, 2, 16]), ALU.mult).then_inc(attw_ready, 1)
            dve.wait_ge(x12_done, 1)
            dve.tensor_copy(x12T, bank[7][:]).then_inc(x12_copied, 1)
            dve.wait_ge(rwT_done, 1)
            dve.tensor_copy(rwT[:], bank[6][:, 0:HC * NE].rearrange("p (c e) -> p c e", c=HC)).then_inc(rwT_copied, 1)
            edge_onehots(0, range(8, EFIRST))
            dve.wait_ge(scaled_done, 1)
            link(dve.tensor_tensor(lrelu, lrelu, bank[5][:].rearrange("p (t s) -> p t s", t=NT), ALU.max))
            link(dve.tensor_reduce(rmax, lrelu, AX.X, ALU.max))
            dve.tensor_scalar(nmax, rmax, -1.0, None, ALU.mult).then_inc(nmax_ready, 1)
            with dve.Fori(EFIRST // NOH, ECH // NOH) as i:
                edge_onehots(i * NOH, range(NOH))

            dve.wait_ge(exp_done, NT)
            dve.wait_ge(onehot_used, ECH)
            link(dve.reciprocal(rinv, rsum))
            A = bank[0][:].rearrange("p (t s) -> p t s", t=NT)
            for t in range(NT):
                link(dve.scalar_tensor_tensor(V[:, t], sim_e[:, t], rinv[:, t:t + 1], A[:, t], ALU.mult, ALU.mult,
                                              accum_out=norm[:, t:t + 1]))
            for t in range(NT):
                d = V[:, t, t * P:(t + 1) * P]
                dve.tensor_tensor(d, d, ident, ALU.add).then_inc(V_ready, 1)
            dve.wait_ge(ab_ready, 1)
            link(dve.tensor_tensor(ab, alpha, beta, ALU.add))
            link(dve.tensor_scalar(den, norm, alpha, ab, ALU.mult, ALU.add))
            link(dve.reciprocal(rden, den))
            link(dve.tensor_scalar(ra, rden, alpha, None, ALU.mult))
            link(dve.tensor_scalar(rb, rden, beta, None, ALU.mult))
            for t in range(NT):
                link(dve.tensor_scalar(inb[:, t], h[:, t], rb[:, t:t + 1], None, ALU.mult))
            dve.wait_ge(VT_done, 1)
            dve.tensor_copy(VT, bank[5][:].rearrange("p (t s) -> p t s", t=NT)).then_inc(VT_copied, 1)
            for k in range(ITERS):
                for t in range(NT):
                    dve.wait_ge(step_done, NT * k + t + 1)
                    dve.scalar_tensor_tensor(out5[:, k % 2, t], step_bank(k, t), ra[:, t:t + 1], inb[:, t],
                                             ALU.mult, ALU.add).then_inc(step_added, 1)
            dve.wait_ge(step_added, NT * ITERS)

            layer_norm(2, lambda t: link(dve.tensor_tensor(x[:, t], x[:, t], out5[:, (ITERS - 1) % 2, t], ALU.add)))
            copy_hT(2)
            dve.wait_ge(router_done, 1)
            link(dve.tensor_copy(RL, bank[7][:, 0:NT * NE].rearrange("p (t e) -> p t e", t=NT)))
            link(dve.tensor_reduce(m1, RL, AX.X, ALU.max))
            dve.tensor_scalar(m1, m1, -1.0, None, ALU.mult).then_inc(rmax_ready, 1)
            eq = lrelu.rearrange("p t (a b) -> p t a b", a=NE)
            for t in range(NT):
                other = RL[:, t].unsqueeze(1).broadcast_to([P, NE, NE])
                own = RL[:, t].unsqueeze(2).broadcast_to([P, NE, NE])
                link(dve.tensor_tensor(cmpg[:, t], other, own, ALU.is_gt))
                link(dve.tensor_tensor(eq[:, t], other, own, ALU.is_equal))
                link(dve.tensor_tensor(eq[:, t], eq[:, t],
                                       cst("earlier_expert").rearrange("p (a b) -> p a b", a=NE), ALU.mult))
            link(dve.tensor_tensor(cmpg, cmpg, eq, ALU.add))
            link(dve.tensor_reduce(rank, cmpg, AX.X, ALU.add))
            dve.tensor_scalar(mask, rank, 1.5, None, ALU.is_lt).then_inc(mask_ready, 1)
            dve.wait_ge(mask_ready, 1)
            dve.wait_ge(rexp_done, NT)
            link(dve.tensor_tensor(rexp, rexp, mask, ALU.mult))
            link(dve.tensor_reduce(s1, rexp, AX.X, ALU.add))
            link(dve.reciprocal(r1, s1))
            for t in range(NT):
                link(dve.tensor_scalar(ce[:, t], rexp[:, t], r1[:, t:t + 1], None, ALU.mult))
            dve.wait_ge(pos_done, 1)
            pos = bank[7][:, 64:64 + NT * NE].rearrange("p (t e) -> p t e", t=NT)
            link(dve.scalar_tensor_tensor(posm, pos, 1.0, mask, ALU.add, ALU.mult))
            link(dve.tensor_scalar(posm, posm, -1.0, None, ALU.add))
            link(dve.tensor_scalar(over, posm, LIMIT - 0.5, None, ALU.is_ge))
            link(dve.tensor_tensor(ce_over, ce, over, ALU.mult))
            dve.tensor_reduce(over_n, over, AX.XY, ALU.add).then_inc(over_counted, 1)
            dve.wait_ge(over_summed, 1)
            dve.tensor_copy(flag[:], bank[7][0:1, 128:129]).then_inc(over_flag, 1)

            slots = cst("slots")

            def select(e, q):
                for t in range(NT):
                    dve.tensor_scalar(S[q][:, t], slots[:, 0:CAP], posm[:, t, bass.ds(e, 1)], None,
                                      ALU.is_equal).then_inc(S_ready, 1)
                    dve.tensor_scalar(SW[q][:, t], slots, posm[:, t, bass.ds(e, 1)], ce[:, t, bass.ds(e, 1)],
                                      ALU.is_equal, ALU.mult).then_inc(S_ready, 1)

            def count_onehots(ch, k):
                col = [edge[:, m, bass.ds(ch, 1)] for m in range(3)]
                wait(dve, count_used, ch - 1)
                dve.tensor_scalar(count_onehot[:, k, 0], iota_b[:], col[1], None, ALU.is_equal)
                dve.tensor_scalar(count_onehot[:, k, 1], iota_b[:], col[0], col[2], ALU.is_equal,
                                  ALU.mult).then_inc(count_ready, 1)

            def add_counts(e):
                dve.wait_ge(count_used, e * CPE)
                dve.tensor_scalar(count_1, bank[7][:], 1.0 / PACK, ROUND, ALU.mult, ALU.add).then_inc(unpacked, 1)
                dve.wait_ge(unpacked, e * 2 - 3)
                dve.tensor_scalar(count_1, count_1, -ROUND, None, ALU.add).then_inc(unpacked, 1)
                dve.wait_ge(unpacked, e * 2 - 2)
                dve.scalar_tensor_tensor(count_0, count_1, -float(PACK), bank[7][:], ALU.mult,
                                         ALU.add).then_inc(unpacked, 2)
                dve.wait_ge(unpacked, e * 2)
                for r, c in enumerate((count_0, count_1)):
                    total = CT[:, r].rearrange("p t s -> p (t s)")
                    dve.tensor_tensor(total, total, c, ALU.add).then_inc(counted, 1)
                dve.wait_ge(counted, e)

            def expert(e, q, first=False, last=False):
                if q == 0 and not first:
                    add_counts(e)
                for k in range(2):
                    count_onehots(e * CPE + k, k)
                if not last:
                    select(e + 1, 1 - q)
                dve.wait_ge(silu_done, e + 1)
                dve.wait_ge(up_done, e + 1)
                dve.tensor_tensor(hid[q], sg, bank[3][:], ALU.mult).then_inc(hid_ready, 1)
                for k in range(2, CPE):
                    count_onehots(e * CPE + k, k % 2)

            dve.wait_ge(zeros_set, 2)
            select(0, 0)
            expert(0, 0, first=True)
            expert(1, 1)
            with dve.Fori(1, NE // 2 - 1) as i:
                for q in range(2):
                    expert(2 * i + q, q)
            expert(NE - 2, 0)
            expert(NE - 1, 1, last=True)
            with dve.If(dve.value_load(flag[:], min_val=0, max_val=NT * P * NE) > 0):
                dve.tensor_copy(small[:, 1022:1023], over_n).then_inc(rest_added, 1)
                with dve.Fori(0, NE) as e:
                    for t in range(NT):
                        for f in range(2):
                            k = 2 * t + f
                            dve.wait_ge(rest_silu, e * 2 * NT + k + 1)
                            dve.tensor_tensor(hid[0], sg, bank[3][:], ALU.mult).then_inc(rest_hid, 1)
                            dve.wait_ge(rest_hidT, e * 2 * NT + k + 1)
                            dve.tensor_copy(hidT[0], bank[2][:]).then_inc(rest_hidT_copied, 1)
                        dve.wait_ge(rest_down, e * NT + t + 1)
                        dve.scalar_tensor_tensor(x[:, t], bank[4][:], ce_over[:, t, bass.ds(e, 1)], x[:, t],
                                                 ALU.mult, ALU.add).then_inc(rest_added, 1)
                dve.wait_ge(rest_added, NE * NT + 1)

            for t in range(NT):
                if t == 0:
                    dve.wait_ge(tile_0_scattered, 1)
                else:
                    dve.wait_ge(scattered, NE)
                layer_norm(3, lambda t: link(dve.tensor_tensor(x[:, t], x[:, t], bank[t][:], ALU.add)), tiles=(t,))
            pair_sum = [wcomb[:, 2 * WC - 2 + r] for r in range(2)]

            def gate_dots(l, t):
                dve.wait_ge(ld_gates[l], 16)
                wait(dve, glog_done, NT * l)
                dve.wait_ge(normed, NT * (2 + l) + t + 1)
                for r in range(2):
                    ins = dve.scalar_tensor_tensor(gate_products[:, t, r], h[:, t], 1.0, gate_w[:, l, r], ALU.mult, ALU.mult,
                                                   accum_out=gate_logits[:, 2 * t + r:2 * t + r + 1])
                ins.then_inc(glog_done, 1)

            for t in range(NT):
                gate_dots(0, t)

            def combine_pair(first, end):
                def add(b):
                    basis = pair_basis[:, bass.ds(b * H, H)]
                    for r in range(2):
                        a = attb[1][:, r, bass.ds(b, 1)]
                        if isinstance(b, int) and b == 0:
                            dve.tensor_scalar(pair_sum[r], basis, a, None, ALU.mult).then_inc(pair_added, 1)
                        else:
                            dve.wait_ge(pair_added, b * 2 + r - 1)
                            dve.scalar_tensor_tensor(pair_sum[r], basis, a, pair_sum[r], ALU.mult,
                                                     ALU.add).then_inc(pair_added, 1)

                for g in range(first // 8, (end + 7) // 8):
                    lo, hi = max(first, 8 * g), min(end, 8 * g + 8)
                    dve.wait_ge(pair_loaded[g], 16)
                    if lo == 0:
                        add(0)
                        lo = 1
                    with dve.Fori(lo, hi) as b:
                        add(b)

            for l in range(2):
                dve.wait_ge(gate_sig, l + 1)
                for t in range(NT):
                    dve.tensor_scalar(gx[:, 0, t], h[:, t], gates[:, 2 * t:2 * t + 1], None,
                                      ALU.mult).then_inc(gx_ready, 1)
                if l == 0:
                    add_counts(NE)
                    for t in range(NT):
                        combine_pair(*PAIR_BASES[t])
                        dve.wait_ge(rgcn_done, t + 1)
                        dve.wait_ge(gx_ready, 4)
                        dve.wait_ge(ld_bias, 16 * 2)
                        link(dve.tensor_tensor(h[:, t], bank[5 + t][:], bias[0][:], ALU.add))
                        dve.tensor_scalar(h[:, t], h[:, t], 0.0, None, ALU.max).then_inc(normed, 1)
                        gate_dots(1, t)
                    combine_pair(*PAIR_BASES[2])
            combine_pair(*PAIR_BASES[3])
            for t in range(NT):
                link(dve.tensor_tensor(x[:, t], x[:, t], bias[1][:], ALU.add))

            def second_layer(t):
                dve.wait_ge(rgcn_done, NT + t + 1)
                link(dve.tensor_tensor(x[:, t], x[:, t], bank[5 + t][:], ALU.add))

            for t in range(NT):
                layer_norm(4, second_layer, tiles=(t,))
            dve.wait_ge(ld_ffn, 16 * (5 + HC))

            def bias_f1(t):
                dve.wait_ge(f1_done, t + 1)
                dve.tensor_tensor(act1[:, t], bank[5 + t][:], b1[:], ALU.add).then_inc(f1_biased, 1)

            bias_f1(0)
            dve.wait_ge(plog_done, 1)
            link(dve.tensor_reduce(pmx, bank[7][0:E2, 0:N], AX.X, ALU.max))
            dve.tensor_scalar(pnm, pmx, -1.0, None, ALU.mult).then_inc(pnm_ready, 1)
            dve.wait_ge(pexp_done, 1)
            link(dve.reciprocal(pinv, psum_))
            dve.tensor_scalar(prow[:], prow[:], pinv, None, ALU.mult).then_inc(prow_ready, 1)

            dve.wait_ge(pt_done, 1)
            dve.tensor_copy(prob, bank[7][:, 256:256 + NT * E2].rearrange("p (t e) -> p t e", t=NT)).then_inc(prob_copied, 1)
            order = cst("tie_order").rearrange("p (t s) -> p t s", t=NT)
            for t in range(NT):
                for e in range(E2):
                    dve.wait_ge(pb_done, e // 2 + 1)
                    ins = dve.scalar_tensor_tensor(cmp[:, t, e], order[:, t], prob[:, t, e:e + 1],
                                                   bank[e // 2][:, (e % 2) * N:(e % 2) * N + N], ALU.mult, ALU.is_lt,
                                                   accum_out=rank2[:, t, e:e + 1])
                link(ins)
                link(dve.tensor_scalar(rank2[:, t], rank2[:, t], C2 - 0.5, None, ALU.is_lt))
                dve.tensor_tensor(sel[:, t], rank2[:, t], prob[:, t], ALU.mult).then_inc(sel_ready, 1)
                dve.wait_ge(sel_ready, t + 1)
                dve.wait_ge(gelu_done, t + 1)
                a = act1[:, t].rearrange("p (e f) -> p e f", e=E2)
                dve.tensor_tensor(a, a, sel[:, t].unsqueeze(2).broadcast_to([P, E2, F2]),
                                  ALU.mult).then_inc(act1_ready, 1)
                if t == 0:
                    bias_f1(1)
            for t in range(NT):
                dve.wait_ge(f2_done, t + 1)
                dve.tensor_tensor(x[:, t], x[:, t], bank[4 - t][:], ALU.add).then_inc(x_final, 1)

        @block.tensor
        def _(pe):
            def mm(out, lhsT, rhs, start, stop):
                return pe.matmul(out, lhsT, rhs, start=start, stop=stop, skip_group_check=True)

            def transpose_h(n, tiles=range(NT)):
                for t in tiles:
                    pe.wait_ge(normed, NT * (n - 1) + t + 1)
                    for c in range(HC):
                        ins = pe.transpose(bank[5 + t][:, c * P:(c + 1) * P], h[:, t, c * P:(c + 1) * P], ident)
                    ins.then_inc(transposed, 1)

            def keep_clock_up(n):
                for _ in range(n):
                    mm(bank[6][:], zero_b[:, 0:P], zero_b[:], True, True)

            def edges(ch, k):
                pe.wait_ge(onehot_ready, ch + 1)
                pe.wait_ge(onehot_scaled, ch + 1)
                for t in range(NT):
                    lhsT = onehot[:, k, 0, t * P:(t + 1) * P]
                    for m in range(3):
                        ins = mm(bank[0][:, t * N:(t + 1) * N], lhsT, onehot[:, k, 2 + m], False, False)
                ins.then_inc(onehot_used, 1)

            def combine(l, slots, acc):
                for g in range(BG):
                    for j in range(4):
                        ins = mm(acc[32 * j:32 * j + 32, :], attw[l][0:BK[g], g].rearrange("p r i -> p (r i)"),
                                 ring[0:BK[g], slots[g // 2], (g % 2 * 4 + j) * H:(g % 2 * 4 + j + 1) * H],
                                 g == 0, g == BG - 1)
                return ins

            def combine_early(l, q, n):
                pe.wait_ge(basis_loaded[q], (n + 1) * 16 * BASIS_DMAS)
                wait(pe, wcopied[q], n)
                combine(l, (2 * q, 2 * q + 1), bank[3 + q]).then_inc(combined[q], 1)

            def regroup(q, n):
                pe.wait_ge(wstaged[q], n + 1)
                mm(bank[3 + q][:], cst("regroup"), wstage[:, q], True, True).then_inc(regrouped[q], 1)

            def weights_and_edges(i):
                for q in range(2):
                    for k in range(EPC):
                        if k == EPC - NOH:
                            combine_early(0, q, i)
                            regroup(1 - q, i - 1 + q)
                        edges(EFIRST + (2 * i - 2 + q) * EPC + k, (q * EPC + k) % NOH)

            pe.wait_ge(zeros_set, 1)
            mm(bank[0][:], zero_b[:, 0:P], zero_b[:], True, False)
            for k in range(4):
                edges(k, k)

            pe.wait_ge(ld_const, 16)
            transpose_h(1)
            pe.wait_ge(hT_copied, NT)
            pe.wait_ge(ld_emb, 32)
            for k in range(2):
                for c in range(HC):
                    ins = mm(bank[7][:, k * N:(k + 1) * N], emb[:, k, c], hT[:, c], c == 0, c == HC - 1)
            ins.then_inc(x12_done, 1)
            pe.wait_ge(ld_rw, 16)
            for c in range(HC):
                ins = pe.transpose(bank[6][:, c * NE:(c + 1) * NE], rw_sb[:, c * P:(c + 1) * P], ident[0:NE, 0:NE])
            ins.then_inc(rwT_done, 1)
            for k in range(4, 8):
                edges(k, k)
            pe.wait_ge(x12_copied, 1)
            for t in range(NT):
                ins = mm(bank[5][:, t * N:(t + 1) * N], x12T[:, t * P:(t + 1) * P], x12T[:, N:2 * N], True, True)
            ins.then_inc(logits_done, 1)

            pe.wait_ge(attw_ready, 2)
            combine_early(0, 0, 0)
            for k in range(8, EFIRST):
                if k == EFIRST - 4:
                    combine_early(0, 1, 0)
                    regroup(0, 0)
                edges(k, k % NOH)
            with pe.Fori(1, EPAIRS) as i:
                weights_and_edges(i)
            combine_early(0, 0, EPAIRS)
            regroup(1, EPAIRS - 1)

            pe.wait_ge(V_ready, NT)
            for s in range(NT):
                for t in range(NT):
                    ins = pe.transpose(bank[5][:, s * N + t * P:s * N + (t + 1) * P], V[:, t, s * P:(s + 1) * P], ident)
            ins.then_inc(VT_done, 1)
            regroup(0, EPAIRS)
            pe.wait_ge(VT_copied, 1)
            for k in range(ITERS):
                if k == 2:
                    combine_early(0, 1, EPAIRS)
                for s in range(NT):
                    wait(pe, step_added, NT * (k - 1) + s + 1)
                    for t in range(NT):
                        cur = h[:, s] if k == 0 else out5[:, (k - 1) % 2, s]
                        ins = mm(step_bank(k, t), VT[:, s, t * P:(t + 1) * P], cur, s == 0, s == NT - 1)
                        if s == NT - 1:
                            ins.then_inc(step_done, 1)

            regroup(1, WC // 2 - 1)
            combine_early(1, 0, WC // 2)
            transpose_h(2)
            pe.wait_ge(hT_copied, 2 * NT)
            pe.wait_ge(rwT_copied, 1)
            for t in range(NT):
                for c in range(HC):
                    ins = mm(bank[7][:, t * NE:(t + 1) * NE], hT[:, c, t * P:(t + 1) * P], rwT[:, c, 0:NE], c == 0, c == HC - 1)
            ins.then_inc(router_done, 1)
            regroup(0, WC // 2)
            combine_early(1, 1, WC // 2)
            pe.wait_ge(mask_ready, 1)
            mm(bank[7][:, 64:64 + NE], cst("before"), mask[:, 0], True, True)
            mm(bank[7][:, 64 + NE:64 + 2 * NE], cst("before"), mask[:, 1], True, False)
            mm(bank[7][:, 64 + NE:64 + 2 * NE], cst("ones"), mask[:, 0], False, True).then_inc(pos_done, 1)

            pe.wait_ge(over_counted, 1)
            mm(bank[7][0:1, 128:129], over_n, cst("ones")[:, 0:1], True, True).then_inc(over_summed, 1)

            pe.wait_ge(over_flag, 1)
            for b in (0, 1):
                mm(bank[b][:], zero_b[:, 0:P], zero_b[:], True, False)

            def gather(e, q):
                pe.wait_ge(S_ready, 4 * (e + 1))
                wait(pe, gather_copied, e)
                for c in range(HC):
                    for s in range(NT):
                        ins = mm(bank[5][:, c * CAP:(c + 1) * CAP], h[:, s, c * P:(c + 1) * P], S[q][:, s],
                                 s == 0, s == NT - 1)
                for t in range(NT):
                    ins = pe.transpose(bank[5][:, N + t * P:N + (t + 1) * P], SW[q][:, t], ident)
                ins.then_inc(gathered, 1)

            def count_edges(e, first, end):
                for k in range(first, end):
                    pe.wait_ge(count_ready, e * CPE + k + 1)
                    for t in range(NT):
                        ins = mm(bank[7][:, t * N:(t + 1) * N], count_onehot[:, k % 2, 0, t * P:(t + 1) * P],
                                 count_onehot[:, k % 2, 1], False, False)
                    ins.then_inc(count_used, 1)

            def scatter_tile(t, e, q):
                pe.wait_ge(y_copied, e + 1)
                return mm(bank[t][:], ST[q][:, t * P:(t + 1) * P], y[q], False, False)

            def scatter(e, q, last=False):
                for t in range(NT):
                    ins = scatter_tile(t, e, q)
                    if last and t == 0:
                        ins.then_inc(tile_0_scattered, 1)
                ins.then_inc(scattered, 1)

            def expert(e, q, first=False, last=False):
                g, u, d = SLOT[q]
                pe.wait_ge(gate_loaded[q], 16 * (e // 2 + 1) if isinstance(e, int) else (e - q) * 8 + 16)
                pe.wait_ge(gather_copied, e + 1)
                for c in range(HC):
                    for f in range(2):
                        ins = mm(bank[2][64 * f:64 * f + 64, :], xg[q][:, c], ring[:, g, c * FF + f * 512:c * FF + f * 512 + 512],
                                 c == 0, c == HC - 1)
                ins.then_inc(gate_done, 1)
                pe.wait_ge(up_loaded[q], 16 * (e // 2 + 1) if isinstance(e, int) else (e - q) * 8 + 16)
                wait(pe, hid_ready, e)
                for c in range(HC):
                    for f in range(2):
                        ins = mm(bank[3][64 * f:64 * f + 64, :], xg[q][:, c], ring[:, u, c * FF + f * 512:c * FF + f * 512 + 512],
                                 c == 0, c == HC - 1)
                ins.then_inc(up_done, 1)
                if last:
                    scatter_tile(0, e - 1, 1 - q)
                elif not first:
                    scatter(e - 1, 1 - q)
                if not last:
                    gather(e + 1, 1 - q)
                pe.wait_ge(hid_ready, e + 1)
                for c in range(HC):
                    ins = pe.transpose(bank[2][:, c * P:(c + 1) * P], hid[q][:, c * P:(c + 1) * P], ident)
                ins.then_inc(hidT_done, 1)
                if q == 0:
                    wait(pe, counted, e)
                    mm(bank[7][:], zero_b[:, 0:P], zero_b[:], True, False)
                count_edges(e, 0, 2)
                pe.wait_ge(down_loaded[q], 16 * (e // 2 + 1) if isinstance(e, int) else (e - q) * 8 + 16)
                pe.wait_ge(hidT_copied, e + 1)
                wait(pe, y_copied, e)
                for c in range(HC):
                    for f in range(2):
                        ins = mm(bank[4][64 * f:64 * f + 64, :], hidT[q][:, c * P + 64 * f:c * P + 64 * f + 64],
                                 ring[:, d, (f * HC + c) * H:(f * HC + c + 1) * H], c == 0, c == HC - 1)
                ins.then_inc(down_done, 1)
                count_edges(e, 2, CPE)
                if last:
                    scatter_tile(1, e - 1, 1 - q).then_inc(scattered, 1)

            regroup(1, WC // 2)
            gather(0, 0)
            for q in range(2):
                pe.wait_ge(wcopied[q], (WC + EARLY) // 2)
            expert(0, 0, first=True)
            expert(1, 1)
            with pe.Fori(1, NE // 2 - 1) as i:
                for q in range(2):
                    expert(2 * i + q, q)
            expert(NE - 2, 0)
            expert(NE - 1, 1, last=True)
            scatter(NE - 1, 1, last=True)

            pe.wait_ge(y_copied, NE)
            with pe.If(pe.value_load(flag[:], min_val=0, max_val=NT * P * NE) > 0):
                with pe.Fori(0, NE) as e:
                    pe.wait_ge(rest_loaded, e * 48 + 48)
                    for t in range(NT):
                        for f in range(2):
                            k = 2 * t + f
                            for w, b in ((0, 2), (1, 3)):
                                for c in range(HC):
                                    ins = mm(bank[b][:], hT[:, c, t * P:(t + 1) * P],
                                             ring[:, w, c * FF + f * 512:c * FF + f * 512 + 512], c == 0, c == HC - 1)
                            ins.then_inc(rest_gate_up, 1)
                            pe.wait_ge(rest_hid, e * 2 * NT + k + 1)
                            for c in range(HC):
                                ins = pe.transpose(bank[2][:, c * P:(c + 1) * P], hid[0][:, c * P:(c + 1) * P], ident)
                            ins.then_inc(rest_hidT, 1)
                            pe.wait_ge(rest_hidT_copied, e * 2 * NT + k + 1)
                            pe.wait_ge(rest_added, e * NT + t + 1)
                            for c in range(HC):
                                ins = mm(bank[4][:], hidT[0][:, c * P:(c + 1) * P],
                                         ring[:, 2, (f * HC + c) * H:(f * HC + c + 1) * H],
                                         f == 0 and c == 0, f == 1 and c == HC - 1)
                        ins.then_inc(rest_down, 1)

            def combine_late(n):
                pe.wait_ge(late_loaded[n], 16 * BASIS_DMAS)
                wait(pe, late_copied, n - (n == 3))
                combine(1, LATE[n], late_bank[n]).then_inc(late_combined, 1)

            def regroup_late(n):
                pe.wait_ge(late_staged, n + 1)
                mm(late_bank[n][:], cst("regroup"), wstage[:, 0], True, True).then_inc(late_regrouped, 1)

            for l in range(2):
                if l == 0:
                    keep_clock_up(12)
                    transpose_h(3, range(1))
                for t in range(NT):
                    pe.wait_ge(hT_copied, (2 + l) * NT + t + 1)
                    pe.wait_ge(ld_root, 16 * (l + 1))
                    for c in range(HC):
                        if l == 0 and t == 0 and c == 2:
                            transpose_h(3, range(1, 2))
                        ins = mm(bank[5 + t][:], hT[:, c, t * P:(t + 1) * P], root[:, c], c == 0, False)
                ins.then_inc(root_used, 1)
                if l == 0:
                    combine_late(0)
                pe.wait_ge(gx_ready, 4 * (l + 1))
                pe.wait_ge(counted, NE)
                wait(pe, YT_copied, 4 * l)
                for k in range(WC // 2):
                    for c in (2 * k, 2 * k + 1):
                        for s in range(NT):
                            for w in range(4):
                                if l == 1 and k == WC // 2 - 1:
                                    r, i = c % 2, (WC - 2) * 64 + 32 * w
                                else:
                                    r, i = w % 2, c * 64 + 32 * (w // 2)
                                ins = mm(bank[k][32 * w:32 * w + 32, (c % 2) * N:(c % 2 + 1) * N],
                                         gx[:, r, s, i:i + 32], CT[:, r, s], s == 0, s == NT - 1)
                    ins.then_inc(YT_done, 1)
                    if k == 0 and l == 0:
                        regroup_late(0)

                def add(t, chunks, last=False):
                    for c in chunks:
                        ins = mm(bank[5 + t][:], YT[:, c, t * P:(t + 1) * P], wcomb[:, l * WC + c], False,
                                 last and c == chunks[-1])
                    return ins

                if l == 0:
                    pe.wait_ge(YT_copied, 3)
                    add(0, range(WC - 2))
                    pe.wait_ge(YT_copied, 4)
                    add(0, range(WC - 2, WC), last=True).then_inc(rgcn_done, 1)
                    add(1, range(WC), last=True).then_inc(rgcn_done, 1)
                    transpose_h(4, range(1))
                    combine_late(1)
                    transpose_h(4, range(1, 2))
                    regroup_late(1)
                else:
                    combine_late(2)
                    pe.wait_ge(YT_copied, 8)
                    add(0, range(4))
                    regroup_late(2)
                    combine_late(3)
                    pe.wait_ge(pair_added, 2 * NB)
                    add(0, (6, 7))
                    pe.wait_ge(late_copied, 3)
                    add(0, (4,))
                    regroup_late(3)
                    add(1, range(1))
                    pe.wait_ge(late_copied, 4)
                    add(0, (5,), last=True).then_inc(rgcn_done, 1)
                    add(1, range(1, 5))
                    transpose_h(5, range(1))
                    add(1, range(5, WC), last=True).then_inc(rgcn_done, 1)

            def first_product(t, chunks):
                for c in chunks:
                    ins = mm(bank[5 + t][:], hT[:, c, t * P:(t + 1) * P], w1v()[:, c], c == 0, c == HC - 1)
                if c == HC - 1:
                    ins.then_inc(f1_done, 1)

            pe.wait_ge(ld_ffn, 16 * (5 + HC))
            pe.wait_ge(hT_copied, 4 * NT + 1)
            first_product(0, range(HC - 1))
            transpose_h(5, range(1, 2))
            first_product(0, range(HC - 1, HC))
            pe.wait_ge(hT_copied, 5 * NT)
            for c in range(HC):
                ins = mm(bank[7][0:E2, 0:N], wr[:, c], hT[:, c], c == 0, c == HC - 1)
            ins.then_inc(plog_done, 1)
            first_product(1, range(HC // 2))
            pe.wait_ge(prow_ready, 1)
            for t in range(NT):
                ins = pe.transpose(bank[7][:, 256 + t * E2:256 + (t + 1) * E2], prow[:, t * P:(t + 1) * P], ident[0:E2, 0:E2])
            ins.then_inc(pt_done, 1)
            pe.wait_ge(prob_copied, 1)
            for e in range(E2):
                for t in range(NT):
                    ins = pe.transpose(bank[e // 2][:, (e % 2) * N + t * P:(e % 2) * N + (t + 1) * P],
                                       prob[:, t, e:e + 1].broadcast_to([P, P]), ident)
                if e % 2:
                    ins.then_inc(pb_done, 1)
            first_product(1, range(HC // 2, HC))
            for t in range(NT):
                pe.wait_ge(sel_ready, t + 1)
                pe.transpose(bank[(7, 2)[t]][0:E2, 0:P], sel[:, t], ident).then_inc(selT_done, 1)
                pe.wait_ge(act1_ready, t + 1)
                for c in range(HC):
                    ins = pe.transpose(bank[5 + t][:, c * P:(c + 1) * P], act1[:, t, c * P:(c + 1) * P], ident)
                ins.then_inc(a1T_done, 1)
                pe.wait_ge(selT_copied, t + 1)
                mm(bank[4 - t][:], PT[:, t * P:(t + 1) * P], b2[:], True, False)
                pe.wait_ge(a1T_copied, t + 1)
                for c in range(HC):
                    ins = mm(bank[4 - t][:], act1T[:, c, t * P:(t + 1) * P], w2v()[:, c], False, c == HC - 1)
                ins.then_inc(f2_done, 1)


_INS = ["x", "src", "dst", "edge_type_2", "edge_weight", "L0_gnn_emb_1", "L0_gnn_emb_2", "L0_gnn_alpha_p",
        "L0_gnn_beta_p", "L0_ffn_router_w", "L0_ffn_gate_w", "L0_ffn_up_w", "L0_ffn_down_w", "L1_gnn_basis1",
        "L1_gnn_att1", "L1_gnn_gate_w1", "L1_gnn_root1", "L1_gnn_bias1", "L1_gnn_basis2", "L1_gnn_att2",
        "L1_gnn_gate_w2", "L1_gnn_root2", "L1_gnn_bias2", "L1_ffn_Wr", "L1_ffn_W1", "L1_ffn_b1", "L1_ffn_W2",
        "L1_ffn_b2"]


def constants():
    import numpy as np
    c = np.zeros((P, NCONST), np.float32)

    def put(name, value):
        a, b = CONST[name]
        c[:, a:b] = value

    p = np.arange(P)
    put("ident", np.eye(P))
    put("before", p[:, None] < p[None, :])
    put("ones", 1.0)
    put("diag16", p[:, None] % 16 == np.arange(16)[None, :])
    put("block16", p[:, None] // 16 == np.arange(8)[None, :])
    j, r, i = p // 32, p // 16 % 2, p % 16
    i = 4 * i + j
    put("regroup", (64 * (i // 32) + 32 * r + i % 32)[:, None] == p[None, :])
    e = np.arange(NE)
    put("earlier_expert", (e[None, :] < e[:, None]).reshape(1, -1))
    t = np.arange(NT)[None, :, None] * P + p[:, None, None]
    put("tie_order", np.where(np.arange(N)[None, None, :] < t, 1 - 2.0**-24, 1.0).reshape(P, -1))
    put("iota", np.arange(N))
    s = np.arange(2 * CAP) % CAP
    put("slots", np.where(s < LIMIT, s, -5))
    return c


def kernel(**inputs):
    import numpy as _np
    import concourse.bacc as _bacc
    from concourse import mybir as _mybir
    from concourse.bass_utils import run_bass_kernel_spmd as _run

    nc = _bacc.Bacc("TRN2", target_bir_lowering=False, num_devices=1)
    arrays, args = {}, []
    for name in _INS + ["shape_constants"]:
        a = constants() if name == "shape_constants" else _np.ascontiguousarray(inputs[name])
        arrays[f"in_{name}_dram"] = a
        args.append(nc.dram_tensor(f"in_{name}_dram", a.shape, _mybir.dt.from_np(a.dtype), kind="ExternalInput").ap())
    args.append(nc.dram_tensor("out_0_dram", (N, H), F32, kind="ExternalOutput").ap())
    build(nc, *args)
    r = _run(nc, [arrays], core_ids=[0])
    return r.results[0]["out_0_dram"]
```
